# Optimizing a Trainium2 kernel written in Bass

```python
import numpy as np
import jax
import jax.numpy as jnp

def _softmax(x, axis=-1):
    return jax.nn.softmax(x, axis=axis)

def _gelu(x):
    return jax.nn.gelu(x, approximate=True)

def _silu(x):
    return jax.nn.silu(x)

def _sigmoid(x):
    return jax.nn.sigmoid(x)

def _layernorm(x, axis=-1, eps=1e-05):
    m = jnp.mean(x, axis=axis, keepdims=True)
    v = jnp.var(x, axis=axis, keepdims=True)
    return (x - m) / jnp.sqrt(v + eps)

def _scatter_add(tgt, idx, src, axis=0):
    return tgt.at[idx].add(src)

def _segment_sum(src, seg, n):
    return jax.ops.segment_sum(src, seg, n)
kernel_name = 'mk_decoder_postln_d1_seqx_r4_83625c'

def setup_inputs(seed: int=0):
    np.random.seed(seed)
    _w = jnp.asarray

    def _rec_inputs():
        import jax
        import jax.numpy as jnp
        _rk = jax.random.key(seed)
        x = -0.0002928 + 1 * jax.random.normal(jax.random.fold_in(_rk, 1), (4, 512, 256), jnp.float32)
        _lenS = 512 - jax.random.randint(jax.random.fold_in(_rk, 7), (4,), 0, max(1, 512 // 4) + 1, jnp.int32)
        _lenS2 = 512 - jax.random.randint(jax.random.fold_in(_rk, 8), (4,), 0, max(1, 512 // 4) + 1, jnp.int32)
        _ctx_1024P = jax.random.normal(jax.random.fold_in(_rk, 11), (4, 16, 256), jnp.float32)
        _ctx_1024c = jax.random.dirichlet(jax.random.fold_in(_rk, 511), 0.3 * jnp.ones((16,), jnp.float32), (4, 512))
        _ctx_1024t = jnp.einsum('bsk,bkd->bsd', _ctx_1024c, _ctx_1024P)
        _ctx_1024t = _ctx_1024t * jax.lax.rsqrt(jnp.mean(jnp.square(_ctx_1024t)) + 1e-12) * 0.953939
        ctx_1024 = -1.39393e-06 + 0.999914 * (_ctx_1024t + 0.3 * jax.random.normal(jax.random.fold_in(_rk, 611), (4, 512, 256), jnp.float32))
        return (x, ctx_1024)
    x, ctx_1024 = _rec_inputs()

    def _L0_attn_setup():
        import jax, jax.numpy as jnp
        import numpy as np
        D_MODEL = 256
        D_STATE = 16
        D_CONV = 4
        EXPAND = 2
        D_INNER = EXPAND * D_MODEL
        DT_MIN, DT_MAX = (0.001, 0.1)
        BATCH, SEQ = (4, 512)

        def _silu(v):
            return v * jax.nn.sigmoid(v)
        key = jax.random.key(seed)
        ks = jax.random.split(key, 5)
        x = jax.random.normal(ks[0], (BATCH, SEQ, D_MODEL), jnp.float32)
        W_in = jax.random.normal(ks[1], (2 * D_INNER, D_MODEL), jnp.float32) / np.sqrt(D_MODEL)
        conv_w = jax.random.normal(ks[2], (D_INNER, D_CONV), jnp.float32) / np.sqrt(D_CONV)
        conv_b = jnp.zeros((D_INNER,), jnp.float32)
        W_xproj = jax.random.normal(ks[3], (2 * D_STATE + 1, D_INNER), jnp.float32) / np.sqrt(D_INNER)
        A_log = jnp.log(jnp.arange(1, D_STATE + 1, dtype=jnp.float32))
        D_param = jnp.ones((D_INNER,), jnp.float32)
        W_out = jax.random.normal(ks[4], (D_MODEL, D_INNER), jnp.float32) / np.sqrt(D_INNER)
        return dict(x=x, W_in=W_in, conv_w=conv_w, conv_b=conv_b, W_xproj=W_xproj, A_log=A_log, D_param=D_param, W_out=W_out)
    _L0_attn_all = _L0_attn_setup()
    _L0_attn_in = {k: v for k, v in _L0_attn_all.items() if k in ('W_in', 'conv_w', 'conv_b', 'W_xproj', 'A_log', 'D_param', 'W_out')}
    del _L0_attn_all

    def _L0_xattn_setup():
        import jax, jax.numpy as jnp
        import numpy as np
        EPS_BACKEND = 1e-06
        NORM_EPS = 1e-06
        NUM_HEADS = 4

        def _mlstm_forward(q, k, v, ig_kernel, ig_bias, fg_kernel, fg_bias, outnorm_weight):
            B, S, E = q.shape
            NH = ig_bias.shape[0]
            DH = E // NH
            gate_input = jnp.concatenate([q, k, v], axis=-1)
            igate = gate_input @ ig_kernel + ig_bias
            fgate = gate_input @ fg_kernel + fg_bias
            qh = q.reshape(B, S, NH, DH).transpose(0, 2, 1, 3)
            kh = k.reshape(B, S, NH, DH).transpose(0, 2, 1, 3)
            vh = v.reshape(B, S, NH, DH).transpose(0, 2, 1, 3)
            ig = igate.transpose(0, 2, 1)
            fg = fgate.transpose(0, 2, 1)
            log_fg = jax.nn.log_sigmoid(fg)
            cums = jnp.concatenate([jnp.zeros((B, NH, 1), log_fg.dtype), jnp.cumsum(log_fg, axis=-1)], axis=-1)
            fg_mat = cums[..., :, None] - cums[..., None, :]
            mask = jnp.tril(jnp.ones((S + 1, S + 1), bool))
            fg_mat = jnp.where(mask, fg_mat, -jnp.inf)[..., 1:, 1:]
            log_D = fg_mat + ig[..., None, :]
            max_log_D = jnp.max(log_D, axis=-1, keepdims=True)
            D = jnp.exp(log_D - max_log_D)
            qk = jnp.einsum('bnsd,bntd->bnst', qh, kh) / jnp.sqrt(jnp.float32(DH))
            C = qk * D
            normalizer = jnp.maximum(jnp.abs(C.sum(-1, keepdims=True)), jnp.exp(-max_log_D))
            h = jnp.einsum('bnst,bntd->bnsd', C / (normalizer + EPS_BACKEND), vh)
            h = h.transpose(0, 2, 1, 3)
            mean = h.mean(-1, keepdims=True)
            var = h.var(-1, keepdims=True)
            hn = (h - mean) * jax.lax.rsqrt(var + NORM_EPS) * outnorm_weight
            return hn.reshape(B, S, E)
        key = jax.random.key(seed)
        ks = jax.random.split(key, 8)
        B, S, E, NH = (2, 512, 256, NUM_HEADS)
        DH = E // NH
        q = jax.random.normal(ks[0], (B, S, E), jnp.float32)
        k = jax.random.normal(ks[1], (B, S, E), jnp.float32)
        v = jax.random.normal(ks[2], (B, S, E), jnp.float32)
        ig_kernel = jax.random.normal(ks[3], (3 * E, NH), jnp.float32) * 0.02
        fg_kernel = jax.random.normal(ks[4], (3 * E, NH), jnp.float32) * 0.02
        ig_bias = jax.random.normal(ks[5], (NH,), jnp.float32) * 0.1
        fg_bias = jnp.linspace(3.0, 6.0, NH, dtype=jnp.float32)
        outnorm_weight = jnp.ones((NH, DH), jnp.float32)
        return {'q': q, 'k': k, 'v': v, 'ig_kernel': ig_kernel, 'ig_bias': ig_bias, 'fg_kernel': fg_kernel, 'fg_bias': fg_bias, 'outnorm_weight': outnorm_weight}
    _L0_xattn_all = _L0_xattn_setup()
    _L0_xattn_in = {k: v for k, v in _L0_xattn_all.items() if k in ('ig_kernel', 'ig_bias', 'fg_kernel', 'fg_bias', 'outnorm_weight')}
    del _L0_xattn_all

    def _L0_ffn_setup():
        import jax, jax.numpy as jnp
        import numpy as np
        E = 8
        JITTER = 0.01

        def _sparse_mixer_routing(logits):
            top_vals, top_idx = jax.lax.top_k(logits, 2)
            eidx = jnp.arange(logits.shape[-1])

            def _multiplier(thr, base_logits, idx):
                factor = jnp.maximum(jnp.abs(logits), thr)
                mask = (thr - logits) / factor > 2.0 * JITTER
                probs = jax.nn.softmax(jnp.where(mask, -jnp.inf, base_logits), axis=-1)
                return jnp.take_along_axis(probs, idx, axis=-1)
            mult1 = _multiplier(top_vals[:, :1], logits, top_idx[:, :1])
            scat = jnp.where(eidx[None, :] == top_idx[:, :1], -jnp.inf, logits)
            mult2 = _multiplier(top_vals[:, 1:2], scat, top_idx[:, 1:2])
            return (jnp.concatenate([mult1, mult2], axis=-1), top_idx)
        key = jax.random.key(seed)
        ks = jax.random.split(key, 5)
        H, F = (256, 1024)
        scale = 0.02
        return {'hidden_states': jax.random.normal(ks[0], (1, 512, H), jnp.float32), 'gate_w': jax.random.normal(ks[1], (H, E), jnp.float32) * scale, 'w1': jax.random.normal(ks[2], (E, H, F), jnp.float32) * scale, 'w2': jax.random.normal(ks[3], (E, F, H), jnp.float32) * scale, 'w3': jax.random.normal(ks[4], (E, H, F), jnp.float32) * scale}
    _L0_ffn_all = _L0_ffn_setup()
    _L0_ffn_in = {k: v for k, v in _L0_ffn_all.items() if k in ('gate_w', 'w1', 'w2', 'w3')}
    del _L0_ffn_all
    return {'x': x, 'ctx_1024': ctx_1024, 'L0_attn_W_in': _L0_attn_in['W_in'], 'L0_attn_conv_w': _L0_attn_in['conv_w'], 'L0_attn_conv_b': _L0_attn_in['conv_b'], 'L0_attn_W_xproj': _L0_attn_in['W_xproj'], 'L0_attn_A_log': _L0_attn_in['A_log'], 'L0_attn_D_param': _L0_attn_in['D_param'], 'L0_attn_W_out': _L0_attn_in['W_out'], 'L0_xattn_ig_kernel': _L0_xattn_in['ig_kernel'], 'L0_xattn_ig_bias': _L0_xattn_in['ig_bias'], 'L0_xattn_fg_kernel': _L0_xattn_in['fg_kernel'], 'L0_xattn_fg_bias': _L0_xattn_in['fg_bias'], 'L0_xattn_outnorm_weight': _L0_xattn_in['outnorm_weight'], 'L0_ffn_gate_w': _L0_ffn_in['gate_w'], 'L0_ffn_w1': _L0_ffn_in['w1'], 'L0_ffn_w2': _L0_ffn_in['w2'], 'L0_ffn_w3': _L0_ffn_in['w3']}

def reference(x, ctx_1024, L0_attn_W_in, L0_attn_conv_w, L0_attn_conv_b, L0_attn_W_xproj, L0_attn_A_log, L0_attn_D_param, L0_attn_W_out, L0_xattn_ig_kernel, L0_xattn_ig_bias, L0_xattn_fg_kernel, L0_xattn_fg_bias, L0_xattn_outnorm_weight, L0_ffn_gate_w, L0_ffn_w1, L0_ffn_w2, L0_ffn_w3):
    import jax
    import jax.numpy as jnp

    def _L0_attn_ref(x, W_in, conv_w, conv_b, W_xproj, A_log, D_param, W_out):
        import jax, jax.numpy as jnp
        import numpy as np
        D_MODEL = 256
        D_STATE = 16
        D_CONV = 4
        EXPAND = 2
        D_INNER = EXPAND * D_MODEL
        DT_MIN, DT_MAX = (0.001, 0.1)
        BATCH, SEQ = (4, 512)

        def _silu(v):
            return v * jax.nn.sigmoid(v)
        b, l, d = x.shape
        xz = x @ W_in.T
        x_proj, z = jnp.split(xz, 2, axis=-1)
        xp = jnp.pad(x_proj, ((0, 0), (D_CONV - 1, 0), (0, 0)))
        x_conv = conv_b + sum((xp[:, k:k + l, :] * conv_w[:, k] for k in range(D_CONV)))
        x_conv = _silu(x_conv)
        x_dbl = x_conv @ W_xproj.T
        Bmat = x_dbl[..., :D_STATE]
        Cmat = x_dbl[..., D_STATE:2 * D_STATE]
        dt = jnp.clip(jax.nn.softplus(x_dbl[..., -1]), DT_MIN, DT_MAX)
        A = -jnp.exp(A_log)

        def step(h, inp):
            x_t, dt_t, B_t, C_t = inp
            dt_A = jnp.clip(dt_t[:, None] * A, -20.0, 0.0)
            A_bar = jnp.exp(dt_A)[:, None, :]
            B_bar = jnp.clip(dt_t[:, None] * B_t, -10.0, 10.0)[:, None, :]
            h = jnp.clip(A_bar * h + B_bar * x_t[:, :, None], -100.0, 100.0)
            y_t = jnp.einsum('bds,bs->bd', h, C_t)
            return (h, y_t)
        h0 = jnp.zeros((b, D_INNER, D_STATE), x.dtype)
        xs = (jnp.swapaxes(x_conv, 0, 1), jnp.swapaxes(dt, 0, 1), jnp.swapaxes(Bmat, 0, 1), jnp.swapaxes(Cmat, 0, 1))
        _, ys = jax.lax.scan(step, h0, xs)
        y = jnp.swapaxes(ys, 0, 1)
        y = y * _silu(z) + x_conv * D_param
        return y @ W_out.T

    def _L0_xattn_ref(q, k, v, ig_kernel, ig_bias, fg_kernel, fg_bias, outnorm_weight):
        import jax, jax.numpy as jnp
        import numpy as np
        EPS_BACKEND = 1e-06
        NORM_EPS = 1e-06
        NUM_HEADS = 4

        def _mlstm_forward(q, k, v, ig_kernel, ig_bias, fg_kernel, fg_bias, outnorm_weight):
            B, S, E = q.shape
            NH = ig_bias.shape[0]
            DH = E // NH
            gate_input = jnp.concatenate([q, k, v], axis=-1)
            igate = gate_input @ ig_kernel + ig_bias
            fgate = gate_input @ fg_kernel + fg_bias
            qh = q.reshape(B, S, NH, DH).transpose(0, 2, 1, 3)
            kh = k.reshape(B, S, NH, DH).transpose(0, 2, 1, 3)
            vh = v.reshape(B, S, NH, DH).transpose(0, 2, 1, 3)
            ig = igate.transpose(0, 2, 1)
            fg = fgate.transpose(0, 2, 1)
            log_fg = jax.nn.log_sigmoid(fg)
            cums = jnp.concatenate([jnp.zeros((B, NH, 1), log_fg.dtype), jnp.cumsum(log_fg, axis=-1)], axis=-1)
            fg_mat = cums[..., :, None] - cums[..., None, :]
            mask = jnp.tril(jnp.ones((S + 1, S + 1), bool))
            fg_mat = jnp.where(mask, fg_mat, -jnp.inf)[..., 1:, 1:]
            log_D = fg_mat + ig[..., None, :]
            max_log_D = jnp.max(log_D, axis=-1, keepdims=True)
            D = jnp.exp(log_D - max_log_D)
            qk = jnp.einsum('bnsd,bntd->bnst', qh, kh) / jnp.sqrt(jnp.float32(DH))
            C = qk * D
            normalizer = jnp.maximum(jnp.abs(C.sum(-1, keepdims=True)), jnp.exp(-max_log_D))
            h = jnp.einsum('bnst,bntd->bnsd', C / (normalizer + EPS_BACKEND), vh)
            h = h.transpose(0, 2, 1, 3)
            mean = h.mean(-1, keepdims=True)
            var = h.var(-1, keepdims=True)
            hn = (h - mean) * jax.lax.rsqrt(var + NORM_EPS) * outnorm_weight
            return hn.reshape(B, S, E)
        return _mlstm_forward(q, k, v, ig_kernel, ig_bias, fg_kernel, fg_bias, outnorm_weight)

    def _L0_ffn_ref(hidden_states, gate_w, w1, w2, w3):
        import jax, jax.numpy as jnp
        import numpy as np
        E = 8
        JITTER = 0.01

        def _sparse_mixer_routing(logits):
            top_vals, top_idx = jax.lax.top_k(logits, 2)
            eidx = jnp.arange(logits.shape[-1])

            def _multiplier(thr, base_logits, idx):
                factor = jnp.maximum(jnp.abs(logits), thr)
                mask = (thr - logits) / factor > 2.0 * JITTER
                probs = jax.nn.softmax(jnp.where(mask, -jnp.inf, base_logits), axis=-1)
                return jnp.take_along_axis(probs, idx, axis=-1)
            mult1 = _multiplier(top_vals[:, :1], logits, top_idx[:, :1])
            scat = jnp.where(eidx[None, :] == top_idx[:, :1], -jnp.inf, logits)
            mult2 = _multiplier(top_vals[:, 1:2], scat, top_idx[:, 1:2])
            return (jnp.concatenate([mult1, mult2], axis=-1), top_idx)
        B, S, H = hidden_states.shape
        x = hidden_states.reshape(-1, H)
        logits = x @ gate_w
        mult, sel = _sparse_mixer_routing(logits)
        w = jnp.sum(mult[:, :, None] * (sel[:, :, None] == jnp.arange(E)[None, None, :]), axis=1)
        h = jax.nn.silu(jnp.einsum('th,ehf->etf', x, w1)) * jnp.einsum('th,ehf->etf', x, w3)
        out = jnp.einsum('etf,efh,te->th', h, w2, w)
        return out.reshape(B, S, H)
    x = _layernorm(x + _L0_attn_ref(x, L0_attn_W_in, L0_attn_conv_w, L0_attn_conv_b, L0_attn_W_xproj, L0_attn_A_log, L0_attn_D_param, L0_attn_W_out), axis=-1)
    x = _layernorm(x + _L0_xattn_ref(x, ctx_1024, ctx_1024, L0_xattn_ig_kernel, L0_xattn_ig_bias, L0_xattn_fg_kernel, L0_xattn_fg_bias, L0_xattn_outnorm_weight), axis=-1)
    x = _layernorm(x + _L0_ffn_ref(x, L0_ffn_gate_w, L0_ffn_w1, L0_ffn_w2, L0_ffn_w3), axis=-1)
    return x

_drawn_inputs = setup_inputs


def setup_inputs(seed=0):
    import zlib

    import numpy as np

    out = dict(_drawn_inputs(seed))
    spreads = {'L0_attn_conv_b': (0.0, 0.1),
     'L0_attn_D_param': (1.0, 0.2),
     'L0_xattn_outnorm_weight': (1.0, 0.2)}
    factors = {}
    for name, (base, spread) in spreads.items():
        noise = np.random.default_rng([zlib.crc32(name.encode()), seed]).standard_normal(out[name].shape)
        drawn = base * np.exp(spread * noise) if base else spread * noise
        out[name] = jnp.asarray(drawn.astype(out[name].dtype))
    for name, factor in factors.items():
        out[name] = (out[name] * factor).astype(out[name].dtype)
    return out
```

```python
from contextlib import ExitStack

import concourse.bass as bass
from concourse import mybir

F32 = mybir.dt.float32
BF16 = mybir.dt.bfloat16
I32 = mybir.dt.int32
ALU = mybir.AluOpType
ACT = mybir.ActivationFunctionType
AX_X = mybir.AxisListType.X
RMAX = bass.bass_isa.ReduceOp.max

P = 128
B, S, D = 4, 512, 256
T = B * S
NQ = S // P
NT = T // P
KD = D // P
DI = 2 * D
NJ = DI // P
NS, NSP = 16, 32
TAPS = 4
NX = 2 * NS + 1
CH = 32
NC = P // CH
H = 4
DH = D // H
DV = DH + 1
E, F = 8, 1024
HALF = F // 2
NB = (2 * T + E * (P - 1)) // P + 1
NB += NB % 2
REGION = T + P
ROW = D + 4
WCOLS = 2 * KD * F + (F // P) * D
RINGW = 3
DT_MIN, DT_MAX = 0.001, 0.1
CLIP = 100.0
JITTER2 = 0.02
BIG = 3.0e38
HORNER = 10
NEWTON = 3
STATE_LIMIT, DECAY_LIMIT = 99.0, 80.0


def decoder_kernel(nc, x, xT, ctx, ctxT, w_inT, conv_w, conv_b, w_xT, a_log, d_param, w_outT, gate_k, gate_b,
                   outnorm, router_w, w_exp, out):
    slots = nc.dram_tensor("slots", [(E * REGION) + P, ROW], F32).ap()
    yrows = nc.dram_tensor("yrows", [2 * T + P, D], F32).ap()
    coef = nc.dram_tensor("scan_coef", [S, 3 * B * NS], F32).ap()

    with ExitStack() as stack:
        def sb(name, cols, dt=F32):
            return stack.enter_context(nc.sbuf_tensor(name, [P, cols], dt))

        def sem(name):
            return stack.enter_context(nc.semaphore(name))

        xtok = sb("xtok", NT * ROW)[:, :].rearrange("p (i c) -> p i c", c=ROW)
        xcol = sb("xcol", KD * T)[:, :].rearrange("p (k t) -> p k t", k=KD)
        region1 = sb("region1", KD * 2 * DI + 4 * 516 + 2 * S)
        region2 = sb("region2", NT * H * DV + KD * T)
        region3 = sb("region3", NJ * T)
        region4 = sb("region4", RINGW * WCOLS)

        def carve(region, at, shape):
            n = 1
            for s in shape:
                n *= s
            v = region[:, at[0]:at[0] + n]
            at[0] += n
            names = "abcdef"[:len(shape)]
            if len(shape) == 1:
                return v
            return v.rearrange(f"p ({' '.join(names)}) -> p {' '.join(names)}",
                               **{c: s for c, s in zip(names[1:], shape[1:])})

        at = [0]
        winT = carve(region1, at, (KD, 2 * DI))
        xpad = carve(region1, at, (4, 516))
        cbuf = carve(region1, at, (2, S))
        at = [0]
        gcT = carve(region1, at, (NQ, P))
        lbT = carve(region1, at, (NQ, P))
        rbT = carve(region1, at, (NQ, P))
        laT = carve(region1, at, (2, NQ, P))
        raT = carve(region1, at, (2, NQ, P))
        hst = carve(region1, at, (NQ - 1, DI))
        at = [0]
        xdbl = carve(region2, at, (NT, NX))
        dtA = carve(region2, at, (NT, NSP))
        abar = carve(region2, at, (NT, NSP))
        vabs = carve(region2, at, (NT, NSP))
        bbar = carve(region2, at, (NT, NS))
        cumt = carve(region2, at, (NT, NS))
        ediff = carve(region2, at, (NC - 1, NT, NS))
        la = carve(region2, at, (NT, 4 * NS))
        ra = carve(region2, at, (NT, 4 * NS))
        lb = carve(region2, at, (NT, NSP))
        rb = carve(region2, at, (NT, NSP))
        rc = carve(region2, at, (NT, NSP))
        wt = carve(region2, at, (NT, NSP))
        aneg = carve(region2, at, (NS,))
        assert at[0] <= NT * H * DV + KD * T, at
        at = [0]
        vaug = carve(region2, at, (NT, H, DV))
        ctxc = carve(region2, at, (KD, T))
        at = [0]
        xc = carve(region3, at, (NJ, T))
        at = [0]
        aT = region3[:, 0:S]
        zsel = carve(region3, at, (NQ, P))
        mrow = carve(region3, at, (S,))
        mS = carve(region3, at, (NQ, B, NSP))
        decay = carve(region3, at, (2, H, P))
        prob = carve(region3, at, (2, H, P))
        tot = carve(region3, at, (2, NQ, H, DV))
        kw = carve(region3, at, (6, H, DH))
        hs = carve(region3, at, (2, NQ - 1, 2, DV))
        assert at[0] <= NJ * T, at
        at = [0]
        zs = carve(region4, at, (NJ, T))
        yx = carve(region4, at, (B + 1, NQ * DI))
        assert at[0] == RINGW * WCOLS, at

        def xct(b, q):
            return yx[:, b + 1, q * DI:(q + 1) * DI]

        def ybuf(b, j):
            return yx[:, b, j * S:(j + 1) * S]
        wring = region4[:, :].rearrange("p (e c) -> p e c", e=RINGW)
        at = [0]
        xg = carve(region1, at, (2, ROW))
        xgT = carve(region1, at, (2, KD, P))
        gsil = carve(region1, at, (2, HALF))
        hmid = carve(region1, at, (2, HALF))
        hT = carve(region1, at, (2, 4, P))
        yout = carve(region1, at, (2, D))
        assert at[0] <= KD * 2 * DI + 4 * 516 + 2 * S
        ya = region4[:, 0:NT * D].rearrange("p (i d) -> p i d", d=D)
        yb = region4[:, NT * D:2 * NT * D].rearrange("p (i d) -> p i d", d=D)

        woutT = sb("woutT", NJ * D)[:, :].rearrange("p (j d) -> p j d", j=NJ)
        wxT = sb("wxT", NJ * NX)[:, :].rearrange("p (j n) -> p j n", j=NJ)
        convw = sb("convw", NJ * TAPS)[:, :].rearrange("p (j k) -> p j k", j=NJ)
        convb = sb("convb", NJ)
        dpar = sb("dpar", NJ)
        alog = sb("alog", NS)
        gk = sb("gk", 3 * KD * 2 * H)[:, :].rearrange("p (k g) -> p k g", k=3 * KD)
        gb = sb("gb", 2 * H)
        onw = sb("onw", D)
        rw = sb("rw", KD * E)[:, :].rearrange("p (k e) -> p k e", k=KD)

        ident = sb("ident", P)
        ones = sb("ones", P)
        tri = sb("tri", P)
        tri32 = sb("tri32", P)
        own = sb("own", P)
        upto = sb("upto", (NC - 1) * P)
        before16 = sb("before16", P, BF16)
        ones16 = sb("ones16", P, BF16)
        mask_la = sb("mask_la", NC - 1)
        mask_ra = sb("mask_ra", NC - 1)
        eid = sb("eid", E)
        eoff = sb("eoff", E)
        tokid = sb("tokid", NT)
        steps128 = sb("steps128", NT)
        blkid = sb("blkid", NB)
        padrow = sb("padrow", ROW)

        small = sb("small", 996)
        at = [0]
        dtv = carve(small, at, (NT,))
        expv = carve(small, at, (NT,))
        horner = carve(small, at, (NT,))
        xmax = carve(small, at, (NT,))
        guard = carve(small, at, (2,))
        guardall = carve(small, at, (2,))
        dec = carve(small, at, (NQ,))
        stats = carve(small, at, (NQ * H, 6))
        mv = carve(small, at, (NQ * H, 2))
        rsv = carve(small, at, (NQ * H,))
        rsy = carve(small, at, (NQ * H,))
        rst = carve(small, at, (NQ * H,))
        gt = carve(small, at, (NT, 2 * H))
        lfa = carve(small, at, (NT, H))
        lfb = carve(small, at, (NT, H))
        lfpre = carve(small, at, (B, NQ, H))
        av = carve(small, at, (NT, H))
        cumS = carve(small, at, (NT, H))
        emx = carve(small, at, (NT, H))
        fac = carve(small, at, (9, B, H))
        den = carve(small, at, (NQ, H))
        assert at[0] <= 996, at
        bad = sb("bad", 1, I32)

        at = [0]
        negsel = carve(region1, at, (H, P))
        apad = carve(region1, at, (NT, NSP))
        hbuf = carve(region1, at, (NQ, H, DH))
        x2c = carve(region1, at, (NQ, KD, P))
        cmp16 = carve(region1, at, (E, NT))
        cmpb = carve(region1, at, (NB, E))
        lg = carve(region1, at, (NQ, E))
        lg2 = carve(region1, at, (NQ, E))
        oh1 = carve(region1, at, (NQ, E))
        oh2 = carve(region1, at, (NQ, E))
        ra_ = carve(region1, at, (NQ, E))
        rb_ = carve(region1, at, (NQ, E))
        rc_ = carve(region1, at, (NQ, E))
        top1 = carve(region1, at, (NQ,))
        top2 = carve(region1, at, (NQ,))
        posf = carve(region1, at, (2, NQ))
        sums = carve(region1, at, (2, NQ))
        assert at[0] <= KD * 2 * DI + 4 * 516 + 2 * S
        pos = sb("pos", 2 * NT, I32)[:, :].rearrange("p (k i) -> p k i", k=2)
        picks = sb("picks", NT * E, BF16)[:, :].rearrange("p (i e) -> p i e", e=E)
        picksum = sb("picksum", (NT + 1) * E, BF16)[:, :].rearrange("p (i e) -> p i e", e=E)
        cnt = sb("cnt", E)
        nblk = sb("nblk", E)
        endblk = sb("endblk", E)
        eblk = sb("eblk", NB)
        sblk = sb("sblk", NB)
        used = sb("used", NB)
        tab_ready = sb("tab_ready", NB, I32)
        tab_ring = sb("tab_ring", NB, I32)
        tab_slot = sb("tab_slot", NB, I32)
        tab_pad = sb("tab_pad", E, I32)
        tab_end = sb("tab_end", E, I32)
        ringf = sb("ringf", NB)
        ringg = sb("ringg", NB)
        meta = sb("meta", 2 * 6)[:, :].rearrange("p (s c) -> p s c", s=2)
        rid = sb("rid", 2, I32)
        fb_c = carve(region1, [2 * B * NJ * NS], (4 * 3 * B * NS,))
        mts = xcol[:, 0, 0:2 * NQ * P].rearrange("p (s q t) -> p s q t", s=2, q=NQ)
        fb_h = carve(region1, [0], (B, NJ, NS))
        fb_t = carve(region1, [B * NJ * NS], (B, NJ, NS))

        bank = [stack.enter_context(nc.psum_tensor(f"bank{k}", [P, 512], F32)) for k in range(8)]

        place, turns = {}, [0] * 8

        def plan(item, k):
            place[item] = (k, turns[k])
            turns[k] += 1

        for n in range(B * NJ):
            plan(("xp", n), n % 2)
            plan(("z", n), 2 + n % 2)
            if n % NJ == 1 and n > NJ:
                b = n // NJ - 1
                plan(("xd", b), 4)
                for q in range(NQ):
                    plan(("xt", NQ * b + q), 5 + (NQ * b + q) % 3)
        plan(("xd", B - 1), 4)
        for q in range(NQ):
            plan(("xt", NQ * (B - 1) + q), 5 + (NQ * (B - 1) + q) % 3)
        for n, k in (("cumA", 0), ("cumB", 1), ("cumC", 2), ("cumD", 3), ("abT", 4), ("vbT", 5), ("gcT", 6),
                     ("lbT", 7), ("rbT", 0), (("laT", 0), 1), (("laT", 1), 2), (("raT", 0), 3), (("raT", 1), 4)):
            plan(n, k)
        for q in range(NQ - 1):
            plan(("S", q), (7, 5, 6)[q])
        for b in range(B):
            plan(("M1", b), 5 + 2 * (b % 2))
            plan(("M2", b), 6 if b % 2 == 0 else 4)
            for j in range(NJ):
                plan(("y", b, j), j)
        for b in range(B):
            plan(("o", b, 0), 4)
            plan(("o", b, 1), 7)
            if b >= 1:
                for k in range(KD):
                    plan(("x1t", b - 1, k), k)
        for k in range(KD):
            plan(("x1t", B - 1, k), k)
        plan("g", 2)
        plan("cum", 2)
        plan("aT", 3)
        plan("mT", 5)
        plan("R", 6)

        def plan_front(i):
            if i % NQ == 0:
                plan(("H", i // NQ), 2)
            plan(("nm", i), 5)
            plan(("sA", i), (6, 0)[i % 2])
            plan(("sB", i), (7, 1)[i % 2])

        plan_front(0)
        for i in range(NT):
            if i + 1 < NT:
                plan_front(i + 1)
            if i % NQ == 2 and i > NQ:
                for q in range(NQ):
                    plan(("x2t", i - NQ - 2 + q), 3)
                plan(("lg", i // NQ - 1), 2)
            if i % NQ == 3 and i > NQ:
                plan(("rk", i // NQ - 1), 2)
            plan(("num", i), 4)
        for q in range(NQ):
            plan(("x2t", NT - NQ + q), 3)
        plan(("lg", B - 1), 2)
        plan(("rk", B - 1), 2)
        plan("cnt", 2)

        filled = [sem(f"bank{k}_filled") for k in range(8)]
        drained = [sem(f"bank{k}_drained") for k in range(8)]
        ld_first, ld_conv, ld_x, ld_small, ld_ctx = (sem(f"{n}_loaded") for n in ("first", "conv", "x", "small", "ctx"))
        consts_done = sem("consts_done")
        pool_step, dve_step, act_step = sem("pool_step"), sem("dve_step"), sem("act_step")
        conv_done, xc_done = sem("conv_done"), sem("xc_done")
        zs_done = sem("zs_done")
        vmin_done, exp_done, dtA_done = sem("vmin_done"), sem("exp_done"), sem("dtA_done")
        aneg_done = sem("aneg_done")
        cum_ready, cumexp_done = sem("cum_ready"), sem("cumexp_done")
        la_done, ra_done, ediff_done, factors_done, guard_in = (sem(n) for n in (
            "la_done", "ra_done", "ediff_done", "factors_done", "guard_in_done"))
        guard_done, guard_red, bad_done, scan_checked = (sem(n) for n in ("guard_done", "guard_reduced", "bad_done", "scan_checked"))
        hst_done, mt_done, y_copied, gated = sem("hst_done"), sem("mt_done"), sem("y_copied"), sem("gated")
        x1_done = sem("x1_done")
        gabs_done, gexp_done, lf_done, a_done, mrow_done, z_done, args_done, fac_done = (sem(n) for n in (
            "gabs_done", "gln_done", "lf_done", "a_done", "mrow_done", "zsel_done", "args_done", "fac_done"))
        vones_done, kw_done, kw_used = sem("vones_done"), sem("kw_done"), sem("kw_used")
        arg_done, masked, decay_done, prob_done, x2_done = (sem(n) for n in (
            "arg_done", "masked", "decay_done", "prob_done", "x2_done"))
        picks_done, rexp_in, rexp_done, row_done, scattered = (sem(n) for n in (
            "picks_done", "router_exp_in", "router_exp_done", "row_done", "scattered"))
        tables_done, padded = sem("tables_done"), sem("padded")
        fb_dma, fb_step, fb_summed = sem("fallback_dma"), sem("fallback_step"), sem("fallback_summed")
        w_loaded, w_ready = sem("w_loaded"), sem("w_ready")
        xg_loaded = [sem(f"xg{s}_loaded") for s in range(2)]
        xg_turned, xgT_done, meta_done, up_done, sil_done, mid_done, turned, hT_done, y_done, yout_done = (sem(n) for n in (
            "xg_turned", "xgT_done", "meta_done", "up_done", "silu_done", "mid_done", "h_turned", "hT_done", "y_done",
            "yout_done"))
        y_sent = [sem(f"y{s}_sent") for s in range(2)]
        y_back = [sem(f"yback{b}_loaded") for b in range(B)]
        fin_done, out_done = sem("fin_done"), sem("out_done")

        def wait_filled(eng, item):
            k, n = place[item]
            eng.wait_ge(filled[k], n + 1)

        def wait_drained(eng, item):
            k, n = place[item]
            eng.wait_ge(drained[k], n + 1)

        def drain(item, ins):
            ins.then_inc(drained[place[item][0]], 1)

        def ps(item):
            return bank[place[item][0]]

        def bc(ap, axis, shape):
            return ap.unsqueeze(axis).to_broadcast(shape)

        block = stack.enter_context(nc.Block())

        @block.sync
        def _(sp):
            sp.dma_start(winT, w_inT.rearrange("(k p) m -> p k m", p=P)).then_inc(ld_first, 16)
            sp.dma_start(xcol, xT.rearrange("(k p) t -> p k t", p=P)).then_inc(ld_first, 16)
            sp.dma_start(convw, conv_w.rearrange("(j p) k -> p j k", p=P)).then_inc(ld_conv, 16)
            sp.dma_start(convb[:, :], conv_b).then_inc(ld_conv, 16)
            sp.dma_start(wxT, w_xT.rearrange("(j p) n -> p j n", p=P)).then_inc(ld_conv, 16)
            sp.dma_start(xtok[:, :, 0:D], x.rearrange("(i p) d -> p i d", p=P)).then_inc(ld_x, 16)
            sp.dma_start(woutT, w_outT.rearrange("(j p) d -> p j d", p=P)).then_inc(ld_x, 16)
            sp.dma_start(dpar[:, :], d_param).then_inc(ld_small, 16)
            sp.dma_start(alog[:, :], a_log.partition_broadcast(P)).then_inc(ld_small, 16)
            sp.dma_start(gk, gate_k.rearrange("(k p) g -> p k g", p=P)).then_inc(ld_small, 16)
            sp.dma_start(gb[:, :], gate_b.partition_broadcast(P)).then_inc(ld_small, 16)
            sp.dma_start(onw[:, :], outnorm.partition_broadcast(P)).then_inc(ld_small, 16)
            sp.dma_start(rw, router_w.rearrange("(k p) e -> p k e", p=P)).then_inc(ld_small, 16)
            sp.wait_ge(scan_checked, 1)
            for q in range(NQ - 1):
                wait_filled(sp, ("S", q))
            wait_drained(sp, "cumD")
            sp.dma_start(ctxc, ctxT.rearrange("(k p) t -> p k t", p=P)).then_inc(ld_ctx, 16)
            for h in range(H):
                sp.dma_start(vaug[:, :, h, 0:DH], ctx.rearrange("(i p) (h d) -> h p i d", p=P, h=H)[h]).then_inc(ld_ctx, 16)
            for b in range(B):
                for o in range(2):
                    wait_filled(sp, ("o", b, o))
            for e in range(E):
                if e == RINGW:
                    sp.wait_ge(tables_done, 1)
                    sp.sem_inc(y_done, 1)
                if e >= RINGW:
                    sp.wait_ge(y_done, sp.value_load(tab_end[0:1, e - RINGW:e - RINGW + 1], min_val=1, max_val=NB + 1))
                sp.dma_start(wring[:, e % RINGW, :], w_exp[e]).then_inc(w_loaded, 16)
                sp.wait_ge(w_loaded, 16 * (e + 1))
                sp.sem_inc(w_ready, 1)
            for s in range(2):
                sp.wait_ge(y_sent[s], 16 * (NB // 2))
            for b in range(B):
                for k, dst in ((0, ya), (1, yb)):
                    sp.dma_start(dst[:, b * NQ:(b + 1) * NQ, :],
                                 yrows[k * T + b * S:k * T + (b + 1) * S, :].rearrange("(i p) d -> p i d", p=P)
                                 ).then_inc(y_back[b], 16)
            for b in range(B):
                sp.wait_ge(fin_done, b + 1)
                sp.dma_start(out[b * S:(b + 1) * S, :].rearrange("(i p) d -> p i d", p=P),
                             xtok[:, b * NQ:(b + 1) * NQ, 0:D]).then_inc(out_done, 16)
            sp.wait_ge(out_done, 16 * B)

        def scan_step_by_step(pool):
            n = [0]

            def link(ins):
                n[0] += 1
                ins.then_inc(fb_step, 1)
                pool.wait_ge(fb_step, n[0])
            dst = coef.rearrange("(q p) (w b n) -> w b p q n", p=P, w=3, b=B)
            for w, src in enumerate((abar[:, :, 0:NS], bbar, xdbl[:, :, NS:2 * NS])):
                for b in range(B):
                    pool.dma_start(dst[w, b], src.rearrange("p (q b) n -> p b q n", b=B)[:, b]).then_inc(fb_dma, 16)
            pool.wait_ge(fb_dma, 16 * 3 * B)
            for b in range(B):
                for j in range(NJ):
                    wait_drained(pool, ("y", b, j))
            link(pool.memset(fb_h, 0.0))
            per = 4
            base = n[0]
            ops = 8
            with pool.Fori(0, S // per) as it:
                pool.dma_start(fb_c, coef.rearrange("(c s) w -> c (s w)", s=per)[bass.ds(it, 1), :]
                               .squeeze(0).partition_broadcast(P)).then_inc(fb_dma, 16)
                pool.wait_ge(fb_dma, 16 * 3 * B + 16 * (it + 1))
                for s in range(per):
                    done = [it * (per * ops) + (base + s * ops)]

                    def step(ins):
                        done[0] = done[0] + 1
                        ins.then_inc(fb_step, 1)
                        pool.wait_ge(fb_step, done[0])
                    c = fb_c[:, s * 3 * B * NS:(s + 1) * 3 * B * NS].rearrange("p (w b n) -> p w b n", w=3, b=B)
                    full = [P, B, NJ, NS]
                    xs = xc.rearrange("p j (b t) -> p b j t", b=B)[:, :, :, bass.ds(it * per + s, 1)].to_broadcast(full)
                    step(pool.tensor_tensor(fb_h, fb_h, bc(c[:, 0], 2, full), ALU.mult))
                    step(pool.tensor_tensor(fb_t, xs, bc(c[:, 1], 2, full), ALU.mult))
                    step(pool.tensor_tensor(fb_h, fb_h, fb_t, ALU.add))
                    pool.sem_inc(fb_summed, 1)
                    step(pool.tensor_scalar(fb_h, fb_h, CLIP, -CLIP, ALU.min, ALU.max))
                    step(pool.tensor_tensor(fb_t, fb_h, bc(c[:, 2], 2, full), ALU.mult))
                    for w in (8, 4):
                        step(pool.tensor_tensor(fb_t[:, :, :, 0:w], fb_t[:, :, :, 0:w], fb_t[:, :, :, w:2 * w], ALU.add))
                    step(pool.tensor_tensor(fb_t[:, :, :, 0:2], fb_t[:, :, :, 0:2], fb_t[:, :, :, 2:4], ALU.add))
                    ydst = yx[:, 0:B, :].rearrange("p b (j t) -> p b j t", j=NJ)[:, :, :, bass.ds(it * per + s, 1)]
                    pool.tensor_tensor(ydst, fb_t[:, :, :, 0:1], fb_t[:, :, :, 1:2], ALU.add)

        @block.gpsimd
        def _(pool):
            count = [0]

            def link(ins):
                count[0] += 1
                ins.then_inc(pool_step, 1)
                pool.wait_ge(pool_step, count[0])

            def keep(ap, pattern, base, cm, op=ALU.is_ge, fill=0.0, out=None):
                link(pool.affine_select(out=out if out is not None else ap, in_=ap, pattern=pattern, compare_op=op,
                                        fill=fill, base=base, channel_multiplier=cm))
            link(pool.memset(xpad[:, :, 0:TAPS - 1], 0.0))
            link(pool.memset(ident[:, :], 0.0))
            keep(ident[:, :], [[-1, P]], 0, 1, ALU.not_equal, 1.0)
            link(pool.memset(ones[:, :], 1.0))
            keep(ones[:, :], [[1, P]], 0, -1, out=tri[:, :])
            keep(tri[:, :].rearrange("p (c t) -> p c t", t=CH), [[-CH, NC], [0, CH]], 0, 1,
                 out=tri32[:, :].rearrange("p (c t) -> p c t", t=CH))
            keep(ones[:, :].rearrange("p (c t) -> p c t", t=CH), [[CH, NC], [0, CH]], CH - 1, -1,
                 out=own[:, :].rearrange("p (c t) -> p c t", t=CH))
            for r in range(NC - 1):
                keep(ones[:, :], [[0, P]], CH * (r + 1) - 1, -1, out=upto[:, r * P:(r + 1) * P])
            keep(ones[:, 0:NC - 1], [[-CH, NC - 1]], 0, 1, out=mask_la[:, :])
            keep(mask_la[:, :], [[CH, NC - 1]], CH - 1, -1)
            keep(ones[:, 0:NC - 1], [[-CH, NC - 1]], -CH, 1, out=mask_ra[:, :])
            link(pool.memset(ones16[:, :], 1.0))
            keep(ones16[:, :], [[1, P]], 0, -1, ALU.is_gt, out=before16[:, :])
            link(pool.iota(eid[:, :], [[1, E]], base=0, channel_multiplier=0, allow_small_or_imprecise_dtypes=True))
            link(pool.iota(eoff[:, :], [[REGION, E]], base=0, channel_multiplier=0, allow_small_or_imprecise_dtypes=True))
            link(pool.iota(tokid[:, :], [[P, NT]], base=0, channel_multiplier=1, allow_small_or_imprecise_dtypes=True))
            link(pool.iota(steps128[:, :], [[P, NT]], base=0, channel_multiplier=0, allow_small_or_imprecise_dtypes=True))
            link(pool.iota(blkid[:, :], [[1, NB]], base=0, channel_multiplier=0, allow_small_or_imprecise_dtypes=True))
            link(pool.memset(padrow[:, :], 0.0))
            link(pool.iota(padrow[:, D:D + 1], [[0, 1]], base=T, channel_multiplier=1, allow_small_or_imprecise_dtypes=True))
            link(pool.memset(padrow[:, D + 1:D + 2], -1.0))
            for t in (dtA, abar, vabs, la, ra, lb, rb, rc, wt):
                link(pool.memset(t, 0.0))
            pool.memset(picksum[:, 0, :], 0.0).then_inc(consts_done, 1)

            pool.wait_ge(guard_done, 1)
            pool.partition_all_reduce(guardall, guard, P, RMAX).then_inc(guard_red, 1)
            pool.wait_ge(bad_done, 1)
            with pool.If(pool.value_load(bad[0:1, 0:1], min_val=0, max_val=1) > 0):
                scan_step_by_step(pool)
            pool.sem_inc(scan_checked, 1)

            pool.wait_ge(scan_checked, 1)
            for q in range(NQ - 1):
                wait_filled(pool, ("S", q))
            wait_drained(pool, "cumD")
            pool.memset(vaug[:, :, :, DH:DV], 1.0).then_inc(vones_done, 1)
            pool.wait_ge(fac_done, 1)
            pool.wait_ge(ld_ctx, 16 * (1 + H))
            link(pool.memset(negsel, 0.0))
            for b in range(B):
                keep(negsel, [[-1, H], [0, P]], -NSP * b, 1, ALU.not_equal, -1.0)

            def weigh_keys(b):
                if b:
                    wait_filled(pool, ("H", b - 1))
                pairs = [(s, c) for c in range(1, NQ) for s in range(c)]
                for n, (s, c) in enumerate(pairs):
                    ins = pool.tensor_tensor(kw[:, n], vaug[:, NQ * b + s, :, 0:DH],
                                             bc(fac[:, NQ - 1 + n, b, :], 2, [P, H, DH]), ALU.mult)
                ins.then_inc(kw_done, 1)

            def mask_tile(i):
                pool.wait_ge(arg_done, i + 1)
                pool.affine_select(out=decay[:, i % 2], in_=decay[:, i % 2], pattern=[[0, H], [1, P]],
                                   compare_op=ALU.is_ge, fill=-1.0e30, base=0, channel_multiplier=-1).then_inc(masked, 1)

            def scatter(b):
                pool.wait_ge(row_done, b + 1)
                for i in range(NQ * b, NQ * (b + 1)):
                    for k in range(2):
                        pool.indirect_dma_start(
                            out=slots, out_offset=bass.IndirectOffsetOnAxis(ap=pos[:, k, i:i + 1], axis=0),
                            in_=xtok[:, i, :], in_offset=None).then_inc(scattered, 16)

            weigh_keys(0)
            mask_tile(0)
            for i in range(NT):
                if i + 1 < NT:
                    if (i + 1) % NQ == 0:
                        weigh_keys((i + 1) // NQ)
                    mask_tile(i + 1)
                if i % NQ == 3 and i > NQ:
                    scatter(i // NQ - 1)
            scatter(B - 1)
            pool.wait_ge(tables_done, 1)
            pool.wait_ge(scattered, 16 * 2 * NT)
            for e in range(E):
                row = pool.value_load(tab_pad[0:1, e:e + 1], min_val=0, max_val=E * REGION)
                pool.dma_start(slots[bass.ds(row, P), :], padrow[:, :]).then_inc(padded, 16)
            pool.dma_start(slots[E * REGION:E * REGION + P, :], padrow[:, :]).then_inc(padded, 16)
            pool.wait_ge(padded, 16 * (E + 1))

            def load_block(g, s):
                row = pool.value_load(tab_slot[0:1, bass.ds(g, 1)], min_val=0, max_val=E * REGION)
                pool.dma_start(xg[:, s], slots[bass.ds(row, P), :]).then_inc(xg_loaded[s], 16)

            def send_block(g, s):
                pool.wait_ge(padded, 16 * (E + 1))
                pool.wait_ge(yout_done, g + 1)
                pool.indirect_dma_start(out=yrows, out_offset=bass.IndirectOffsetOnAxis(ap=rid[:, s:s + 1], axis=0),
                                        in_=yout[:, s], in_offset=None).then_inc(y_sent[s], 16)
            for s in range(2):
                load_block(s, s)
            with pool.Fori(0, NB // 2 - 1) as it:
                for s in range(2):
                    g = 2 * it + s
                    pool.wait_ge(xg_turned, g + 1)
                    pool.wait_ge(meta_done, g + 1)
                    load_block(g + 2, s)
                    send_block(g, s)
                    pool.wait_ge(y_sent[s], 16 * (it + 1))
            for s in range(2):
                send_block(NB - 2 + s, s)
                pool.wait_ge(y_sent[s], 16 * (NB // 2))

        @block.scalar
        def _(act):
            def conv_in(n):
                wait_filled(act, ("xp", n))
                if n == 0:
                    act.wait_ge(pool_step, 1)
                if n >= 4:
                    act.wait_ge(conv_done, n - 3)
                drain(("xp", n), act.copy(xpad[:, n % 4, TAPS - 1:TAPS - 1 + S], ps(("xp", n))[:, :]))

            def gate_in(n):
                b, j = divmod(n, NJ)
                wait_filled(act, ("z", n))
                drain(("z", n), act.activation(zs[:, j, b * S:(b + 1) * S], ps(("z", n))[:, :], ACT.Silu))

            def conv_out(n):
                b, j = divmod(n, NJ)
                act.wait_ge(conv_done, n + 1)
                act.activation(xc[:, j, b * S:(b + 1) * S], cbuf[:, n % 2], ACT.Silu).then_inc(xc_done, 1)

            def by_tokens(b):
                for q in range(NQ):
                    i = NQ * b + q
                    wait_filled(act, ("xt", i))
                    drain(("xt", i), act.copy(xct(b, q), ps(("xt", i))[:, :]))
            for n in range(B * NJ):
                if n % NJ == 2 and n > NJ:
                    by_tokens(n // NJ - 1)
                conv_in(n)
                gate_in(n)
                if n:
                    conv_out(n - 1)
            conv_out(B * NJ - 1)
            by_tokens(B - 1)

            act.wait_ge(ld_small, 16 * 6)
            act.activation(aneg, alog[:, :], ACT.Exp).then_inc(exp_done, 1)
            act.wait_ge(vmin_done, 1)
            act.activation(expv, horner, ACT.Exp).then_inc(exp_done, 1)
            act.wait_ge(dtA_done, 1)
            act.activation(abar[:, :, 0:NS], dtA[:, :, 0:NS], ACT.Exp).then_inc(exp_done, 1)
            act.wait_ge(cum_ready, 1)

            def cum(item, h):
                return ps(item)[:, h * 256:(h + 1) * 256].rearrange("p (i n) -> p i n", n=NS)
            act.activation(lb[:, :, 0:NS], cum("cumA", 0), ACT.Exp, scale=-1.0).then_inc(cumexp_done, 1)
            act.activation(rb[:, :, 0:NS], cum("cumA", 0), ACT.Exp).then_inc(cumexp_done, 1)
            act.activation(rc[:, :, 0:NS], cum("cumA", 1), ACT.Exp).then_inc(cumexp_done, 1)
            act.wait_ge(ediff_done, 1)
            act.activation(wt[:, :, 0:NS], wt[:, :, 0:NS], ACT.Exp).then_inc(cumexp_done, 1)
            act.activation(la[:, :, 3 * NS:4 * NS], la[:, :, 3 * NS:4 * NS], ACT.Exp).then_inc(cumexp_done, 1)
            act.activation(ediff, ediff, ACT.Exp).then_inc(cumexp_done, 1)
            wait_filled(act, "cumD")
            drain("cumD", act.activation(dec, ps("cumD")[:, 256:256 + NQ], ACT.Exp))
            wait_filled(act, "abT")
            drain("abT", act.copy(hst[:, 0], ps("abT")[:, :]))
            for item, dst in (("gcT", gcT), ("lbT", lbT), ("rbT", rbT), (("laT", 0), laT[:, 0]), (("laT", 1), laT[:, 1]),
                              (("raT", 0), raT[:, 0]), (("raT", 1), raT[:, 1])):
                wait_filled(act, item)
                drain(item, act.copy(dst, ps(item)[:, :].rearrange("p (q t) -> p q t", t=P)))
            for b in range(B):
                for j in range(NJ):
                    wait_filled(act, ("y", b, j))
                    drain(("y", b, j), act.copy(ybuf(b, j), ps(("y", b, j))[:, :]))
            for b in range(B):
                for k in range(KD):
                    wait_filled(act, ("x1t", b, k))
                    drain(("x1t", b, k), act.copy(xcol[:, k, b * S:(b + 1) * S], ps(("x1t", b, k))[:, :]))

            act.wait_ge(gabs_done, 1)
            act.activation(lfb, lfa, ACT.Exp, scale=-1.0).then_inc(act_step, 1)
            act.wait_ge(act_step, 1)
            act.activation(lfa, lfb, ACT.Ln, bias=1.0).then_inc(gexp_done, 1)
            wait_filled(act, "aT")
            drain("aT", act.copy(aT, ps("aT")[:, :]))
            wait_filled(act, "mT")
            drain("mT", act.copy(mS, ps("mT")[:, :].rearrange("p (q b n) -> p q b n", q=NQ, b=B)))
            act.wait_ge(args_done, 1)
            act.activation(fac, fac, ACT.Exp).then_inc(fac_done, 1)
            act.activation(emx, emx, ACT.Exp).then_inc(fac_done, 1)

            def states(b):
                wait_filled(act, ("H", b))
                drain(("H", b), act.copy(hs[:, b % 2], ps(("H", b))[:, 0:(NQ - 1) * 2 * DV].rearrange(
                    "p (c h d) -> p c h d", c=NQ - 1, h=2)))

            def decays(i):
                act.wait_ge(masked, i + 1)
                act.activation(decay[:, i % 2], decay[:, i % 2], ACT.Exp).then_inc(decay_done, 1)

            def norm2_turned(i):
                b, q = divmod(i, NQ)
                wait_filled(act, ("x2t", i))
                if b:
                    wait_filled(act, ("lg", b - 1))
                drain(("x2t", i), act.copy(x2c[:, q], ps(("x2t", i))[:, 0:D].rearrange("p (k t) -> p k t", k=KD)))

            def router_exp(b):
                act.wait_ge(rexp_in, b + 1)
                act.activation(rb_, rb_, ACT.Exp).then_inc(act_step, 1)
                act.activation(rc_, rc_, ACT.Exp).then_inc(rexp_done, 1)
            states(0)
            decays(0)
            for i in range(NT):
                if i + 1 < NT:
                    if (i + 1) % NQ == 0:
                        states((i + 1) // NQ)
                    decays(i + 1)
                if i % NQ == 2 and i > NQ:
                    for q in range(NQ):
                        norm2_turned(i - NQ - 2 + q)
                    router_exp(i // NQ - 1)
            for q in range(NQ):
                norm2_turned(NT - NQ + q)
            router_exp(B - 1)

            def expert_half(g, u):
                act.wait_ge(up_done, 2 * g + (u + 1))
                act.activation(gsil[:, u], bank[2 * u][:, :], ACT.Silu).then_inc(sil_done, 1)

            def turned_half(g, u):
                act.wait_ge(turned, 2 * g + (u + 1))
                act.copy(hT[:, u], bank[4 + u][:, :].rearrange("p (c t) -> p c t", t=P)).then_inc(hT_done, 1)

            expert_half(0, 0)
            with act.Fori(0, NB - 1) as g:
                expert_half(g, 1)
                turned_half(g, 0)
                expert_half(g + 1, 0)
                turned_half(g, 1)
            expert_half(NB - 1, 1)
            turned_half(NB - 1, 0)
            turned_half(NB - 1, 1)

        @block.vector
        def _(dve):
            count = [0]

            def link(ins):
                count[0] += 1
                ins.then_inc(dve_step, 1)
                dve.wait_ge(dve_step, count[0])

            def note(ins, s, value):
                ins.then_inc(s, 1)
                dve.wait_ge(s, value)

            def convolve(n):
                j = n % NJ
                src = xpad[:, n % 4]
                dst = cbuf[:, n % 2]
                wait_drained(dve, ("xp", n))
                if n >= 2:
                    dve.wait_ge(xc_done, n - 1)
                link(dve.tensor_scalar(dst, src[:, 0:S], convw[:, j, 0:1], convb[:, j:j + 1], ALU.mult, ALU.add))
                for k in range(1, TAPS - 1):
                    link(dve.scalar_tensor_tensor(dst, src[:, k:k + S], convw[:, j, k:k + 1], dst, ALU.mult, ALU.add))
                note(dve.scalar_tensor_tensor(dst, src[:, TAPS - 1:TAPS - 1 + S], convw[:, j, TAPS - 1:TAPS], dst,
                                              ALU.mult, ALU.add), conv_done, n + 1)

            def scan_inputs(b):
                wait_filled(dve, ("xd", b))
                drain(("xd", b), dve.tensor_copy(xdbl.rearrange("p (q b) n -> p b q n", b=B)[:, b],
                                                 ps(("xd", b))[:, 0:NQ * NX].rearrange("p (q n) -> p q n", n=NX)))

            def largest_input(b):
                for q in range(NQ):
                    wait_drained(dve, ("xt", NQ * b + q))
                    ins = dve.tensor_reduce(xmax[:, B * q + b:B * q + b + 1], xct(b, q), AX_X, ALU.max,
                                            apply_absolute_value=True)
                return ins
            dve.wait_ge(ld_conv, 16 * 3)
            for n in range(B * NJ):
                convolve(n)
                if n % NJ == 2 and n > NJ:
                    scan_inputs(n // NJ - 1)
                    link(largest_input(n // NJ - 1))
            dve.wait_ge(consts_done, 1)
            scan_inputs(B - 1)
            for b in range(B):
                wait_drained(dve, ("xd", b))
            note(dve.tensor_scalar(horner, xdbl[:, :, 2 * NS], -2.0, None, ALU.min), vmin_done, 1)
            link(largest_input(B - 1))
            dve.wait_ge(exp_done, 2)
            link(dve.tensor_scalar(aneg, aneg, -1.0, None, ALU.mult))
            link(dve.tensor_scalar(horner, expv, (-1.0) ** (HORNER + 1) / HORNER, None, ALU.mult))
            for k in range(HORNER - 1, 0, -1):
                link(dve.scalar_tensor_tensor(horner, horner, (-1.0) ** (k + 1) / k, expv, ALU.add, ALU.mult))
            link(dve.tensor_scalar(dtv, horner, DT_MIN, DT_MAX, ALU.max, ALU.min))
            full = [P, NT, NS]
            link(dve.tensor_tensor(dtA[:, :, 0:NS], bc(dtv, 2, full), bc(aneg, 1, full), ALU.mult))
            note(dve.tensor_scalar(dtA[:, :, 0:NS], dtA[:, :, 0:NS], -20.0, 0.0, ALU.max, ALU.min), dtA_done, 1)
            link(dve.tensor_tensor(bbar, xdbl[:, :, 0:NS], bc(dtv, 2, full), ALU.mult))
            link(dve.tensor_scalar(bbar, bbar, -10.0, 10.0, ALU.max, ALU.min))
            link(dve.scalar_tensor_tensor(vabs[:, :, 0:NS], bbar, -1.0, bbar, ALU.mult, ALU.max))
            note(dve.tensor_tensor(vabs[:, :, 0:NS], vabs[:, :, 0:NS], bc(xmax, 2, full), ALU.mult), guard_in, 1)

            def cum(item, h):
                return ps(item)[:, h * 256:(h + 1) * 256].rearrange("p (i n) -> p i n", n=NS)
            cmat = xdbl[:, :, NS:2 * NS]
            wait_filled(dve, "cumA")
            link(dve.tensor_copy(cumt, cum("cumA", 1)))
            note(dve.tensor_reduce(guard[:, 1:2], ps("cumA")[:, 0:256], AX_X, ALU.min, negate=True), cum_ready, 1)
            wait_filled(dve, "cumB")
            for r in range(2):
                link(dve.tensor_tensor(ediff[:, r], cumt, cum("cumB", r), ALU.subtract))
            wait_filled(dve, "cumC")
            link(dve.tensor_tensor(ediff[:, 2], cumt, cum("cumC", 0), ALU.subtract))
            link(dve.tensor_scalar(ediff, ediff, 0.0, None, ALU.min))
            drain("cumC", dve.tensor_tensor(wt[:, :, 0:NS], cum("cumC", 1), cumt, ALU.subtract))
            wait_drained(dve, "cumC")
            wait_filled(dve, "cumD")
            note(dve.tensor_tensor(la[:, :, 3 * NS:4 * NS], cum("cumD", 0), cumt, ALU.subtract), ediff_done, 1)
            dve.wait_ge(cumexp_done, 6)
            dve.sem_inc(drained[place["cumA"][0]], 1)
            dve.sem_inc(drained[place["cumB"][0]], 1)
            link(dve.tensor_tensor(lb[:, :, 0:NS], lb[:, :, 0:NS], bbar, ALU.mult))
            link(dve.tensor_tensor(rb[:, :, 0:NS], rb[:, :, 0:NS], cmat, ALU.mult))
            link(dve.tensor_tensor(rc[:, :, 0:NS], rc[:, :, 0:NS], cmat, ALU.mult))
            link(dve.tensor_tensor(wt[:, :, 0:NS], wt[:, :, 0:NS], bbar, ALU.mult))
            for r in range(NC - 1):
                link(dve.scalar_tensor_tensor(la[:, :, r * NS:(r + 1) * NS], la[:, :, 3 * NS:4 * NS], mask_la[:, r:r + 1],
                                              bbar, ALU.mult, ALU.mult))
                link(dve.scalar_tensor_tensor(ra[:, :, r * NS:(r + 1) * NS], ediff[:, r], mask_ra[:, r:r + 1],
                                              cmat, ALU.mult, ALU.mult))
            note(dve.memset(la[:, :, 3 * NS:4 * NS], 0.0), factors_done, 1)
            wait_drained(dve, "abT")
            wait_filled(dve, "vbT")
            drain("vbT", dve.tensor_tensor_scan(hst[:, 1], hst[:, 0], ps("vbT")[:, :], 0.0, ALU.mult, ALU.add))
            wait_drained(dve, "vbT")
            note(dve.tensor_reduce(guard[:, 0:1], hst[:, 1], AX_X, ALU.max), guard_done, 1)
            dve.wait_ge(guard_red, 1)
            link(dve.tensor_scalar(guardall[:, 0:1], guardall[:, 0:1], STATE_LIMIT, None, ALU.is_lt))
            link(dve.scalar_tensor_tensor(guardall[:, 0:1], guardall[:, 1:2], DECAY_LIMIT, guardall[:, 0:1],
                                          ALU.is_lt, ALU.mult))
            note(dve.tensor_scalar(bad[:, :], guardall[:, 0:1], -1.0, 1.0, ALU.mult, ALU.add), bad_done, 1)
            wait_drained(dve, "cumD")
            for q in range(NQ - 1):
                wait_filled(dve, ("S", q))
                if q == 0:
                    ins = dve.tensor_copy(hst[:, 0], ps(("S", 0))[:, :])
                else:
                    ins = dve.scalar_tensor_tensor(hst[:, q], hst[:, q - 1], dec[:, q:q + 1], ps(("S", q))[:, :],
                                                   ALU.mult, ALU.add)
                drain(("S", q), ins)
                wait_drained(dve, ("S", q))
            dve.sem_inc(hst_done, 1)

            def mix(b):
                m1 = ps(("M1", b))[:, :].rearrange("p (q t) -> p q t", t=P)
                mt = mts[:, b % 2]
                wait_filled(dve, ("M1", b))
                if b >= 2:
                    wait_filled(dve, ("y", b - 2, NJ - 1))
                drain(("M1", b), dve.tensor_tensor(mt, m1, bc(tri32[:, :], 1, [P, NQ, P]), ALU.mult))
                wait_drained(dve, ("M1", b))
                wait_filled(dve, ("M2", b))
                drain(("M2", b), dve.tensor_tensor(mt, mt, ps(("M2", b))[:, :].rearrange("p (q t) -> p q t", t=P), ALU.add))

            def gate(b):
                for j in range(NJ):
                    part = slice(b * S, (b + 1) * S)
                    wait_drained(dve, ("y", b, j))
                    link(dve.tensor_tensor(zs[:, j, part], zs[:, j, part], ybuf(b, j), ALU.mult))
                    note(dve.scalar_tensor_tensor(zs[:, j, part], xc[:, j, part], dpar[:, j:j + 1], zs[:, j, part],
                                                  ALU.mult, ALU.add), gated, NJ * b + j + 1)

            def rsqrt(var, eps, n):
                v, y, t = rsv[:, 0:n], rsy[:, 0:n], rst[:, 0:n]
                link(dve.tensor_scalar(v, var, eps, None, ALU.add))
                link(dve.tensor_scalar(y.bitcast(I32), v.bitcast(I32), 1, None, ALU.logical_shift_right))
                link(dve.tensor_scalar(y.bitcast(I32), y.bitcast(I32), -1.0, float(0x5F3759DF), ALU.mult, ALU.add))
                link(dve.tensor_scalar(v, v, -0.5, None, ALU.mult))
                for _ in range(NEWTON):
                    link(dve.tensor_tensor(t, y, y, ALU.mult))
                    link(dve.tensor_tensor(t, t, v, ALU.mult))
                    link(dve.scalar_tensor_tensor(y, t, 1.5, y, ALU.add, ALU.mult))

            def layernorm(tiles, eps):
                n = len(tiles)
                for k, i in enumerate(tiles):
                    ins = dve.bn_stats(stats[:, k, :], xtok[:, i, 0:D])
                link(ins)
                for k, i in enumerate(tiles):
                    ins = dve.bn_aggr(mv[:, k, :], stats[:, k, :])
                link(ins)
                rsqrt(mv[:, 0:n, 1], eps, n)
                for k, i in enumerate(tiles):
                    ins = dve.tensor_scalar(xtok[:, i, 0:D], xtok[:, i, 0:D], mv[:, k, 0:1], rsy[:, k:k + 1],
                                            ALU.subtract, ALU.mult)
                return ins

            def norm1(b):
                for o in range(2):
                    wait_filled(dve, ("o", b, o))
                    two = xtok[:, NQ * b + 2 * o:NQ * b + 2 * o + 2, 0:D]
                    drain(("o", b, o), dve.tensor_tensor(two, two, ps(("o", b, o))[:, :].rearrange("p (i d) -> p i d", d=D),
                                                         ALU.add))
                for o in range(2):
                    wait_drained(dve, ("o", b, o))
                note(layernorm(range(NQ * b, NQ * (b + 1)), 1e-5), x1_done, b + 1)
            for b in range(B):
                mix(b)
            dve.wait_ge(ld_x, 32)
            dve.wait_ge(ld_small, 16 * 6)
            dve.wait_ge(scan_checked, 1)
            gate(0)
            for b in range(B):
                if b + 1 < B:
                    gate(b + 1)
                norm1(b)

            all8 = [P, NT, 2 * H]
            wait_filled(dve, "g")
            drain("g", dve.tensor_tensor(gt, ps("g")[:, 0:NT * 2 * H].rearrange("p (i g) -> p i g", g=2 * H),
                                         bc(gb[:, :], 1, all8), ALU.add))
            wait_drained(dve, "g")
            note(dve.scalar_tensor_tensor(lfa, gt[:, :, H:2 * H], -1.0, gt[:, :, H:2 * H], ALU.mult, ALU.max), gabs_done, 1)
            dve.wait_ge(gexp_done, 1)
            link(dve.scalar_tensor_tensor(lfb, gt[:, :, H:2 * H], 0.0, lfa, ALU.min, ALU.subtract))
            link(dve.memset(apad, 0.0))
            lf4 = lfb.rearrange("p (b q) h -> p b q h", b=B)
            link(dve.memset(lfpre[:, :, 0, :], 0.0))
            for q in range(1, NQ):
                link(dve.tensor_tensor(lfpre[:, :, q, :], lfpre[:, :, q - 1, :], lf4[:, :, q - 1, :], ALU.add))
            dve.sem_inc(lf_done, 1)
            wait_filled(dve, "cum")
            csum = ps("cum")[:, 0:NT * H].rearrange("p (i h) -> p i h", h=H)
            link(dve.tensor_tensor(av, gt[:, :, 0:H], csum, ALU.subtract))
            drain("cum", dve.tensor_copy(cumS, csum))
            note(dve.tensor_copy(apad[:, :, 0:H], av), a_done, 1)
            wait_drained(dve, "aT")
            note(dve.tensor_tensor_scan(mrow, aT, aT, -BIG, ALU.max, ALU.max), mrow_done, 1)
            note(dve.tensor_tensor(zsel, bc(ident[:, :], 1, [P, NQ, P]), bc(mrow[:, P - 1:S:P], 2, [P, NQ, P]), ALU.mult),
                 z_done, 1)
            wait_drained(dve, "mT")
            wait_filled(dve, "R")
            rend = ps("R")[:, :].rearrange("p (q b n) -> p q b n", q=NQ, b=B)
            av4 = av.rearrange("p (b q) h -> p b q h", b=B)
            n = NQ - 1
            for c in range(1, NQ):
                link(dve.tensor_tensor(fac[:, c - 1], rend[:, c - 1, :, 0:H], mS[:, c, :, 0:H], ALU.subtract))
                for s in range(c):
                    ins = dve.tensor_tensor(fac[:, n], av4[:, :, s, :], rend[:, c - 1, :, 0:H], ALU.subtract)
                    n += 1
            drain("R", ins)
            wait_drained(dve, "R")
            wait_drained(dve, "cum")
            for q in range(NQ):
                cq = cumS.rearrange("p (b q) h -> p b q h", b=B)[:, :, q, :]
                ins = dve.scalar_tensor_tensor(emx.rearrange("p (b q) h -> p b q h", b=B)[:, :, q, :], cq, -1.0,
                                               mS[:, q, :, 0:H], ALU.mult, ALU.subtract)
            note(ins, args_done, 1)
            dve.wait_ge(fac_done, 2)
            link(dve.tensor_scalar(fac[:, 0:NQ - 1], fac[:, 0:NQ - 1], DH ** -0.5, None, ALU.mult))

            def exponents(i):
                wait_filled(dve, ("nm", i))
                if i >= 2:
                    dve.wait_ge(prob_done, 2 * (i - 1))
                k, _ = place[("nm", i)]
                ins = dve.tensor_tensor(decay[:, i % 2], ps(("nm", i))[:, :].rearrange("p (h s) -> p h s", h=H),
                                        bc(av[:, i, :], 2, [P, H, P]), ALU.add)
                note(ins, arg_done, i + 1)
                dve.sem_inc(drained[k], 1)

            def weights(i):
                b, c = divmod(i, NQ)
                dve.wait_ge(decay_done, i + 1)
                if i >= 2:
                    wait_filled(dve, ("num", i - 2))
                for par, item in ((0, ("sA", i)), (1, ("sB", i))):
                    wait_filled(dve, item)
                    sc = ps(item)[:, 0:2 * P].rearrange("p (h s) -> p h s", h=2)
                    ins = dve.scalar_tensor_tensor(prob[:, i % 2, par::2, :], sc, DH ** -0.5, decay[:, i % 2, par::2, :],
                                                   ALU.mult, ALU.mult)
                    ins.then_inc(prob_done, 1)
                    if c:
                        st = ps(item)[:, 2 * P:2 * P + 2 * DV].rearrange("p (h d) -> p h d", h=2)
                        ins = dve.tensor_tensor(tot[:, b % 2, c, par::2, :], st,
                                                bc(fac[:, c - 1, b, par::2], 2, [P, 2, DV]), ALU.mult)
                        drain(item, ins)
                    else:
                        dve.wait_ge(prob_done, 2 * i + par + 1)
                        dve.sem_inc(drained[place[item][0]], 1)

            def sums_of(i):
                b, c = divmod(i, NQ)
                tt = tot[:, b % 2, c]
                wait_filled(dve, ("num", i))
                num = ps(("num", i))[:, 0:H * DV].rearrange("p (h d) -> p h d", h=H)
                if c:
                    wait_drained(dve, ("sA", i))
                    wait_drained(dve, ("sB", i))
                    drain(("num", i), dve.tensor_tensor(tt, tt, num, ALU.add))
                else:
                    drain(("num", i), dve.tensor_copy(tt, num))

            def finish(b):
                tt = tot[:, b % 2]
                tiles = slice(NQ * b, NQ * (b + 1))
                for q in range(NQ):
                    wait_drained(dve, ("num", NQ * b + q))
                link(dve.scalar_tensor_tensor(den, tt[:, :, :, DH], -1.0, tt[:, :, :, DH], ALU.mult, ALU.max))
                link(dve.tensor_tensor(den, den, emx[:, tiles, :], ALU.max))
                link(dve.tensor_scalar(den, den, 1e-6, None, ALU.add))
                link(dve.reciprocal(den, den))
                link(dve.tensor_tensor(hbuf, tt[:, :, :, 0:DH], bc(den, 3, [P, NQ, H, DH]), ALU.mult))
                heads = hbuf.rearrange("p q h d -> p (q h) d")
                for n in range(NQ * H):
                    ins = dve.bn_stats(stats[:, n, :], heads[:, n, :])
                link(ins)
                for n in range(NQ * H):
                    ins = dve.bn_aggr(mv[:, n, :], stats[:, n, :])
                link(ins)
                rsqrt(mv[:, :, 1], 1e-6, NQ * H)
                full = [P, NQ * H, DH]
                link(dve.tensor_tensor(heads, heads, bc(mv[:, :, 0], 2, full), ALU.subtract))
                link(dve.tensor_tensor(heads, heads, bc(rsy, 2, full), ALU.mult))
                rows = hbuf.rearrange("p q h d -> p q (h d)")
                link(dve.tensor_tensor(rows, rows, bc(onw[:, :], 1, [P, NQ, D]), ALU.mult))
                link(dve.tensor_tensor(xtok[:, tiles, 0:D], xtok[:, tiles, 0:D], rows, ALU.add))
                note(layernorm(range(NQ * b, NQ * (b + 1)), 1e-5), x2_done, b + 1)

            def pick(dst, values, top, cand):
                full = [P, NQ, E]
                link(dve.tensor_reduce(top, values, AX_X, ALU.max))
                link(dve.tensor_tensor(cand, values, bc(top, 2, full), ALU.not_equal))
                link(dve.scalar_tensor_tensor(cand, cand, float(E), bc(eid[:, :], 1, full), ALU.mult, ALU.add))
                link(dve.tensor_reduce(sums[:, 0], cand, AX_X, ALU.min))
                link(dve.tensor_tensor(dst, bc(sums[:, 0], 2, full), bc(eid[:, :], 1, full), ALU.is_equal))

            def route_batch(b):
                full = [P, NQ, E]
                tiles = slice(NQ * b, NQ * (b + 1))
                wait_filled(dve, ("lg", b))
                drain(("lg", b), dve.tensor_copy(lg, ps(("lg", b))[:, 0:NQ * E].rearrange("p (q e) -> p q e", e=E)))
                wait_drained(dve, ("lg", b))
                if b:
                    dve.wait_ge(act_step, 1 + b)
                pick(oh1, lg, top1, ra_)
                link(dve.tensor_copy(xtok[:, tiles, D + 1], sums[:, 0]))
                link(dve.scalar_tensor_tensor(lg2, oh1, -BIG, lg, ALU.mult, ALU.add))
                pick(oh2, lg2, top2, ra_)
                note(dve.tensor_tensor(picks[:, tiles, :], oh1, oh2, ALU.add), picks_done, 2 * b + 1)
                for i in range(NQ * b, NQ * (b + 1)):
                    ins = dve.tensor_tensor(picksum[:, i + 1, :], picksum[:, i, :], picks[:, i, :], ALU.add)
                    if i + 1 < NQ * (b + 1):
                        link(ins)
                note(ins, picks_done, 2 * b + 2)
                for top, dst, base in ((top1, rb_, lg), (top2, rc_, lg2)):
                    tb = bc(top, 2, full)
                    link(dve.scalar_tensor_tensor(ra_, lg, -1.0, lg, ALU.mult, ALU.max))
                    link(dve.tensor_tensor(ra_, ra_, tb, ALU.max))
                    link(dve.tensor_tensor(dst, tb, lg, ALU.subtract))
                    link(dve.scalar_tensor_tensor(ra_, ra_, JITTER2, dst, ALU.mult, ALU.is_lt))
                    link(dve.tensor_tensor(dst, base, tb, ALU.subtract))
                    link(dve.scalar_tensor_tensor(dst, ra_, -1.0e30, dst, ALU.mult, ALU.add))
                dve.sem_inc(rexp_in, 1)
                wait_filled(dve, ("rk", b))
                rank = ps(("rk", b))[:, 0:NQ * E].rearrange("p (q e) -> p q e", e=E)
                drain(("rk", b), dve.tensor_tensor(lg, rank, bc(eoff[:, :], 1, full), ALU.add))
                wait_drained(dve, ("rk", b))
                for k, oh in ((0, oh1), (1, oh2)):
                    link(dve.tensor_tensor(ra_, oh, lg, ALU.mult))
                    link(dve.tensor_reduce(posf[:, k], ra_, AX_X, ALU.add))
                    link(dve.tensor_copy(pos[:, k, tiles], posf[:, k]))
                dve.wait_ge(rexp_done, b + 1)
                dve.wait_ge(act_step, 2 + b)
                for k, src in ((0, rb_), (1, rc_)):
                    link(dve.tensor_reduce(sums[:, k], src, AX_X, ALU.add))
                    link(dve.reciprocal(sums[:, k], sums[:, k]))
                    link(dve.tensor_copy(xtok[:, tiles, D + 2 + k], sums[:, k]))
                note(dve.tensor_copy(xtok[:, tiles, D], tokid[:, tiles]), row_done, b + 1)

            dve.wait_ge(consts_done, 1)
            exponents(0)
            for i in range(NT):
                weights(i)
                if i + 1 < NT:
                    exponents(i + 1)
                sums_of(i)
                if i % NQ == 1 and i > NQ:
                    finish(i // NQ - 1)
                if i % NQ == 2 and i > NQ:
                    route_batch(i // NQ - 1)
            finish(B - 1)
            route_batch(B - 1)

            wait_filled(dve, "cnt")
            drain("cnt", dve.tensor_copy(cnt[:, :], ps("cnt")[:, 0:E]))
            wait_drained(dve, "cnt")
            link(dve.tensor_tensor(cmp16, bc(cnt[:, :], 2, [P, E, NT]), bc(steps128[:, :], 1, [P, E, NT]), ALU.is_gt))
            link(dve.tensor_reduce(nblk[:, :], cmp16, AX_X, ALU.add))
            link(dve.memset(ringf[:, 0:E], 0.0))
            link(dve.tensor_tensor_scan(endblk[:, :], nblk[:, :], ringf[:, 0:E], 0.0, ALU.add, ALU.add))
            link(dve.tensor_scalar(ringf[:, 0:E], endblk[:, :], 1.0, None, ALU.add))
            link(dve.tensor_copy(tab_end[:, :], ringf[:, 0:E]))
            full = [P, NB, E]
            link(dve.tensor_tensor(cnt[:, :], cnt[:, :], eoff[:, :], ALU.add))
            link(dve.tensor_copy(tab_pad[:, :], cnt[:, :]))
            link(dve.tensor_tensor(cmpb, bc(blkid[:, :], 2, full), bc(endblk[:, :], 1, full), ALU.is_ge))
            link(dve.tensor_reduce(eblk[:, :], cmpb, AX_X, ALU.add))
            link(dve.tensor_scalar(used[:, :], eblk[:, :], float(E), None, ALU.is_lt))
            link(dve.tensor_tensor(cmpb, cmpb, bc(nblk[:, :], 1, full), ALU.mult))
            link(dve.tensor_reduce(sblk[:, :], cmpb, AX_X, ALU.add))
            link(dve.tensor_tensor(sblk[:, :], blkid[:, :], sblk[:, :], ALU.subtract))
            link(dve.tensor_scalar(ringf[:, :], eblk[:, :], float(REGION), None, ALU.mult))
            link(dve.scalar_tensor_tensor(sblk[:, :], sblk[:, :], float(P), ringf[:, :], ALU.mult, ALU.add))
            link(dve.tensor_scalar(sblk[:, :], sblk[:, :], float(E * REGION), None, ALU.min))
            link(dve.tensor_copy(tab_slot[:, :], sblk[:, :]))
            link(dve.tensor_scalar(eblk[:, :], eblk[:, :], float(E - 1), None, ALU.min))
            link(dve.tensor_scalar(ringf[:, :], eblk[:, :], 1.0, None, ALU.add))
            link(dve.tensor_copy(tab_ready[:, :], ringf[:, :]))
            link(dve.tensor_scalar(ringf[:, :], eblk[:, :], float(RINGW), -float(RINGW), ALU.is_ge, ALU.mult))
            for m in range(2 * RINGW, E, RINGW):
                link(dve.tensor_scalar(ringg[:, :], eblk[:, :], float(m), -float(RINGW), ALU.is_ge, ALU.mult))
                link(dve.tensor_tensor(ringf[:, :], ringf[:, :], ringg[:, :], ALU.add))
            link(dve.tensor_tensor(ringf[:, :], ringf[:, :], eblk[:, :], ALU.add))
            note(dve.tensor_copy(tab_ring[:, :], ringf[:, :]), tables_done, 1)

            def row_meta(g, s):
                dve.wait_ge(xg_loaded[s], 16 * (g // 2 + 1) if isinstance(g, int) else 8 * (g - s) + 16)
                if not (isinstance(g, int) and g < 2):
                    dve.wait_ge(y_sent[s], 8 * (g - s))
                m = meta[:, s]
                first, a, b_ = m[:, 0:1], m[:, 1:2], m[:, 2:3]
                chain = dve_chain(g)
                chain(dve.tensor_tensor(first, xg[:, s, D + 1:D + 2], eblk[:, bass.ds(g, 1)], ALU.is_equal))
                chain(dve.tensor_tensor(a, xg[:, s, D + 2:D + 3], first, ALU.mult))
                chain(dve.tensor_scalar(b_, first, -1.0, 1.0, ALU.mult, ALU.add))
                chain(dve.scalar_tensor_tensor(m[:, 3:4], b_, float(T), xg[:, s, D:D + 1], ALU.mult, ALU.add))
                chain(dve.tensor_copy(rid[:, s:s + 1], m[:, 3:4]))
                chain(dve.tensor_tensor(b_, b_, xg[:, s, D + 3:D + 4], ALU.mult))
                dve.tensor_tensor(m[:, 4:5], a, b_, ALU.add).then_inc(meta_done, 1)

            start = [count[0]]

            def dve_chain(g):
                done = [g * 6 + start[0]]

                def go(ins):
                    done[0] = done[0] + 1
                    ins.then_inc(dve_step, 1)
                    dve.wait_ge(dve_step, done[0])
                return go

            def turn_rows(g, s):
                dve.wait_ge(xg_turned, g + 1)
                dve.tensor_copy(xgT[:, s], bank[7][:, 0:D].rearrange("p (k t) -> p k t", k=KD)).then_inc(xgT_done, 1)

            def middle(g, u):
                dve.wait_ge(sil_done, 2 * g + (u + 1))
                dve.tensor_tensor(hmid[:, u], gsil[:, u], bank[2 * u + 1][:, :], ALU.mult).then_inc(mid_done, 1)

            def weigh_rows(g, s):
                dve.wait_ge(y_done, g + 2)
                dve.wait_ge(meta_done, g + 1)
                dve.tensor_scalar(yout[:, s], bank[6][:, 0:D], meta[:, s, 4:5], None, ALU.mult).then_inc(yout_done, 1)

            row_meta(0, 0)
            turn_rows(0, 0)
            middle(0, 0)

            def rest(g, s):
                row_meta(g + 1, 1 - s)
                turn_rows(g + 1, 1 - s)
                middle(g, 1)
                middle(g + 1, 0)
                weigh_rows(g, s)
            rest(0, 0)
            with dve.Fori(0, NB // 2 - 1) as it:
                for s in range(2):
                    rest(2 * it + (s + 1), 1 - s)
            middle(NB - 1, 1)
            weigh_rows(NB - 1, 1)

            for b in range(B):
                tiles = slice(NQ * b, NQ * (b + 1))
                dve.wait_ge(y_back[b], 32)
                if b == 0:
                    count[0] += 6 * NB
                    dve.wait_ge(scattered, 16 * 2 * NT)
                link(dve.tensor_tensor(ya[:, tiles, :], ya[:, tiles, :], yb[:, tiles, :], ALU.add))
                link(dve.tensor_tensor(xtok[:, tiles, 0:D], xtok[:, tiles, 0:D], ya[:, tiles, :], ALU.add))
                layernorm(range(NQ * b, NQ * (b + 1)), 1e-5).then_inc(fin_done, 1)

        @block.tensor
        def _(pe):
            def claim(item):
                k, n = place[item]
                if n:
                    pe.wait_ge(drained[k], n)
                return bank[k]

            def fill(item, ins):
                ins.then_inc(filled[place[item][0]], 1)

            def project(kind, n):
                b, j = divmod(n, NJ)
                o = claim((kind, n))
                col = (0 if kind == "xp" else DI) + j * P
                for k in range(KD):
                    mm = pe.matmul(o[:, :], winT[:, k, col:col + P], xcol[:, k, b * S:(b + 1) * S],
                                   start=(k == 0), stop=(k == KD - 1))
                fill((kind, n), mm)

            def scan_inputs(b):
                pe.wait_ge(xc_done, NJ * (b + 1))
                o = claim(("xd", b))
                for q in range(NQ):
                    t = b * S + q * P
                    for j in range(NJ):
                        mm = pe.matmul(o[:, q * NX:(q + 1) * NX], xc[:, j, t:t + P], wxT[:, j, :],
                                       start=(j == 0), stop=(j == NJ - 1))
                fill(("xd", b), mm)
                for q in range(NQ):
                    i = NQ * b + q
                    o = claim(("xt", i))
                    for j in range(NJ):
                        mm = pe.transpose(o[:, j * P:(j + 1) * P], xc[:, j, i * P:(i + 1) * P], ident[:, :])
                    fill(("xt", i), mm)
            pe.wait_ge(ld_first, 32)
            for n in range(B * NJ):
                project("xp", n)
                project("z", n)
                if n % NJ == 1 and n > NJ:
                    if n < 2 * NJ:
                        pe.wait_ge(consts_done, 1)
                        pe.wait_ge(ld_conv, 16 * 3)
                    scan_inputs(n // NJ - 1)
            scan_inputs(B - 1)

            pe.wait_ge(dtA_done, 1)

            def total(item, h, left, last=False):
                mm = pe.matmul(ps(item)[:, h * 256:(h + 1) * 256], left, dtA[:, :, 0:NS], start=True, stop=True)
                if last:
                    fill(item, mm)
            claim("cumA")
            total("cumA", 0, tri32[:, :])
            total("cumA", 1, tri[:, :], True)
            claim("cumB")
            total("cumB", 0, upto[:, 0:P])
            total("cumB", 1, upto[:, P:2 * P], True)
            claim("cumC")
            total("cumC", 0, upto[:, 2 * P:3 * P])
            total("cumC", 1, ones[:, :], True)
            claim("cumD")
            total("cumD", 0, own[:, :])

            def same_place(t, q):
                return t[:, B * q:B * (q + 1), :].rearrange("p b n -> p (b n)")
            for q in range(NQ):
                mm = pe.matmul(ps("cumD")[:, 256 + q:257 + q], same_place(dtA, q), ones[:, 0:1], start=True, stop=True)
            fill("cumD", mm)
            pe.wait_ge(exp_done, 3)
            pe.wait_ge(guard_in, 1)

            def turn4(item, src):
                o = claim(item)
                for q in range(NQ):
                    mm = pe.transpose(o[:, q * P:(q + 1) * P], src(q), ident[:, :])
                fill(item, mm)
            turn4("abT", lambda q: same_place(abar, q))
            turn4("vbT", lambda q: same_place(vabs, q))
            pe.wait_ge(factors_done, 1)
            turn4("gcT", lambda q: same_place(rc, q))
            turn4("lbT", lambda q: same_place(lb, q))
            turn4("rbT", lambda q: same_place(rb, q))
            for name, src in (("laT", la), ("raT", ra)):
                for g in range(2):
                    turn4((name, g), lambda q: src[:, B * q + 2 * g:B * q + 2 * g + 2, :].rearrange("p b n -> p (b n)"))
            for q in range(NQ - 1):
                o = claim(("S", q))
                for b in range(B):
                    mm = pe.matmul(o[NSP * b:NSP * (b + 1), :], wt[:, B * q + b, :], xct(b, q), start=True, stop=True)
                fill(("S", q), mm)
            for item in ("gcT", "lbT", "rbT", ("laT", 0), ("laT", 1), ("raT", 0), ("raT", 1)):
                wait_drained(pe, item)

            def mixes(b):
                o = claim(("M1", b))
                r = slice(NSP * b, NSP * (b + 1))
                for q in range(NQ):
                    mm = pe.matmul(o[:, q * P:(q + 1) * P], lbT[r, q, :], rbT[r, q, :], start=True, stop=True)
                fill(("M1", b), mm)
                o = claim(("M2", b))
                r = slice(64 * (b % 2), 64 * (b % 2) + 64)
                for q in range(NQ):
                    mm = pe.matmul(o[:, q * P:(q + 1) * P], laT[r, b // 2, q, :], raT[r, b // 2, q, :], start=True, stop=True)
                fill(("M2", b), mm)

            def outputs(b):
                wait_drained(pe, ("M2", b))
                r = slice(NSP * b, NSP * (b + 1))
                for j in range(NJ):
                    o = claim(("y", b, j))
                    for q in range(NQ):
                        part = o[:, q * P:(q + 1) * P]
                        mm = pe.matmul(part, xct(b, q)[:, j * P:(j + 1) * P], mts[:, b % 2, q, :], start=True, stop=(q == 0))
                        if q:
                            mm = pe.matmul(part, hst[r, q - 1, j * P:(j + 1) * P], gcT[r, q, :], start=False, stop=True)
                    fill(("y", b, j), mm)
            for b in range(B):
                mixes(b)
                if b == 0:
                    pe.wait_ge(hst_done, 1)
                outputs(b)

            def out_project(b):
                pe.wait_ge(gated, NJ * (b + 1))
                if b == 0:
                    pe.wait_ge(ld_x, 32)
                for o2 in range(2):
                    o = claim(("o", b, o2))
                    for q in range(2):
                        t = (NQ * b + 2 * o2 + q) * P
                        for j in range(NJ):
                            mm = pe.matmul(o[:, q * D:(q + 1) * D], zs[:, j, t:t + P], woutT[:, j, :],
                                           start=(j == 0), stop=(j == NJ - 1))
                    fill(("o", b, o2), mm)

            def turn_norm1(b):
                pe.wait_ge(x1_done, b + 1)
                for k in range(KD):
                    o = claim(("x1t", b, k))
                    for q in range(NQ):
                        mm = pe.transpose(o[:, q * P:(q + 1) * P], xtok[:, NQ * b + q, k * P:(k + 1) * P], ident[:, :])
                    fill(("x1t", b, k), mm)
            for b in range(B):
                out_project(b)
                if b:
                    turn_norm1(b - 1)
            turn_norm1(B - 1)

            for b in range(B):
                for k in range(KD):
                    wait_drained(pe, ("x1t", b, k))
            pe.wait_ge(ld_ctx, 16 * (1 + H))
            pe.wait_ge(ld_small, 16 * 6)
            o = claim("g")
            for i in range(NT):
                t = slice(i * P, (i + 1) * P)
                for n, src in enumerate((xcol, ctxc, ctxc)):
                    for k in range(KD):
                        mm = pe.matmul(o[:, i * 2 * H:(i + 1) * 2 * H], src[:, k, t], gk[:, n * KD + k, :],
                                       start=(n == 0 and k == 0), stop=(n == 2 and k == KD - 1))
            fill("g", mm)
            pe.wait_ge(lf_done, 1)
            o = claim("cum")
            pe.matmul(o[:, 0:NT * H], tri[:, :], lfb, start=True, stop=False)
            fill("cum", pe.matmul(o[:, 0:NT * H], ones[:, :], lfpre, start=False, stop=True))
            pe.wait_ge(a_done, 1)
            o = claim("aT")
            for i in range(NT):
                b, q = divmod(i, NQ)
                mm = pe.matmul(o[NSP * b:NSP * (b + 1), q * P:(q + 1) * P], apad[:, i, :], ident[:, :], start=True, stop=True)
            fill("aT", mm)
            pe.wait_ge(mrow_done, 1)
            o = claim("mT")
            for q in range(NQ):
                mm = pe.transpose(o[:, q * P:(q + 1) * P], mrow[:, q * P:(q + 1) * P], ident[:, :])
            fill("mT", mm)
            pe.wait_ge(z_done, 1)
            o = claim("R")
            fill("R", pe.matmul(o[:, :], ones[:, :], zsel, start=True, stop=True))

            def states(b):
                pe.wait_ge(kw_done, b + 1)
                pe.wait_ge(vones_done, 1)
                o = claim(("H", b))
                n = 0
                for c in range(1, NQ):
                    for h in range(H):
                        r = slice(64 * (h % 2), 64 * (h % 2) + 64)
                        col = ((c - 1) * 2 + h // 2) * DV
                        for s in range(c):
                            mm = pe.matmul(o[r, col:col + DV], kw[:, n + s, h, :], vaug[:, NQ * b + s, h, :],
                                           start=(s == 0), stop=(s == c - 1))
                    n += c
                fill(("H", b), mm)

            def front(i):
                b, c = divmod(i, NQ)
                t = slice(i * P, (i + 1) * P)
                if c == 0:
                    states(b)
                o = claim(("nm", i))
                r = slice(NSP * b, NSP * (b + 1))
                for h in range(H):
                    mm = pe.matmul(o[:, h * P:(h + 1) * P], negsel[r, h, :], mrow[r, c * P:(c + 1) * P],
                                   start=True, stop=True)
                fill(("nm", i), mm)
                if c:
                    wait_drained(pe, ("H", b))
                for par, item in ((0, ("sA", i)), (1, ("sB", i))):
                    o = claim(item)
                    r = slice(64 * par, 64 * par + 64)
                    for k in range(KD):
                        mm = pe.matmul(o[:, k * P:(k + 1) * P], ctxc[r, k, t], xcol[r, k, t], start=True, stop=True)
                    for k in range(KD if c else 0):
                        mm = pe.matmul(o[:, 2 * P + k * DV:2 * P + (k + 1) * DV], xcol[r, k, t], hs[r, b % 2, c - 1, k, :],
                                       start=True, stop=True)
                    fill(item, mm)

            def values(i):
                pe.wait_ge(prob_done, 2 * (i + 1))
                o = claim(("num", i))
                for h in range(H):
                    mm = pe.matmul(o[:, h * DV:(h + 1) * DV], prob[:, i % 2, h, :], vaug[:, i, h, :], start=True, stop=True)
                fill(("num", i), mm)

            def turn_norm2(b):
                pe.wait_ge(x2_done, b + 1)
                for i in range(NQ * b, NQ * (b + 1)):
                    o = claim(("x2t", i))
                    for k in range(KD):
                        mm = pe.transpose(o[:, k * P:(k + 1) * P], xtok[:, i, k * P:(k + 1) * P], ident[:, :])
                    fill(("x2t", i), mm)

            def logits(b):
                o = claim(("lg", b))
                for q in range(NQ):
                    wait_drained(pe, ("x2t", NQ * b + q))
                    for k in range(KD):
                        mm = pe.matmul(o[:, q * E:(q + 1) * E], x2c[:, q, k, :], rw[:, k, :],
                                       start=(k == 0), stop=(k == KD - 1))
                fill(("lg", b), mm)

            def ranks(b):
                pe.wait_ge(picks_done, 2 * (b + 1))
                o = claim(("rk", b))
                pe.matmul(o[:, 0:NQ * E], before16[:, :], picks[:, NQ * b:NQ * (b + 1), :], start=True, stop=False)
                fill(("rk", b), pe.matmul(o[:, 0:NQ * E], ones16[:, :], picksum[:, NQ * b:NQ * (b + 1), :],
                                          start=False, stop=True))
            front(0)
            for i in range(NT):
                if i + 1 < NT:
                    front(i + 1)
                if i % NQ == 2 and i > NQ:
                    turn_norm2(i // NQ - 1)
                    logits(i // NQ - 1)
                if i % NQ == 3 and i > NQ:
                    ranks(i // NQ - 1)
                values(i)
            turn_norm2(B - 1)
            logits(B - 1)
            ranks(B - 1)
            fill("cnt", pe.matmul(claim("cnt")[:, 0:E], ones16[:, :], picksum[:, NT, :], start=True, stop=True))

            wait_drained(pe, "cnt")
            pe.wait_ge(tables_done, 1)

            def turn_rows(g, s):
                pe.wait_ge(xg_loaded[s], 8 * (g - s) + 16)
                if not isinstance(g, int) or g:
                    pe.wait_ge(xgT_done, g)
                for k in range(KD):
                    mm = pe.transpose(bank[7][:, k * P:(k + 1) * P], xg[:, s, k * P:(k + 1) * P], ident[:, :])
                mm.then_inc(xg_turned, 1)

            def ready_of(g):
                return pe.value_load(tab_ready[0:1, bass.ds(g, 1)], min_val=1, max_val=E)

            def ring_of(g):
                return pe.value_load(tab_ring[0:1, bass.ds(g, 1)], min_val=0, max_val=RINGW - 1)

            def moving(ring, col, n):
                return wring[:, bass.ds(ring, 1), col:col + n].squeeze(1)

            def up(g, s, u, ring):
                pe.wait_ge(xgT_done, g + 1)
                if not isinstance(g, int) or g:
                    pe.wait_ge(mid_done, 2 * g + (u - 1))
                for m in range(2):
                    for k in range(KD):
                        mm = pe.matmul(bank[2 * u + m][:, :], xgT[:, s, k, :],
                                       moving(ring, m * KD * F + k * F + u * HALF, HALF), start=(k == 0), stop=(k == KD - 1))
                mm.then_inc(up_done, 1)

            def down(g, u, ring):
                pe.wait_ge(mid_done, 2 * g + (u + 1))
                for c in range(4):
                    mm = pe.transpose(bank[4 + u][:, c * P:(c + 1) * P], hmid[:, u, c * P:(c + 1) * P], ident[:, :])
                mm.then_inc(turned, 1)
                pe.wait_ge(hT_done, 2 * g + (u + 1))
                if u == 0 and (not isinstance(g, int) or g):
                    pe.wait_ge(yout_done, g)
                for c in range(4):
                    mm = pe.matmul(bank[6][:, 0:D], hT[:, u, c, :], moving(ring, 2 * KD * F + (4 * u + c) * D, D),
                                   start=(u == 0 and c == 0), stop=(u == 1 and c == 3))
                if u == 1:
                    mm.then_inc(y_done, 1)

            def expert_block(g, s, last=False):
                ring = ring_of(g)
                up(g, s, 1, ring)
                down(g, 0, ring)
                if not last:
                    ready, next_ring = ready_of(g + 1), ring_of(g + 1)
                    turn_rows(g + 1, 1 - s)
                    pe.wait_ge(w_ready, ready)
                    up(g + 1, 1 - s, 0, next_ring)
                down(g, 1, ring)
            turn_rows(0, 0)
            ready, next_ring = ready_of(0), ring_of(0)
            pe.wait_ge(w_ready, ready)
            up(0, 0, 0, next_ring)
            expert_block(0, 0)
            with pe.Fori(0, NB // 2 - 1) as it:
                for s in range(2):
                    expert_block(2 * it + (s + 1), 1 - s)
            expert_block(NB - 1, 1, last=True)


_INS = ["x", "xT", "ctx", "ctxT", "w_inT", "conv_w", "conv_b", "w_xT", "a_log", "d_param", "w_outT", "gate_k", "gate_b",
        "outnorm", "router_w", "w_exp"]


def kernel(**inputs):
    import numpy as np
    import concourse.bacc as bacc
    from concourse.bass_utils import run_bass_kernel_spmd

    a = {k: np.asarray(v) for k, v in inputs.items()}
    x, ctx = (a[k].reshape(T, D) for k in ("x", "ctx_1024"))
    w1, w3 = (a[k].reshape(E, KD, P, F).transpose(0, 2, 1, 3).reshape(E, P, KD * F) for k in ("L0_ffn_w1", "L0_ffn_w3"))
    w2 = a["L0_ffn_w2"].reshape(E, F // P, P, D).transpose(0, 2, 1, 3).reshape(E, P, (F // P) * D)
    laid = {
        "x": x, "xT": x.T, "ctx": ctx, "ctxT": ctx.T,
        "w_inT": a["L0_attn_W_in"].T, "conv_w": a["L0_attn_conv_w"], "conv_b": a["L0_attn_conv_b"].reshape(NJ, P).T,
        "w_xT": a["L0_attn_W_xproj"].T, "a_log": a["L0_attn_A_log"], "d_param": a["L0_attn_D_param"].reshape(NJ, P).T,
        "w_outT": a["L0_attn_W_out"].T,
        "gate_k": np.concatenate([a["L0_xattn_ig_kernel"], a["L0_xattn_fg_kernel"]], axis=1),
        "gate_b": np.concatenate([a["L0_xattn_ig_bias"], a["L0_xattn_fg_bias"]]),
        "outnorm": a["L0_xattn_outnorm_weight"].reshape(D), "router_w": a["L0_ffn_gate_w"],
        "w_exp": np.concatenate([w1, w3, w2], axis=2),
    }
    nc = bacc.Bacc("TRN2", target_bir_lowering=False, num_devices=1)
    arrays, args = {}, []
    for name in _INS:
        v = np.ascontiguousarray(laid[name])
        arrays[f"in_{name}"] = v
        args.append(nc.dram_tensor(f"in_{name}", v.shape, mybir.dt.from_np(v.dtype), kind="ExternalInput").ap())
    args.append(nc.dram_tensor("out", (T, D), F32, kind="ExternalOutput").ap())
    decoder_kernel(nc, *args)
    r = run_bass_kernel_spmd(nc, [arrays], core_ids=[0])
    return r.results[0]["out"].reshape(B, S, D)
```

```python
from contextlib import ExitStack

import concourse.bass as bass
from concourse import mybir

F32 = mybir.dt.float32
F32R = mybir.dt.float32r
BF16 = mybir.dt.bfloat16
I32 = mybir.dt.int32
ALU = mybir.AluOpType
ACT = mybir.ActivationFunctionType
AX_X = mybir.AxisListType.X
RMAX = bass.bass_isa.ReduceOp.max

P = 128
B, S, D = 4, 512, 256
T = B * S
NQ = S // P
NT = T // P
KD = D // P
DI = 2 * D
NJ = DI // P
NS, NSP = 16, 32
TAPS = 4
NX = 2 * NS + 1
CH = 32
NC = P // CH
H = 4
DH = D // H
DV = DH + 1
E, F = 8, 1024
HALF = F // 2
NB = (2 * T + E * (P - 1)) // P + 1
NB += NB % 2
REGION = T + P
ROW = D + 4
WCOLS = 2 * KD * F + (F // P) * D
SURE = 2 * T // P // 2
DT_MIN, DT_MAX = 0.001, 0.1
CLIP = 100.0
JITTER2 = 0.02
BIG = 3.0e38
HORNER = 10
NEWTON = 3
STATE_LIMIT, DECAY_LIMIT = 99.0, 80.0


def decoder_kernel(nc, x, xT, ctx, ctxT, w_inT, conv_w, conv_b, w_xT, a_log, d_param, w_outT, gate_k, gate_b,
                   outnorm, router_w, w_exp, out):
    slots = nc.dram_tensor("slots", [(E * REGION) + P, ROW], F32).ap()
    yrows = nc.dram_tensor("yrows", [2 * T + P, D], F32).ap()
    yscan = nc.dram_tensor("scan_out", [P, B, NJ, S], F32).ap()
    coef = nc.dram_tensor("scan_coef", [S, 3 * B * NS], F32).ap()

    with ExitStack() as stack:
        def sb(name, cols, dt=F32):
            return stack.enter_context(nc.sbuf_tensor(name, [P, cols], dt))

        def sem(name):
            return stack.enter_context(nc.semaphore(name))

        xtok = sb("xtok", NT * ROW)[:, :].rearrange("p (i c) -> p i c", c=ROW)
        xcol = sb("xcol", KD * T)[:, :].rearrange("p (k t) -> p k t", k=KD)
        n1, n2, n3, n4 = KD * 2 * DI + 4 * 516 + 2 * S, NT * H * DV + KD * T, NJ * T, 3 * WCOLS
        with ExitStack() as early:
            region1, region2, region3, region4 = (
                early.enter_context(nc.sbuf_tensor(f"region{k + 1}", [P, n], F32))[:, :] for k, n in enumerate((n1, n2, n3, n4)))
        with nc.sbuf_tensor("under_wstage", [P, n1 + n2 + n3], F32), nc.sbuf_tensor("wstage", [P, WCOLS], F32) as raw:
            wstage = raw[:, :]
        region1r = sb("experts_x", n1, F32R)
        bigr = sb("experts_w", n2 + n3 + n4, F32R)
        region3r = bigr[:, n2:n2 + n3]

        def carve(region, at, shape):
            n = 1
            for s in shape:
                n *= s
            v = region[:, at[0]:at[0] + n]
            at[0] += n
            names = "abcdef"[:len(shape)]
            if len(shape) == 1:
                return v
            return v.rearrange(f"p ({' '.join(names)}) -> p {' '.join(names)}",
                               **{c: s for c, s in zip(names[1:], shape[1:])})

        at = [0]
        winT = carve(region1, at, (KD, 2 * DI))
        xpad = carve(region1, at, (4, 516))
        cbuf = carve(region1, at, (2, S))
        at = [0]
        gcT = carve(region1, at, (NQ, P))
        lbT = carve(region1, at, (NQ, P))
        rbT = carve(region1, at, (NQ, P))
        laT = carve(region1, at, (2, NQ, P))
        raT = carve(region1, at, (2, NQ, P))
        hst = carve(region1, at, (NQ - 1, DI))
        at = [0]
        xdbl = carve(region2, at, (NT, NX))
        dtA = carve(region2, at, (NT, NSP))
        abar = carve(region2, at, (NT, NSP))
        vabs = carve(region2, at, (NT, NSP))
        bbar = carve(region2, at, (NT, NS))
        cumt = carve(region2, at, (NT, NS))
        ediff = carve(region2, at, (NC - 1, NT, NS))
        la = carve(region2, at, (NT, 4 * NS))
        ra = carve(region2, at, (NT, 4 * NS))
        lb = carve(region2, at, (NT, NSP))
        rb = carve(region2, at, (NT, NSP))
        rc = carve(region2, at, (NT, NSP))
        wt = carve(region2, at, (NT, NSP))
        aneg = carve(region2, at, (NS,))
        assert at[0] <= NT * H * DV + KD * T, at
        at = [0]
        vaug = carve(region2, at, (NT, H, DV))
        ctxc = carve(region2, at, (KD, T))
        at = [0]
        xc = carve(region3, at, (NJ, T))
        at = [0]
        aT = region3[:, 0:S]
        zsel = carve(region3, at, (NQ, P))
        mrow = carve(region3, at, (S,))
        mS = carve(region3, at, (NQ, B, NSP))
        decay = carve(region3, at, (2, H, P))
        prob = carve(region3, at, (2, H, P))
        kw = carve(region3, at, (6, H, DH))
        hs = carve(region3, at, (2, NQ - 1, 2, DV))
        late = 2 * WCOLS - n2
        tot_at = NJ * T - 2 * NQ * H * DV
        assert max(at[0], late) <= tot_at, at
        tot = carve(region3, [tot_at], (2, NQ, H, DV))
        at = [0]
        zs = carve(region4, at, (NJ, T))
        yx = carve(region4, at, (B + 1, NQ * DI))
        assert at[0] <= 3 * WCOLS, at

        def xct(b, q):
            return yx[:, b + 1, q * DI:(q + 1) * DI]

        def ybuf(b, j):
            return yx[:, b, j * S:(j + 1) * S]
        slot_at = (n2 + n3 + WCOLS, 0)

        def wslot(off):
            return bigr[:, bass.ds(off, 2 * WCOLS)]
        at = [0]
        xg = carve(region1, at, (2, ROW))
        xTh = carve(region1r, at, (2, KD, P))
        xTl = carve(region1r, at, (2, KD, P))
        gsil = carve(region1, at, (2, HALF))
        hmid = carve(region1, at, (2, HALF))
        yout = carve(region1, at, (2, D))
        assert at[0] <= KD * 2 * DI + 4 * 516 + 2 * S
        at = [late]
        hTh = carve(region3r, at, (2, 4, P))
        hTl = carve(region3r, at, (2, 4, P))
        assert at[0] <= NJ * T, at
        ya = region2[:, 0:NT * D].rearrange("p (i d) -> p i d", d=D)
        yb = region2[:, NT * D:2 * NT * D].rearrange("p (i d) -> p i d", d=D)

        woutT = sb("woutT", NJ * D)[:, :].rearrange("p (j d) -> p j d", j=NJ)
        wxT = sb("wxT", NJ * NX)[:, :].rearrange("p (j n) -> p j n", j=NJ)
        convw = sb("convw", NJ * TAPS)[:, :].rearrange("p (j k) -> p j k", j=NJ)
        convb = sb("convb", NJ)
        dpar = sb("dpar", NJ)
        alog = sb("alog", NS)
        gk = sb("gk", 3 * KD * 2 * H)[:, :].rearrange("p (k g) -> p k g", k=3 * KD)
        gb = sb("gb", 2 * H)
        onw = sb("onw", D)
        rw = sb("rw", KD * E)[:, :].rearrange("p (k e) -> p k e", k=KD)

        ident = sb("ident", P)
        ones = sb("ones", P)
        tri = sb("tri", P)
        tri32 = sb("tri32", P)
        own = sb("own", P)
        upto = sb("upto", (NC - 1) * P)
        before16 = sb("before16", P, BF16)
        ones16 = sb("ones16", P, BF16)
        mask_la = sb("mask_la", NC - 1)
        mask_ra = sb("mask_ra", NC - 1)
        eid = sb("eid", E)
        eoff = sb("eoff", E)
        tokid = sb("tokid", NT)
        steps128 = sb("steps128", NT)
        blkid = sb("blkid", NB + 2)
        padrow = sb("padrow", ROW)

        small = sb("small", 996)
        at = [0]
        dtv = carve(small, at, (NT,))
        expv = carve(small, at, (NT,))
        horner = carve(small, at, (NT,))
        xmax = carve(small, at, (NT,))
        guard = carve(small, at, (2,))
        guardall = carve(small, at, (2,))
        dec = carve(small, at, (NQ,))
        stats = carve(small, at, (NQ * H, 6))
        mv = carve(small, at, (NQ * H, 2))
        rsv = carve(small, at, (NQ * H,))
        rsy = carve(small, at, (NQ * H,))
        rst = carve(small, at, (NQ * H,))
        gt = carve(small, at, (NT, 2 * H))
        lfa = carve(small, at, (NT, H))
        lfb = carve(small, at, (NT, H))
        lfpre = carve(small, at, (B, NQ, H))
        av = carve(small, at, (NT, H))
        cumS = carve(small, at, (NT, H))
        emx = carve(small, at, (NT, H))
        fac = carve(small, at, (9, B, H))
        den = carve(small, at, (NQ, H))
        assert at[0] <= 996, at
        bad = sb("bad", 1, I32)

        at = [0]
        negsel = carve(region1, at, (H, P))
        apad = carve(region1, at, (NT, NSP))
        hbuf = carve(region1, at, (NQ, H, DH))
        x2c = carve(region1, at, (NQ, KD, P))
        cmp16 = carve(region1, at, (E, NT))
        cmpb = carve(region1, at, (NB + 2, E))
        lg = carve(region1, at, (NQ, E))
        lg2 = carve(region1, at, (NQ, E))
        oh1 = carve(region1, at, (NQ, E))
        oh2 = carve(region1, at, (NQ, E))
        ra_ = carve(region1, at, (NQ, E))
        rb_ = carve(region1, at, (NQ, E))
        rc_ = carve(region1, at, (NQ, E))
        top1 = carve(region1, at, (NQ,))
        top2 = carve(region1, at, (NQ,))
        posf = carve(region1, at, (2, NQ))
        sums = carve(region1, at, (2, NQ))
        assert at[0] <= KD * 2 * DI + 4 * 516 + 2 * S
        pos = sb("pos", 2 * NT, I32)[:, :].rearrange("p (k i) -> p k i", k=2)
        picks = sb("picks", NT * E, BF16)[:, :].rearrange("p (i e) -> p i e", e=E)
        picksum = sb("picksum", (NT + 1) * E, BF16)[:, :].rearrange("p (i e) -> p i e", e=E)
        cnt = sb("cnt", E)
        nblk = sb("nblk", E)
        endblk = sb("endblk", E)
        eblk = sb("eblk", NB + 2)
        sblk = sb("sblk", NB + 2)
        hasblk = sb("hasblk", E)
        cumev = sb("cumev", E)
        evblk = sb("evblk", NB)
        tab_slot = sb("tab_slot", NB + 2, I32)
        tab_event = sb("tab_event", NB, I32)
        tab_noff = sb("tab_noff", NB, I32)
        tab_first = sb("tab_first", NB, I32)
        tab_pad = sb("tab_pad", E, I32)
        tab_ev = sb("tab_ev", E + 2, I32)
        tab_n = sb("tab_n", 3, I32)
        ringf = sb("ringf", NB + 2)
        ringg = sb("ringg", NB)
        zero = sb("zero", 1)
        meta = sb("meta", 2 * 6)[:, :].rearrange("p (s c) -> p s c", s=2)
        rid = sb("rid", 2, I32)
        fb_c = carve(region1, [2 * B * NJ * NS], (4 * 3 * B * NS,))
        mts = xcol[:, :, (B - 1) * S:].rearrange("p s (q t) -> p s q t", q=NQ)
        fb_h = carve(region1, [0], (B, NJ, NS))
        fb_t = carve(region1, [B * NJ * NS], (B, NJ, NS))
        fb_y = carve(region1, [2 * B * NJ * NS + 4 * 3 * B * NS], (B, NJ, 4))

        bank = [stack.enter_context(nc.psum_tensor(f"bank{k}", [P, 512], F32)) for k in range(8)]

        place, turns = {}, [0] * 8

        def plan(item, k):
            place[item] = (k, turns[k])
            turns[k] += 1

        for n in range(B * NJ):
            plan(("xp", n), n % 2)
            plan(("z", n), 2 + n % 2)
            if n % NJ == 1 and n > NJ:
                b = n // NJ - 1
                plan(("xd", b), 4)
                for q in range(NQ):
                    plan(("xt", NQ * b + q), 5 + (NQ * b + q) % 3)
        plan(("xd", B - 1), 4)
        for q in range(NQ):
            plan(("xt", NQ * (B - 1) + q), 5 + (NQ * (B - 1) + q) % 3)
        for n, k in (("cumA", 0), ("cumB", 1), ("cumC", 2), ("cumD", 3), ("abT", 4), ("vbT", 5), ("gcT", 6),
                     ("lbT", 7), ("rbT", 0), (("laT", 0), 1), (("laT", 1), 2), (("raT", 0), 3), (("raT", 1), 4)):
            plan(n, k)
        for q in range(NQ - 1):
            plan(("S", q), (7, 5, 6)[q])
        for b in range(B + 2):
            for m in ((0, 1) if b == 0 else (b + 1,)):
                if m < B:
                    plan(("M1", m), 4)
                    plan(("M2", m), 5)
            for j in range(NJ if b < B else 0):
                plan(("y", b, j), (NJ * b + j) % 3)
            for o in range(2 if 1 <= b <= B else 0):
                plan(("o", b - 1, o), 6 + o)
            for k in range(KD if b >= 2 else 0):
                plan(("x1t", b - 2, k), 4 + k)
        plan("g", 3)
        plan("cum", 2)
        plan("aT", 3)
        plan("mT", 5)
        plan("R", 6)

        def plan_front(i):
            if i % NQ == 0:
                plan(("H", i // NQ), 2)
            plan(("nm", i), 5)
            plan(("sA", i), (6, 0)[i % 2])
            plan(("sB", i), (7, 1)[i % 2])

        plan_front(0)
        for i in range(NT):
            if i + 1 < NT:
                plan_front(i + 1)
            if i % NQ == 2 and i > NQ:
                for q in range(NQ):
                    plan(("x2t", i - NQ - 2 + q), 3)
                plan(("lg", i // NQ - 1), 2)
            if i % NQ == 3 and i > NQ:
                plan(("rk", i // NQ - 1), 2)
            plan(("num", i), 4)
        for q in range(NQ):
            plan(("x2t", NT - NQ + q), 3)
        plan(("lg", B - 1), 2)
        plan(("rk", B - 1), 2)
        plan("cnt", 2)

        WPARTS = 6
        WPART = WCOLS // WPARTS
        SPLIT_HI, SPLIT_LO = 2, 8

        def hi_of(off):
            return wslot(off)[:, 0:WCOLS]

        def lo_of(off):
            return wslot(off)[:, WCOLS:2 * WCOLS]

        filled = [sem(f"bank{k}_filled") for k in range(8)]
        drained = [sem(f"bank{k}_drained") for k in range(8)]
        ld_first, ld_conv, ld_x, ld_small, ld_ctx = (sem(f"{n}_loaded") for n in ("first", "conv", "x", "small", "ctx"))
        consts_done = sem("consts_done")
        pool_step, dve_step, act_step = sem("pool_step"), sem("dve_step"), sem("act_step")
        conv_done, xc_done = sem("conv_done"), sem("xc_done")
        zs_done = sem("zs_done")
        vmin_done, exp_done, dtA_done = sem("vmin_done"), sem("exp_done"), sem("dtA_done")
        aneg_done = sem("aneg_done")
        cum_ready, cumexp_done = sem("cum_ready"), sem("cumexp_done")
        la_done, ra_done, ediff_done, factors_done, guard_in = (sem(n) for n in (
            "la_done", "ra_done", "ediff_done", "factors_done", "guard_in_done"))
        guard_done, guard_red, bad_done, scan_checked = (sem(n) for n in ("guard_done", "guard_reduced", "bad_done", "scan_checked"))
        hst_done, mt_done, y_copied, gated = sem("hst_done"), sem("mt_done"), sem("y_copied"), sem("gated")
        x1_done, gk_done = sem("x1_done"), sem("gk_done")
        gabs_done, gexp_done, lf_done, a_done, mrow_done, z_done, args_done, fac_done = (sem(n) for n in (
            "gabs_done", "gln_done", "lf_done", "a_done", "mrow_done", "zsel_done", "args_done", "fac_done"))
        vones_done, kw_done, kw_used = sem("vones_done"), sem("kw_done"), sem("kw_used")
        arg_done, masked, decay_done, prob_done, x2_done = (sem(n) for n in (
            "arg_done", "masked", "decay_done", "prob_done", "x2_done"))
        picks_done, rexp_in, rexp_done, row_done, scattered = (sem(n) for n in (
            "picks_done", "router_exp_in", "router_exp_done", "row_done", "scattered"))
        tables_done, padded = sem("tables_done"), sem("padded")
        fb_dma, fb_step, fb_gate, fb_out = (sem(f"fallback_{n}") for n in ("dma", "step", "gate", "out"))
        w_loaded, w_hi, w_ready, w_again, w_step = (sem(n) for n in ("w_loaded", "w_hi", "w_ready", "w_again", "w_step"))
        w_lo, pool_gate = sem("w_lo"), sem("pool_gate")
        xg_loaded = [sem(f"xg{s}_loaded") for s in range(2)]
        (xg_turned, xgh_done, xgT_done, meta_step, meta_done, up_done, sil_done, mid_done, turned, hTh_done, hTl_done, y_done,
         rid_done, yout_done) = (sem(n) for n in (
             "xg_turned", "xgh_done", "xgT_done", "meta_step", "meta_done", "up_done", "silu_done", "mid_done", "h_turned",
             "hTh_done", "hTl_done", "y_done", "rid_done", "yout_done"))
        y_sent = [sem(f"y{s}_sent") for s in range(2)]
        y_back = [sem(f"yback{b}_loaded") for b in range(B)]
        fin_done, out_done = sem("fin_done"), sem("out_done")

        def wait_filled(eng, item):
            k, n = place[item]
            eng.wait_ge(filled[k], n + 1)

        def wait_drained(eng, item):
            k, n = place[item]
            eng.wait_ge(drained[k], n + 1)

        def drain(item, ins):
            ins.then_inc(drained[place[item][0]], 1)

        def ps(item):
            return bank[place[item][0]]

        def bc(ap, axis, shape):
            return ap.unsqueeze(axis).to_broadcast(shape)

        block = stack.enter_context(nc.Block())

        @block.sync
        def _(sp):
            sp.dma_start(winT, w_inT.rearrange("(k p) m -> p k m", p=P)).then_inc(ld_first, 16)
            sp.dma_start(xcol, xT.rearrange("(k p) t -> p k t", p=P)).then_inc(ld_first, 16)
            sp.dma_start(convw, conv_w.rearrange("(j p) k -> p j k", p=P)).then_inc(ld_conv, 16)
            sp.dma_start(convb[:, :], conv_b).then_inc(ld_conv, 16)
            sp.dma_start(wxT, w_xT.rearrange("(j p) n -> p j n", p=P)).then_inc(ld_conv, 16)
            sp.dma_start(xtok[:, :, 0:D], x.rearrange("(i p) d -> p i d", p=P)).then_inc(ld_x, 16)
            sp.dma_start(woutT, w_outT.rearrange("(j p) d -> p j d", p=P)).then_inc(ld_x, 16)
            sp.dma_start(dpar[:, :], d_param).then_inc(ld_small, 16)
            sp.dma_start(alog[:, :], a_log.partition_broadcast(P)).then_inc(ld_small, 16)
            sp.dma_start(gk, gate_k.rearrange("(k p) g -> p k g", p=P)).then_inc(ld_small, 16)
            sp.dma_start(gb[:, :], gate_b.partition_broadcast(P)).then_inc(ld_small, 16)
            sp.dma_start(onw[:, :], outnorm.partition_broadcast(P)).then_inc(ld_small, 16)
            sp.dma_start(rw, router_w.rearrange("(k p) e -> p k e", p=P)).then_inc(ld_small, 16)
            sp.wait_ge(scan_checked, 1)
            for q in range(NQ - 1):
                wait_filled(sp, ("S", q))
            wait_drained(sp, "cumD")
            sp.dma_start(ctxc, ctxT.rearrange("(k p) t -> p k t", p=P)).then_inc(ld_ctx, 16)
            for h in range(H):
                sp.dma_start(vaug[:, :, h, 0:DH], ctx.rearrange("(i p) (h d) -> h p i d", p=P, h=H)[h]).then_inc(ld_ctx, 16)
            for b in range(B):
                for o in range(2):
                    wait_filled(sp, ("o", b, o))
            for e in range(2):
                if e:
                    sp.wait_ge(w_ready, 1)
                sp.dma_start(wstage, w_exp[e]).then_inc(w_loaded, 16)

            sp.wait_ge(tables_done, 1)
            npair = sp.value_load(tab_n[0:1, 0:1], min_val=SURE, max_val=NB // 2)
            events = sp.value_load(tab_n[0:1, 2:3], min_val=2, max_val=E)
            for n in range(2, E):
                with sp.If(events > n):
                    e = sp.value_load(tab_ev[0:1, n:n + 1], min_val=0, max_val=E - 1)
                    sp.wait_ge(w_ready, n)
                    sp.dma_start(wstage, w_exp[bass.ds(e, 1)].squeeze(0)).then_inc(w_loaded, 16)
            sent, loaded = 16 * npair, 16 * npair + 16
            for s in range(2):
                sp.wait_ge(xg_loaded[s], loaded)
                sp.wait_ge(y_sent[s], sent)
            for b in range(B):
                for k, dst in ((0, ya), (1, yb)):
                    sp.dma_start(dst[:, b * NQ:(b + 1) * NQ, :],
                                 yrows[k * T + b * S:k * T + (b + 1) * S, :].rearrange("(i p) d -> p i d", p=P)
                                 ).then_inc(y_back[b], 16)
            for b in range(B):
                sp.wait_ge(fin_done, b + 1)
                sp.dma_start(out[b * S:(b + 1) * S, :].rearrange("(i p) d -> p i d", p=P),
                             xtok[:, b * NQ:(b + 1) * NQ, 0:D]).then_inc(out_done, 16)
            sp.wait_ge(out_done, 16 * B)

        def scan_step_by_step(pool):
            n = [0]

            def link(ins):
                n[0] += 1
                ins.then_inc(fb_step, 1)
                pool.wait_ge(fb_step, n[0])
            dst = coef.rearrange("(q p) (w b n) -> w b p q n", p=P, w=3, b=B)
            for w, src in enumerate((abar[:, :, 0:NS], bbar, xdbl[:, :, NS:2 * NS])):
                for b in range(B):
                    pool.dma_start(dst[w, b], src.rearrange("p (q b) n -> p b q n", b=B)[:, b]).then_inc(fb_dma, 16)
            pool.wait_ge(fb_dma, 16 * 3 * B)
            for item in ("gcT", "lbT", "rbT", ("laT", 0), ("laT", 1), ("raT", 0), ("raT", 1)):
                wait_drained(pool, item)
            for q in range(NQ - 1):
                wait_filled(pool, ("S", q))
            for b in range(2):
                wait_filled(pool, ("M1", b))
                wait_filled(pool, ("M2", b))
            pool.wait_ge(hst_done, 1)
            link(pool.memset(fb_h, 0.0))
            per = 4
            base = n[0]
            ops = 9
            with pool.Fori(0, S // per) as it:
                pool.dma_start(fb_c, coef.rearrange("(c s) w -> c (s w)", s=per)[bass.ds(it, 1), :]
                               .squeeze(0).partition_broadcast(P)).then_inc(fb_dma, 16)
                pool.wait_ge(fb_dma, 16 * 3 * B + 16 * (it + 1))
                for s in range(per):
                    done = [it * (per * ops) + (base + s * ops)]

                    def step(ins):
                        done[0] = done[0] + 1
                        ins.then_inc(fb_step, 1)
                        pool.wait_ge(fb_step, done[0])
                    c = fb_c[:, s * 3 * B * NS:(s + 1) * 3 * B * NS].rearrange("p (w b n) -> p w b n", w=3, b=B)
                    full = [P, B, NJ, NS]
                    xs = xc.rearrange("p j (b t) -> p b j t", b=B)[:, :, :, bass.ds(it * per + s, 1)].to_broadcast(full)
                    step(pool.tensor_tensor(fb_h, fb_h, bc(c[:, 0], 2, full), ALU.mult))
                    step(pool.tensor_tensor(fb_t, xs, bc(c[:, 1], 2, full), ALU.mult))
                    step(pool.tensor_tensor(fb_h, fb_h, fb_t, ALU.add))
                    pool.sem_inc(fb_gate, 1)
                    step(pool.tensor_scalar(fb_h, fb_h, CLIP, -CLIP, ALU.min, ALU.max))
                    step(pool.tensor_tensor(fb_t, fb_h, bc(c[:, 2], 2, full), ALU.mult))
                    for w in (8, 4):
                        step(pool.tensor_tensor(fb_t[:, :, :, 0:w], fb_t[:, :, :, 0:w], fb_t[:, :, :, w:2 * w], ALU.add))
                    step(pool.tensor_tensor(fb_t[:, :, :, 0:2], fb_t[:, :, :, 0:2], fb_t[:, :, :, 2:4], ALU.add))
                    step(pool.tensor_tensor(fb_y[:, :, :, s:s + 1], fb_t[:, :, :, 0:1], fb_t[:, :, :, 1:2], ALU.add))
                pool.sem_inc(fb_gate, 1)
                pool.dma_start(yscan.rearrange("p b j t -> p (b j) t")[:, :, bass.ds(it * per, per)],
                               fb_y.rearrange("p b j t -> p (b j) t")).then_inc(fb_out, 16)
                pool.wait_ge(fb_out, 16 * (it + 1))
            pool.dma_start(yx[:, 0:B, :], yscan.rearrange("p b j t -> p b (j t)")).then_inc(fb_out, 16)
            pool.wait_ge(fb_out, 16 * (S // per + 1))

        @block.gpsimd
        def _(pool):
            count = [0]

            def link(ins):
                count[0] += 1
                ins.then_inc(pool_step, 1)
                pool.wait_ge(pool_step, count[0])

            def keep(ap, pattern, base, cm, op=ALU.is_ge, fill=0.0, out=None):
                link(pool.affine_select(out=out if out is not None else ap, in_=ap, pattern=pattern, compare_op=op,
                                        fill=fill, base=base, channel_multiplier=cm))
            link(pool.memset(xpad[:, :, 0:TAPS - 1], 0.0))
            link(pool.memset(ident[:, :], 0.0))
            keep(ident[:, :], [[-1, P]], 0, 1, ALU.not_equal, 1.0)
            link(pool.memset(ones[:, :], 1.0))
            keep(ones[:, :], [[1, P]], 0, -1, out=tri[:, :])
            keep(tri[:, :].rearrange("p (c t) -> p c t", t=CH), [[-CH, NC], [0, CH]], 0, 1,
                 out=tri32[:, :].rearrange("p (c t) -> p c t", t=CH))
            keep(ones[:, :].rearrange("p (c t) -> p c t", t=CH), [[CH, NC], [0, CH]], CH - 1, -1,
                 out=own[:, :].rearrange("p (c t) -> p c t", t=CH))
            for r in range(NC - 1):
                keep(ones[:, :], [[0, P]], CH * (r + 1) - 1, -1, out=upto[:, r * P:(r + 1) * P])
            keep(ones[:, 0:NC - 1], [[-CH, NC - 1]], 0, 1, out=mask_la[:, :])
            keep(mask_la[:, :], [[CH, NC - 1]], CH - 1, -1)
            keep(ones[:, 0:NC - 1], [[-CH, NC - 1]], -CH, 1, out=mask_ra[:, :])
            link(pool.memset(ones16[:, :], 1.0))
            keep(ones16[:, :], [[1, P]], 0, -1, ALU.is_gt, out=before16[:, :])
            link(pool.iota(eid[:, :], [[1, E]], base=0, channel_multiplier=0, allow_small_or_imprecise_dtypes=True))
            link(pool.iota(eoff[:, :], [[REGION, E]], base=0, channel_multiplier=0, allow_small_or_imprecise_dtypes=True))
            link(pool.iota(tokid[:, :], [[P, NT]], base=0, channel_multiplier=1, allow_small_or_imprecise_dtypes=True))
            link(pool.iota(steps128[:, :], [[P, NT]], base=0, channel_multiplier=0, allow_small_or_imprecise_dtypes=True))
            link(pool.iota(blkid[:, :], [[1, NB + 2]], base=0, channel_multiplier=0, allow_small_or_imprecise_dtypes=True))
            link(pool.memset(zero[:, :], 0.0))
            link(pool.memset(padrow[:, :], 0.0))
            link(pool.iota(padrow[:, D:D + 1], [[0, 1]], base=T, channel_multiplier=1, allow_small_or_imprecise_dtypes=True))
            link(pool.memset(padrow[:, D + 1:D + 2], -1.0))
            for t in (dtA, abar, vabs, la, ra, lb, rb, rc, wt):
                link(pool.memset(t, 0.0))
            pool.memset(picksum[:, 0, :], 0.0).then_inc(consts_done, 1)

            pool.wait_ge(guard_done, 1)
            pool.partition_all_reduce(guardall, guard, P, RMAX).then_inc(guard_red, 1)
            pool.wait_ge(bad_done, 1)
            with pool.If(pool.value_load(bad[0:1, 0:1], min_val=0, max_val=1) > 0):
                scan_step_by_step(pool)
            pool.sem_inc(scan_checked, 1)

            pool.wait_ge(scan_checked, 1)
            for q in range(NQ - 1):
                wait_filled(pool, ("S", q))
            wait_drained(pool, "cumD")
            pool.memset(vaug[:, :, :, DH:DV], 1.0).then_inc(vones_done, 1)
            pool.wait_ge(fac_done, 1)
            pool.wait_ge(ld_ctx, 16 * (1 + H))
            link(pool.memset(negsel, 0.0))
            for b in range(B):
                keep(negsel, [[-1, H], [0, P]], -NSP * b, 1, ALU.not_equal, -1.0)

            def weigh_keys(b):
                if b:
                    wait_filled(pool, ("H", b - 1))
                pairs = [(s, c) for c in range(1, NQ) for s in range(c)]
                for n, (s, c) in enumerate(pairs):
                    ins = pool.tensor_tensor(kw[:, n], vaug[:, NQ * b + s, :, 0:DH],
                                             bc(fac[:, NQ - 1 + n, b, :], 2, [P, H, DH]), ALU.mult)
                ins.then_inc(kw_done, 1)

            def mask_tile(i):
                pool.wait_ge(arg_done, i + 1)
                pool.affine_select(out=decay[:, i % 2], in_=decay[:, i % 2], pattern=[[0, H], [1, P]],
                                   compare_op=ALU.is_ge, fill=-1.0e30, base=0, channel_multiplier=-1).then_inc(masked, 1)

            def scatter(b):
                pool.wait_ge(row_done, b + 1)
                for i in range(NQ * b, NQ * (b + 1)):
                    for k in range(2):
                        pool.indirect_dma_start(
                            out=slots, out_offset=bass.IndirectOffsetOnAxis(ap=pos[:, k, i:i + 1], axis=0),
                            in_=xtok[:, i, :], in_offset=None).then_inc(scattered, 16)

            weigh_keys(0)
            mask_tile(0)
            for i in range(NT):
                if i + 1 < NT:
                    if (i + 1) % NQ == 0:
                        weigh_keys((i + 1) // NQ)
                    mask_tile(i + 1)
                if i % NQ == 3 and i > NQ:
                    scatter(i // NQ - 1)
                if SPLIT_LO <= i < SPLIT_LO + WPARTS:
                    part = slice((i - SPLIT_LO) * WPART, (i - SPLIT_LO + 1) * WPART)
                    if i == SPLIT_LO:
                        pool.wait_ge(w_hi, 1)
                    pool.tensor_tensor(lo_of(slot_at[0])[:, part], wstage[:, part], hi_of(slot_at[0]).bitcast(F32)[:, part],
                                       ALU.subtract).then_inc(w_lo, 1)
                    if i == SPLIT_LO + WPARTS - 1:
                        pool.wait_ge(w_lo, WPARTS)
                        pool.sem_inc(w_ready, 1)
            pool.wait_ge(w_hi, 2)
            pool.tensor_tensor(lo_of(slot_at[1]), wstage, hi_of(slot_at[1]).bitcast(F32), ALU.subtract).then_inc(w_lo, 1)
            scatter(B - 1)
            pool.wait_ge(tables_done, 1)
            pool.wait_ge(scattered, 16 * 2 * NT)
            for e in range(E):
                row = pool.value_load(tab_pad[0:1, e:e + 1], min_val=0, max_val=E * REGION)
                pool.dma_start(slots[bass.ds(row, P), :], padrow[:, :]).then_inc(padded, 16)
            pool.dma_start(slots[E * REGION:E * REGION + P, :], padrow[:, :]).then_inc(padded, 16)
            pool.wait_ge(padded, 16 * (E + 1))

            pool.wait_ge(w_lo, WPARTS + 1)
            e = pool.value_load(tab_ev[0:1, 1:2], min_val=1, max_val=E - 1)
            with pool.If(e > 1):
                pool.dma_start(wstage, w_exp[bass.ds(e, 1)].squeeze(0)).then_inc(w_again, 16)
                pool.wait_ge(w_again, 16)
                pool.tensor_tensor(hi_of(slot_at[1]), wstage, bc(zero[:, 0], 1, [P, WCOLS]), ALU.add).then_inc(w_step, 1)
                pool.wait_ge(w_step, 1)
                pool.tensor_tensor(lo_of(slot_at[1]), wstage, hi_of(slot_at[1]).bitcast(F32), ALU.subtract).then_inc(w_step, 1)
                pool.wait_ge(w_step, 2)
            pool.sem_inc(w_ready, 1)
            npair = pool.value_load(tab_n[0:1, 0:1], min_val=SURE, max_val=NB // 2)

            def event_of(g):
                return pool.value_load(tab_event[0:1, bass.ds(g, 1)], min_val=1, max_val=E - 1)

            def next_off(g):
                return pool.value_load(tab_noff[0:1, bass.ds(g, 1)], min_val=0, max_val=max(slot_at))

            def next_high(g):
                event, off = event_of(g), next_off(g)
                if not isinstance(g, int) or g:
                    pool.wait_ge(y_done, g)
                pool.wait_ge(w_loaded, 16 * event + 32)
                pool.sem_inc(pool_gate, 1)
                pool.tensor_tensor(hi_of(off), wstage, bc(zero[:, 0], 1, [P, WCOLS]), ALU.add).then_inc(w_hi, 1)

            def next_low(g):
                event, off = event_of(g), next_off(g)
                pool.wait_ge(w_hi, event + 2)
                pool.sem_inc(pool_gate, 1)
                pool.tensor_tensor(lo_of(off), wstage, hi_of(off).bitcast(F32), ALU.subtract).then_inc(w_ready, 1)

            def send_block(g, s):
                if isinstance(g, int):
                    if g:
                        pool.wait_ge(y_sent[0], 16 * g)
                else:
                    pool.wait_ge(y_sent[1 - s], 8 * (g + s))
                pool.wait_ge(yout_done, g + 1)
                pool.sem_inc(pool_gate, 1)
                pool.indirect_dma_start(out=yrows, out_offset=bass.IndirectOffsetOnAxis(ap=rid[:, s:s + 1], axis=0),
                                        in_=yout[:, s], in_offset=None).then_inc(y_sent[s], 16)

            def pair(p):
                for s in range(2):
                    g = 2 * p + s
                    first = pool.value_load(tab_first[0:1, bass.ds(g, 1)], min_val=0, max_val=1)
                    with pool.If(first > 0):
                        next_high(g)
                    send_block(g, s)
                    with pool.If(first > 0):
                        next_low(g)
            pair(0)
            with pool.Fori(0, SURE - 1) as it:
                pair(it + 1)
            with pool.Fori(0, NB // 2 - SURE) as it:
                with pool.If(npair - it > SURE):
                    pair(it + SURE)

        @block.scalar
        def _(act):
            def conv_in(n):
                wait_filled(act, ("xp", n))
                if n == 0:
                    act.wait_ge(pool_step, 1)
                if n >= 4:
                    act.wait_ge(conv_done, n - 3)
                drain(("xp", n), act.copy(xpad[:, n % 4, TAPS - 1:TAPS - 1 + S], ps(("xp", n))[:, :]))

            def gate_in(n):
                b, j = divmod(n, NJ)
                wait_filled(act, ("z", n))
                drain(("z", n), act.activation(zs[:, j, b * S:(b + 1) * S], ps(("z", n))[:, :], ACT.Silu))

            def conv_out(n):
                b, j = divmod(n, NJ)
                act.wait_ge(conv_done, n + 1)
                act.activation(xc[:, j, b * S:(b + 1) * S], cbuf[:, n % 2], ACT.Silu).then_inc(xc_done, 1)

            def by_tokens(b):
                for q in range(NQ):
                    i = NQ * b + q
                    wait_filled(act, ("xt", i))
                    drain(("xt", i), act.copy(xct(b, q), ps(("xt", i))[:, :]))
            for n in range(B * NJ):
                if n % NJ == 2 and n > NJ:
                    by_tokens(n // NJ - 1)
                conv_in(n)
                gate_in(n)
                if n:
                    conv_out(n - 1)
            conv_out(B * NJ - 1)
            by_tokens(B - 1)

            act.wait_ge(ld_small, 16 * 6)
            act.activation(aneg, alog[:, :], ACT.Exp).then_inc(exp_done, 1)
            act.wait_ge(vmin_done, 1)
            act.activation(expv, horner, ACT.Exp).then_inc(exp_done, 1)
            act.wait_ge(dtA_done, 1)
            act.activation(abar[:, :, 0:NS], dtA[:, :, 0:NS], ACT.Exp).then_inc(exp_done, 1)
            act.wait_ge(cum_ready, 1)

            def cum(item, h):
                return ps(item)[:, h * 256:(h + 1) * 256].rearrange("p (i n) -> p i n", n=NS)
            act.activation(lb[:, :, 0:NS], cum("cumA", 0), ACT.Exp, scale=-1.0).then_inc(cumexp_done, 1)
            act.activation(rb[:, :, 0:NS], cum("cumA", 0), ACT.Exp).then_inc(cumexp_done, 1)
            act.activation(rc[:, :, 0:NS], cum("cumA", 1), ACT.Exp).then_inc(cumexp_done, 1)
            act.wait_ge(ediff_done, 1)
            act.activation(wt[:, :, 0:NS], wt[:, :, 0:NS], ACT.Exp).then_inc(cumexp_done, 1)
            act.activation(la[:, :, 3 * NS:4 * NS], la[:, :, 3 * NS:4 * NS], ACT.Exp).then_inc(cumexp_done, 1)
            act.activation(ediff, ediff, ACT.Exp).then_inc(cumexp_done, 1)
            wait_filled(act, "cumD")
            drain("cumD", act.activation(dec, ps("cumD")[:, 256:256 + NQ], ACT.Exp))
            wait_filled(act, "abT")
            drain("abT", act.copy(hst[:, 0], ps("abT")[:, :]))
            for item, dst in (("gcT", gcT), ("lbT", lbT), ("rbT", rbT), (("laT", 0), laT[:, 0]), (("laT", 1), laT[:, 1]),
                              (("raT", 0), raT[:, 0]), (("raT", 1), raT[:, 1])):
                wait_filled(act, item)
                drain(item, act.copy(dst, ps(item)[:, :].rearrange("p (q t) -> p q t", t=P)))
            act.wait_ge(scan_checked, 1)
            clipped = act.value_load(bad[0:1, 0:1], min_val=0, max_val=1)

            def scan_out(b):
                with act.If(clipped < 1):
                    for j in range(NJ):
                        wait_filled(act, ("y", b, j))
                        drain(("y", b, j), act.copy(ybuf(b, j), ps(("y", b, j))[:, :]))
                with act.If(clipped > 0):
                    for j in range(NJ):
                        wait_filled(act, ("y", b, j))
                        act.sem_inc(drained[place[("y", b, j)][0]], 1)

            def norm1_turned(b):
                for k in range(KD):
                    wait_filled(act, ("x1t", b, k))
                    drain(("x1t", b, k), act.copy(xcol[:, k, b * S:(b + 1) * S], ps(("x1t", b, k))[:, :]))
            for b in range(B + 2):
                if b < B:
                    scan_out(b)
                if b >= 2:
                    norm1_turned(b - 2)

            act.wait_ge(gabs_done, 1)
            act.activation(lfb, lfa, ACT.Exp, scale=-1.0).then_inc(act_step, 1)
            act.wait_ge(act_step, 1)
            act.activation(lfa, lfb, ACT.Ln, bias=1.0).then_inc(gexp_done, 1)
            wait_filled(act, "aT")
            drain("aT", act.copy(aT, ps("aT")[:, :]))
            wait_filled(act, "mT")
            drain("mT", act.copy(mS, ps("mT")[:, :].rearrange("p (q b n) -> p q b n", q=NQ, b=B)))
            act.wait_ge(args_done, 1)
            act.activation(fac, fac, ACT.Exp).then_inc(fac_done, 1)
            act.activation(emx, emx, ACT.Exp).then_inc(fac_done, 1)

            def states(b):
                wait_filled(act, ("H", b))
                drain(("H", b), act.copy(hs[:, b % 2], ps(("H", b))[:, 0:(NQ - 1) * 2 * DV].rearrange(
                    "p (c h d) -> p c h d", c=NQ - 1, h=2)))

            def decays(i):
                act.wait_ge(masked, i + 1)
                act.activation(decay[:, i % 2], decay[:, i % 2], ACT.Exp).then_inc(decay_done, 1)

            def norm2_turned(i):
                b, q = divmod(i, NQ)
                wait_filled(act, ("x2t", i))
                if b:
                    wait_filled(act, ("lg", b - 1))
                drain(("x2t", i), act.copy(x2c[:, q], ps(("x2t", i))[:, 0:D].rearrange("p (k t) -> p k t", k=KD)))

            def router_exp(b):
                act.wait_ge(rexp_in, b + 1)
                act.activation(rb_, rb_, ACT.Exp).then_inc(act_step, 1)
                act.activation(rc_, rc_, ACT.Exp).then_inc(rexp_done, 1)
            states(0)
            decays(0)
            for i in range(NT):
                if i + 1 < NT:
                    if (i + 1) % NQ == 0:
                        states((i + 1) // NQ)
                    decays(i + 1)
                if i % NQ == 2 and i > NQ:
                    for q in range(NQ):
                        norm2_turned(i - NQ - 2 + q)
                    router_exp(i // NQ - 1)
                if SPLIT_HI <= i < SPLIT_HI + WPARTS:
                    if i == SPLIT_HI:
                        act.wait_ge(w_loaded, 16)
                    part = slice((i - SPLIT_HI) * WPART, (i - SPLIT_HI + 1) * WPART)
                    ins = act.copy(hi_of(slot_at[0])[:, part], wstage[:, part])
                    ins.then_inc(act_step if i < SPLIT_HI + WPARTS - 1 else w_hi, 1)
            wait_filled(act, ("num", NT - 1))
            act.wait_ge(w_loaded, 32)
            act.copy(hi_of(slot_at[1]), wstage).then_inc(w_hi, 1)
            for q in range(NQ):
                norm2_turned(NT - NQ + q)
            router_exp(B - 1)

            def slot_of(g):
                return act.value_load(tab_slot[0:1, bass.ds(g, 1)], min_val=0, max_val=E * REGION)

            def load_block(slot, s):
                act.dma_start(xg[:, s], slots[bass.ds(slot, P), :]).then_inc(xg_loaded[s], 16)

            def silu(g, u):
                act.wait_ge(up_done, 2 * g + (u + 1))
                act.activation(gsil[:, u], bank[2 * u][:, :], ACT.Silu).then_inc(sil_done, 1)

            def high_turned(g, u):
                act.wait_ge(turned, 2 * g + (u + 1))
                act.copy(hTh[:, u], bank[4 + u][:, :].rearrange("p (c t) -> p c t", t=P)).then_inc(hTh_done, 1)

            def pair(p):
                for s in range(2):
                    g = 2 * p + s
                    silu(g, 0)
                    if not isinstance(g, int) or g:
                        high_turned(g - 1, 1)
                    slot = slot_of(g + 2)
                    act.wait_ge(xg_turned, g + 1)
                    act.wait_ge(meta_done, g + 1)
                    load_block(slot, s)
                    silu(g, 1)
                    high_turned(g, 0)
            act.wait_ge(tables_done, 1)
            slot = [slot_of(s) for s in range(2)]
            npair = act.value_load(tab_n[0:1, 0:1], min_val=SURE, max_val=NB // 2)
            act.wait_ge(scattered, 16 * 2 * NT)
            act.wait_ge(padded, 16 * (E + 1))
            for s in range(2):
                load_block(slot[s], s)
            pair(0)
            with act.Fori(0, SURE - 1) as it:
                pair(it + 1)
            with act.Fori(0, NB // 2 - SURE) as it:
                with act.If(npair - it > SURE):
                    pair(it + SURE)
            high_turned(act.value_load(tab_n[0:1, 1:2], min_val=2 * SURE - 2, max_val=NB - 2) + 1, 1)

        @block.vector
        def _(dve):
            count = [0]

            def link(ins):
                count[0] += 1
                ins.then_inc(dve_step, 1)
                dve.wait_ge(dve_step, count[0])

            def note(ins, s, value):
                ins.then_inc(s, 1)
                dve.wait_ge(s, value)

            def convolve(n):
                j = n % NJ
                src = xpad[:, n % 4]
                dst = cbuf[:, n % 2]
                wait_drained(dve, ("xp", n))
                if n >= 2:
                    dve.wait_ge(xc_done, n - 1)
                link(dve.tensor_scalar(dst, src[:, 0:S], convw[:, j, 0:1], convb[:, j:j + 1], ALU.mult, ALU.add))
                for k in range(1, TAPS - 1):
                    link(dve.scalar_tensor_tensor(dst, src[:, k:k + S], convw[:, j, k:k + 1], dst, ALU.mult, ALU.add))
                note(dve.scalar_tensor_tensor(dst, src[:, TAPS - 1:TAPS - 1 + S], convw[:, j, TAPS - 1:TAPS], dst,
                                              ALU.mult, ALU.add), conv_done, n + 1)

            def scan_inputs(b):
                wait_filled(dve, ("xd", b))
                drain(("xd", b), dve.tensor_copy(xdbl.rearrange("p (q b) n -> p b q n", b=B)[:, b],
                                                 ps(("xd", b))[:, 0:NQ * NX].rearrange("p (q n) -> p q n", n=NX)))

            def largest_input(b):
                for q in range(NQ):
                    wait_drained(dve, ("xt", NQ * b + q))
                    ins = dve.tensor_reduce(xmax[:, B * q + b:B * q + b + 1], xct(b, q), AX_X, ALU.max,
                                            apply_absolute_value=True)
                return ins
            dve.wait_ge(ld_conv, 16 * 3)
            for n in range(B * NJ):
                convolve(n)
                if n % NJ == 2 and n > NJ:
                    scan_inputs(n // NJ - 1)
                    link(largest_input(n // NJ - 1))
            dve.wait_ge(consts_done, 1)
            scan_inputs(B - 1)
            for b in range(B):
                wait_drained(dve, ("xd", b))
            note(dve.tensor_scalar(horner, xdbl[:, :, 2 * NS], -2.0, None, ALU.min), vmin_done, 1)
            link(largest_input(B - 1))
            dve.wait_ge(exp_done, 2)
            link(dve.tensor_scalar(aneg, aneg, -1.0, None, ALU.mult))
            link(dve.tensor_scalar(horner, expv, (-1.0) ** (HORNER + 1) / HORNER, None, ALU.mult))
            for k in range(HORNER - 1, 0, -1):
                link(dve.scalar_tensor_tensor(horner, horner, (-1.0) ** (k + 1) / k, expv, ALU.add, ALU.mult))
            link(dve.tensor_scalar(dtv, horner, DT_MIN, DT_MAX, ALU.max, ALU.min))
            full = [P, NT, NS]
            link(dve.tensor_tensor(dtA[:, :, 0:NS], bc(dtv, 2, full), bc(aneg, 1, full), ALU.mult))
            note(dve.tensor_scalar(dtA[:, :, 0:NS], dtA[:, :, 0:NS], -20.0, 0.0, ALU.max, ALU.min), dtA_done, 1)
            link(dve.tensor_tensor(bbar, xdbl[:, :, 0:NS], bc(dtv, 2, full), ALU.mult))
            link(dve.tensor_scalar(bbar, bbar, -10.0, 10.0, ALU.max, ALU.min))
            link(dve.scalar_tensor_tensor(vabs[:, :, 0:NS], bbar, -1.0, bbar, ALU.mult, ALU.max))
            note(dve.tensor_tensor(vabs[:, :, 0:NS], vabs[:, :, 0:NS], bc(xmax, 2, full), ALU.mult), guard_in, 1)

            def cum(item, h):
                return ps(item)[:, h * 256:(h + 1) * 256].rearrange("p (i n) -> p i n", n=NS)
            cmat = xdbl[:, :, NS:2 * NS]
            wait_filled(dve, "cumA")
            link(dve.tensor_copy(cumt, cum("cumA", 1)))
            note(dve.tensor_reduce(guard[:, 1:2], ps("cumA")[:, 0:256], AX_X, ALU.min, negate=True), cum_ready, 1)
            wait_filled(dve, "cumB")
            for r in range(2):
                link(dve.tensor_tensor(ediff[:, r], cumt, cum("cumB", r), ALU.subtract))
            wait_filled(dve, "cumC")
            link(dve.tensor_tensor(ediff[:, 2], cumt, cum("cumC", 0), ALU.subtract))
            link(dve.tensor_scalar(ediff, ediff, 0.0, None, ALU.min))
            drain("cumC", dve.tensor_tensor(wt[:, :, 0:NS], cum("cumC", 1), cumt, ALU.subtract))
            wait_drained(dve, "cumC")
            wait_filled(dve, "cumD")
            note(dve.tensor_tensor(la[:, :, 3 * NS:4 * NS], cum("cumD", 0), cumt, ALU.subtract), ediff_done, 1)
            dve.wait_ge(cumexp_done, 6)
            dve.sem_inc(drained[place["cumA"][0]], 1)
            dve.sem_inc(drained[place["cumB"][0]], 1)
            link(dve.tensor_tensor(lb[:, :, 0:NS], lb[:, :, 0:NS], bbar, ALU.mult))
            link(dve.tensor_tensor(rb[:, :, 0:NS], rb[:, :, 0:NS], cmat, ALU.mult))
            link(dve.tensor_tensor(rc[:, :, 0:NS], rc[:, :, 0:NS], cmat, ALU.mult))
            link(dve.tensor_tensor(wt[:, :, 0:NS], wt[:, :, 0:NS], bbar, ALU.mult))
            for r in range(NC - 1):
                link(dve.scalar_tensor_tensor(la[:, :, r * NS:(r + 1) * NS], la[:, :, 3 * NS:4 * NS], mask_la[:, r:r + 1],
                                              bbar, ALU.mult, ALU.mult))
                link(dve.scalar_tensor_tensor(ra[:, :, r * NS:(r + 1) * NS], ediff[:, r], mask_ra[:, r:r + 1],
                                              cmat, ALU.mult, ALU.mult))
            note(dve.memset(la[:, :, 3 * NS:4 * NS], 0.0), factors_done, 1)
            wait_drained(dve, "abT")
            wait_filled(dve, "vbT")
            drain("vbT", dve.tensor_tensor_scan(hst[:, 1], hst[:, 0], ps("vbT")[:, :], 0.0, ALU.mult, ALU.add))
            wait_drained(dve, "vbT")
            note(dve.tensor_reduce(guard[:, 0:1], hst[:, 1], AX_X, ALU.max), guard_done, 1)
            dve.wait_ge(guard_red, 1)
            link(dve.tensor_scalar(guardall[:, 0:1], guardall[:, 0:1], STATE_LIMIT, None, ALU.is_lt))
            link(dve.scalar_tensor_tensor(guardall[:, 0:1], guardall[:, 1:2], DECAY_LIMIT, guardall[:, 0:1],
                                          ALU.is_lt, ALU.mult))
            note(dve.tensor_scalar(bad[:, :], guardall[:, 0:1], -1.0, 1.0, ALU.mult, ALU.add), bad_done, 1)
            wait_drained(dve, "cumD")
            for q in range(NQ - 1):
                wait_filled(dve, ("S", q))
                if q == 0:
                    ins = dve.tensor_copy(hst[:, 0], ps(("S", 0))[:, :])
                else:
                    ins = dve.scalar_tensor_tensor(hst[:, q], hst[:, q - 1], dec[:, q:q + 1], ps(("S", q))[:, :],
                                                   ALU.mult, ALU.add)
                drain(("S", q), ins)
                wait_drained(dve, ("S", q))
            dve.sem_inc(hst_done, 1)

            def mix(b):
                m1 = ps(("M1", b))[:, :].rearrange("p (q t) -> p q t", t=P)
                mt = mts[:, b % 2]
                wait_filled(dve, ("M1", b))
                if b >= 2:
                    wait_filled(dve, ("y", b - 2, NJ - 1))
                drain(("M1", b), dve.tensor_tensor(mt, m1, bc(tri32[:, :], 1, [P, NQ, P]), ALU.mult))
                wait_drained(dve, ("M1", b))
                wait_filled(dve, ("M2", b))
                drain(("M2", b), dve.tensor_tensor(mt, mt, ps(("M2", b))[:, :].rearrange("p (q t) -> p q t", t=P), ALU.add))

            def gate(b):
                for j in range(NJ):
                    part = slice(b * S, (b + 1) * S)
                    wait_drained(dve, ("y", b, j))
                    link(dve.tensor_tensor(zs[:, j, part], zs[:, j, part], ybuf(b, j), ALU.mult))
                    note(dve.scalar_tensor_tensor(zs[:, j, part], xc[:, j, part], dpar[:, j:j + 1], zs[:, j, part],
                                                  ALU.mult, ALU.add), gated, NJ * b + j + 1)

            def rsqrt(var, eps, n):
                v, y, t = rsv[:, 0:n], rsy[:, 0:n], rst[:, 0:n]
                link(dve.tensor_scalar(v, var, eps, None, ALU.add))
                link(dve.tensor_scalar(y.bitcast(I32), v.bitcast(I32), 1, None, ALU.logical_shift_right))
                link(dve.tensor_scalar(y.bitcast(I32), y.bitcast(I32), -1.0, float(0x5F3759DF), ALU.mult, ALU.add))
                link(dve.tensor_scalar(v, v, -0.5, None, ALU.mult))
                for _ in range(NEWTON):
                    link(dve.tensor_tensor(t, y, y, ALU.mult))
                    link(dve.tensor_tensor(t, t, v, ALU.mult))
                    link(dve.scalar_tensor_tensor(y, t, 1.5, y, ALU.add, ALU.mult))

            def layernorm(tiles, eps):
                n = len(tiles)
                for k, i in enumerate(tiles):
                    ins = dve.bn_stats(stats[:, k, :], xtok[:, i, 0:D])
                link(ins)
                for k, i in enumerate(tiles):
                    ins = dve.bn_aggr(mv[:, k, :], stats[:, k, :])
                link(ins)
                rsqrt(mv[:, 0:n, 1], eps, n)
                for k, i in enumerate(tiles):
                    ins = dve.tensor_scalar(xtok[:, i, 0:D], xtok[:, i, 0:D], mv[:, k, 0:1], rsy[:, k:k + 1],
                                            ALU.subtract, ALU.mult)
                return ins

            def norm1(b):
                for o in range(2):
                    wait_filled(dve, ("o", b, o))
                    two = xtok[:, NQ * b + 2 * o:NQ * b + 2 * o + 2, 0:D]
                    drain(("o", b, o), dve.tensor_tensor(two, two, ps(("o", b, o))[:, :].rearrange("p (i d) -> p i d", d=D),
                                                         ALU.add))
                for o in range(2):
                    wait_drained(dve, ("o", b, o))
                note(layernorm(range(NQ * b, NQ * (b + 1)), 1e-5), x1_done, b + 1)
            dve.wait_ge(ld_x, 32)
            dve.wait_ge(ld_small, 16 * 6)
            dve.tensor_tensor(gk[:, KD:2 * KD], gk[:, KD:2 * KD], gk[:, 2 * KD:3 * KD], ALU.add).then_inc(gk_done, 1)
            mix(0)
            for b in range(B + 1):
                if b + 1 < B:
                    mix(b + 1)
                if b < B:
                    gate(b)
                if b:
                    norm1(b - 1)

            all8 = [P, NT, 2 * H]
            wait_filled(dve, "g")
            drain("g", dve.tensor_tensor(gt, ps("g")[:, 0:NT * 2 * H].rearrange("p (i g) -> p i g", g=2 * H),
                                         bc(gb[:, :], 1, all8), ALU.add))
            wait_drained(dve, "g")
            note(dve.scalar_tensor_tensor(lfa, gt[:, :, H:2 * H], -1.0, gt[:, :, H:2 * H], ALU.mult, ALU.max), gabs_done, 1)
            dve.wait_ge(gexp_done, 1)
            link(dve.scalar_tensor_tensor(lfb, gt[:, :, H:2 * H], 0.0, lfa, ALU.min, ALU.subtract))
            link(dve.memset(apad, 0.0))
            lf4 = lfb.rearrange("p (b q) h -> p b q h", b=B)
            link(dve.memset(lfpre[:, :, 0, :], 0.0))
            for q in range(1, NQ):
                link(dve.tensor_tensor(lfpre[:, :, q, :], lfpre[:, :, q - 1, :], lf4[:, :, q - 1, :], ALU.add))
            dve.sem_inc(lf_done, 1)
            wait_filled(dve, "cum")
            csum = ps("cum")[:, 0:NT * H].rearrange("p (i h) -> p i h", h=H)
            link(dve.tensor_tensor(av, gt[:, :, 0:H], csum, ALU.subtract))
            drain("cum", dve.tensor_copy(cumS, csum))
            note(dve.tensor_copy(apad[:, :, 0:H], av), a_done, 1)
            wait_drained(dve, "aT")
            note(dve.tensor_tensor_scan(mrow, aT, aT, -BIG, ALU.max, ALU.max), mrow_done, 1)
            note(dve.tensor_tensor(zsel, bc(ident[:, :], 1, [P, NQ, P]), bc(mrow[:, P - 1:S:P], 2, [P, NQ, P]), ALU.mult),
                 z_done, 1)
            wait_drained(dve, "mT")
            wait_filled(dve, "R")
            rend = ps("R")[:, :].rearrange("p (q b n) -> p q b n", q=NQ, b=B)
            av4 = av.rearrange("p (b q) h -> p b q h", b=B)
            n = NQ - 1
            for c in range(1, NQ):
                link(dve.tensor_tensor(fac[:, c - 1], rend[:, c - 1, :, 0:H], mS[:, c, :, 0:H], ALU.subtract))
                for s in range(c):
                    ins = dve.tensor_tensor(fac[:, n], av4[:, :, s, :], rend[:, c - 1, :, 0:H], ALU.subtract)
                    n += 1
            drain("R", ins)
            wait_drained(dve, "R")
            wait_drained(dve, "cum")
            for q in range(NQ):
                cq = cumS.rearrange("p (b q) h -> p b q h", b=B)[:, :, q, :]
                ins = dve.scalar_tensor_tensor(emx.rearrange("p (b q) h -> p b q h", b=B)[:, :, q, :], cq, -1.0,
                                               mS[:, q, :, 0:H], ALU.mult, ALU.subtract)
            note(ins, args_done, 1)
            dve.wait_ge(fac_done, 2)
            link(dve.tensor_scalar(fac[:, 0:NQ - 1], fac[:, 0:NQ - 1], DH ** -0.5, None, ALU.mult))

            def exponents(i):
                wait_filled(dve, ("nm", i))
                if i >= 2:
                    dve.wait_ge(prob_done, 2 * (i - 1))
                k, _ = place[("nm", i)]
                ins = dve.tensor_tensor(decay[:, i % 2], ps(("nm", i))[:, :].rearrange("p (h s) -> p h s", h=H),
                                        bc(av[:, i, :], 2, [P, H, P]), ALU.add)
                note(ins, arg_done, i + 1)
                dve.sem_inc(drained[k], 1)

            def weights(i):
                b, c = divmod(i, NQ)
                dve.wait_ge(decay_done, i + 1)
                if i >= 2:
                    wait_filled(dve, ("num", i - 2))
                for par, item in ((0, ("sA", i)), (1, ("sB", i))):
                    wait_filled(dve, item)
                    sc = ps(item)[:, 0:2 * P].rearrange("p (h s) -> p h s", h=2)
                    ins = dve.scalar_tensor_tensor(prob[:, i % 2, par::2, :], sc, DH ** -0.5, decay[:, i % 2, par::2, :],
                                                   ALU.mult, ALU.mult)
                    ins.then_inc(prob_done, 1)
                    if c:
                        st = ps(item)[:, 2 * P:2 * P + 2 * DV].rearrange("p (h d) -> p h d", h=2)
                        ins = dve.tensor_tensor(tot[:, b % 2, c, par::2, :], st,
                                                bc(fac[:, c - 1, b, par::2], 2, [P, 2, DV]), ALU.mult)
                        drain(item, ins)
                    else:
                        dve.wait_ge(prob_done, 2 * i + par + 1)
                        dve.sem_inc(drained[place[item][0]], 1)

            def sums_of(i):
                b, c = divmod(i, NQ)
                tt = tot[:, b % 2, c]
                wait_filled(dve, ("num", i))
                num = ps(("num", i))[:, 0:H * DV].rearrange("p (h d) -> p h d", h=H)
                if c:
                    wait_drained(dve, ("sA", i))
                    wait_drained(dve, ("sB", i))
                    drain(("num", i), dve.tensor_tensor(tt, tt, num, ALU.add))
                else:
                    drain(("num", i), dve.tensor_copy(tt, num))

            def finish(b):
                tt = tot[:, b % 2]
                tiles = slice(NQ * b, NQ * (b + 1))
                for q in range(NQ):
                    wait_drained(dve, ("num", NQ * b + q))
                link(dve.scalar_tensor_tensor(den, tt[:, :, :, DH], -1.0, tt[:, :, :, DH], ALU.mult, ALU.max))
                link(dve.tensor_tensor(den, den, emx[:, tiles, :], ALU.max))
                link(dve.tensor_scalar(den, den, 1e-6, None, ALU.add))
                link(dve.reciprocal(den, den))
                link(dve.tensor_tensor(hbuf, tt[:, :, :, 0:DH], bc(den, 3, [P, NQ, H, DH]), ALU.mult))
                heads = hbuf.rearrange("p q h d -> p (q h) d")
                for n in range(NQ * H):
                    ins = dve.bn_stats(stats[:, n, :], heads[:, n, :])
                link(ins)
                for n in range(NQ * H):
                    ins = dve.bn_aggr(mv[:, n, :], stats[:, n, :])
                link(ins)
                rsqrt(mv[:, :, 1], 1e-6, NQ * H)
                full = [P, NQ * H, DH]
                link(dve.tensor_tensor(heads, heads, bc(mv[:, :, 0], 2, full), ALU.subtract))
                link(dve.tensor_tensor(heads, heads, bc(rsy, 2, full), ALU.mult))
                rows = hbuf.rearrange("p q h d -> p q (h d)")
                link(dve.tensor_tensor(rows, rows, bc(onw[:, :], 1, [P, NQ, D]), ALU.mult))
                link(dve.tensor_tensor(xtok[:, tiles, 0:D], xtok[:, tiles, 0:D], rows, ALU.add))
                note(layernorm(range(NQ * b, NQ * (b + 1)), 1e-5), x2_done, b + 1)

            def pick(dst, values, top, cand):
                full = [P, NQ, E]
                link(dve.tensor_reduce(top, values, AX_X, ALU.max))
                link(dve.tensor_tensor(cand, values, bc(top, 2, full), ALU.not_equal))
                link(dve.scalar_tensor_tensor(cand, cand, float(E), bc(eid[:, :], 1, full), ALU.mult, ALU.add))
                link(dve.tensor_reduce(sums[:, 0], cand, AX_X, ALU.min))
                link(dve.tensor_tensor(dst, bc(sums[:, 0], 2, full), bc(eid[:, :], 1, full), ALU.is_equal))

            def route_batch(b):
                full = [P, NQ, E]
                tiles = slice(NQ * b, NQ * (b + 1))
                wait_filled(dve, ("lg", b))
                drain(("lg", b), dve.tensor_copy(lg, ps(("lg", b))[:, 0:NQ * E].rearrange("p (q e) -> p q e", e=E)))
                wait_drained(dve, ("lg", b))
                if b:
                    dve.wait_ge(act_step, 1 + b)
                pick(oh1, lg, top1, ra_)
                link(dve.tensor_copy(xtok[:, tiles, D + 1], sums[:, 0]))
                link(dve.scalar_tensor_tensor(lg2, oh1, -BIG, lg, ALU.mult, ALU.add))
                pick(oh2, lg2, top2, ra_)
                note(dve.tensor_tensor(picks[:, tiles, :], oh1, oh2, ALU.add), picks_done, 2 * b + 1)
                for i in range(NQ * b, NQ * (b + 1)):
                    ins = dve.tensor_tensor(picksum[:, i + 1, :], picksum[:, i, :], picks[:, i, :], ALU.add)
                    if i + 1 < NQ * (b + 1):
                        link(ins)
                note(ins, picks_done, 2 * b + 2)
                for top, dst, base in ((top1, rb_, lg), (top2, rc_, lg2)):
                    tb = bc(top, 2, full)
                    link(dve.scalar_tensor_tensor(ra_, lg, -1.0, lg, ALU.mult, ALU.max))
                    link(dve.tensor_tensor(ra_, ra_, tb, ALU.max))
                    link(dve.tensor_tensor(dst, tb, lg, ALU.subtract))
                    link(dve.scalar_tensor_tensor(ra_, ra_, JITTER2, dst, ALU.mult, ALU.is_lt))
                    link(dve.tensor_tensor(dst, base, tb, ALU.subtract))
                    link(dve.scalar_tensor_tensor(dst, ra_, -1.0e30, dst, ALU.mult, ALU.add))
                dve.sem_inc(rexp_in, 1)
                wait_filled(dve, ("rk", b))
                rank = ps(("rk", b))[:, 0:NQ * E].rearrange("p (q e) -> p q e", e=E)
                drain(("rk", b), dve.tensor_tensor(lg, rank, bc(eoff[:, :], 1, full), ALU.add))
                wait_drained(dve, ("rk", b))
                for k, oh in ((0, oh1), (1, oh2)):
                    link(dve.tensor_tensor(ra_, oh, lg, ALU.mult))
                    link(dve.tensor_reduce(posf[:, k], ra_, AX_X, ALU.add))
                    link(dve.tensor_copy(pos[:, k, tiles], posf[:, k]))
                dve.wait_ge(rexp_done, b + 1)
                dve.wait_ge(act_step, 2 + b)
                for k, src in ((0, rb_), (1, rc_)):
                    link(dve.tensor_reduce(sums[:, k], src, AX_X, ALU.add))
                    link(dve.reciprocal(sums[:, k], sums[:, k]))
                    link(dve.tensor_copy(xtok[:, tiles, D + 2 + k], sums[:, k]))
                note(dve.tensor_copy(xtok[:, tiles, D], tokid[:, tiles]), row_done, b + 1)

            dve.wait_ge(consts_done, 1)
            exponents(0)
            for i in range(NT):
                weights(i)
                if i + 1 < NT:
                    exponents(i + 1)
                sums_of(i)
                if i % NQ == 1 and i > NQ:
                    finish(i // NQ - 1)
                if i % NQ == 2 and i > NQ:
                    route_batch(i // NQ - 1)
            finish(B - 1)
            route_batch(B - 1)

            wait_filled(dve, "cnt")
            drain("cnt", dve.tensor_copy(cnt[:, :], ps("cnt")[:, 0:E]))
            wait_drained(dve, "cnt")
            link(dve.tensor_tensor(cmp16, bc(cnt[:, :], 2, [P, E, NT]), bc(steps128[:, :], 1, [P, E, NT]), ALU.is_gt))
            link(dve.tensor_reduce(nblk[:, :], cmp16, AX_X, ALU.add))
            link(dve.memset(ringf[:, 0:E], 0.0))
            link(dve.tensor_tensor_scan(endblk[:, :], nblk[:, :], ringf[:, 0:E], 0.0, ALU.add, ALU.add))
            link(dve.tensor_tensor(cnt[:, :], cnt[:, :], eoff[:, :], ALU.add))
            link(dve.tensor_copy(tab_pad[:, :], cnt[:, :]))
            full = [P, NB + 2, E]
            link(dve.tensor_tensor(cmpb, bc(blkid[:, :], 2, full), bc(endblk[:, :], 1, full), ALU.is_ge))
            link(dve.tensor_reduce(eblk[:, :], cmpb, AX_X, ALU.add))
            link(dve.tensor_scalar(hasblk[:, :], nblk[:, :], 0.0, None, ALU.is_gt))
            link(dve.memset(hasblk[:, 0:1], 1.0))
            link(dve.tensor_tensor_scan(cumev[:, :], hasblk[:, :], ringf[:, 0:E], 0.0, ALU.add, ALU.add))
            full2 = [P, NB, E]
            cmp2 = cmpb[:, 0:NB, :]
            link(dve.tensor_tensor(cmpb, cmpb, bc(nblk[:, :], 1, full), ALU.mult))
            link(dve.tensor_reduce(sblk[:, :], cmpb, AX_X, ALU.add))
            link(dve.tensor_tensor(cmp2, bc(blkid[:, 0:NB], 2, full2), bc(endblk[:, :], 1, full2), ALU.is_ge))
            link(dve.tensor_tensor(cmp2, cmp2, bc(hasblk[:, :], 1, full2), ALU.mult))
            link(dve.tensor_reduce(evblk[:, :], cmp2, AX_X, ALU.add))
            link(dve.tensor_scalar(ringg[:, 0:1], cumev[:, E - 1:E], -1.0, None, ALU.add))
            link(dve.tensor_scalar(evblk[:, :], evblk[:, :], ringg[:, 0:1], None, ALU.min))
            link(dve.tensor_tensor(sblk[:, :], blkid[:, :], sblk[:, :], ALU.subtract))
            link(dve.tensor_scalar(ringf[:, :], eblk[:, :], float(REGION), None, ALU.mult))
            link(dve.scalar_tensor_tensor(sblk[:, :], sblk[:, :], float(P), ringf[:, :], ALU.mult, ALU.add))
            link(dve.tensor_scalar(sblk[:, :], sblk[:, :], float(E * REGION), None, ALU.min))
            link(dve.tensor_copy(tab_slot[:, :], sblk[:, :]))
            link(dve.tensor_copy(ringf[:, 0:1], evblk[:, 0:1]))
            link(dve.tensor_tensor(ringf[:, 1:NB], evblk[:, 1:NB], evblk[:, 0:NB - 1], ALU.subtract))
            link(dve.scalar_tensor_tensor(ringf[:, 0:NB], evblk[:, :], ringg[:, 0:1], ringf[:, 0:NB], ALU.is_lt, ALU.mult))
            link(dve.tensor_copy(tab_first[:, :], ringf[:, 0:NB]))
            link(dve.tensor_copy(tab_event[:, :], evblk[:, :]))
            link(dve.tensor_scalar(ringf[:, 0:NB], evblk[:, :], 1.0, None, ALU.is_ge))
            for v in range(2, E):
                link(dve.scalar_tensor_tensor(ringf[:, 0:NB], evblk[:, :], float(v), ringf[:, 0:NB], ALU.is_ge,
                                              ALU.subtract))
            link(dve.tensor_tensor(ringf[:, 0:NB], ringf[:, 0:NB], ringf[:, 0:NB], ALU.mult))
            link(dve.tensor_scalar(ringg[:, :], ringf[:, 0:NB], float(slot_at[0] - slot_at[1]), float(slot_at[1]),
                                   ALU.mult, ALU.add))
            link(dve.tensor_copy(tab_noff[:, :], ringg[:, :]))
            full = [P, E + 2, E]
            cmp2 = cmpb[:, 0:E + 2, :]
            link(dve.tensor_tensor(cmp2, bc(blkid[:, 0:E + 2], 2, full), bc(cumev[:, :], 1, full), ALU.is_ge))
            link(dve.tensor_reduce(ringf[:, 0:E + 2], cmp2, AX_X, ALU.add))
            link(dve.tensor_scalar(ringf[:, 0:E + 2], ringf[:, 0:E + 2], float(E - 1), None, ALU.min))
            link(dve.tensor_copy(tab_ev[:, :], ringf[:, 0:E + 2]))
            link(dve.tensor_scalar(ringf[:, 0:NB // 2], blkid[:, 0:NB:2], endblk[:, E - 1:E], None, ALU.is_lt))
            link(dve.tensor_reduce(ringg[:, 0:1], ringf[:, 0:NB // 2], AX_X, ALU.add))
            link(dve.tensor_scalar(ringg[:, 1:2], ringg[:, 0:1], 2.0, -2.0, ALU.mult, ALU.add))
            link(dve.tensor_copy(ringg[:, 2:3], cumev[:, E - 1:E]))
            note(dve.tensor_copy(tab_n[:, :], ringg[:, 0:3]), tables_done, 1)

            def row_meta(g, s):
                m = meta[:, s]
                first, a, b_ = m[:, 0:1], m[:, 1:2], m[:, 2:3]
                done = [g * 5]

                def chain(ins):
                    done[0] = done[0] + 1
                    ins.then_inc(meta_step, 1)
                    dve.wait_ge(meta_step, done[0])
                dve.wait_ge(xg_loaded[s], 16 * (g // 2 + 1) if isinstance(g, int) else 8 * (g - s) + 16)
                chain(dve.tensor_tensor(first, xg[:, s, D + 1:D + 2], eblk[:, bass.ds(g, 1)], ALU.is_equal))
                chain(dve.tensor_tensor(a, xg[:, s, D + 2:D + 3], first, ALU.mult))
                chain(dve.tensor_scalar(b_, first, -1.0, 1.0, ALU.mult, ALU.add))
                chain(dve.scalar_tensor_tensor(m[:, 3:4], b_, float(T), xg[:, s, D:D + 1], ALU.mult, ALU.add))
                chain(dve.tensor_tensor(b_, b_, xg[:, s, D + 3:D + 4], ALU.mult))
                dve.tensor_tensor(m[:, 4:5], a, b_, ALU.add).then_inc(meta_done, 1)

            def rows(g, s):
                src = bank[7][:, 0:D].rearrange("p (k t) -> p k t", k=KD)
                dve.wait_ge(xg_turned, g + 1)
                dve.tensor_copy(xTh[:, s], src).then_inc(xgh_done, 1)
                dve.wait_ge(xgh_done, g + 1)
                dve.tensor_tensor(xTl[:, s], src, xTh[:, s].bitcast(F32), ALU.subtract).then_inc(xgT_done, 1)

            def middle(g, u):
                dve.wait_ge(sil_done, 2 * g + (u + 1))
                dve.tensor_tensor(hmid[:, u], gsil[:, u], bank[2 * u + 1][:, :], ALU.mult).then_inc(mid_done, 1)

            def low_turned(g, u):
                dve.wait_ge(hTh_done, 2 * g + (u + 1))
                dve.tensor_tensor(hTl[:, u], bank[4 + u][:, :].rearrange("p (c t) -> p c t", t=P), hTh[:, u].bitcast(F32),
                                  ALU.subtract).then_inc(hTl_done, 1)

            def weigh(g, s):
                dve.wait_ge(meta_done, g + 1)
                if not isinstance(g, int) or g >= 2:
                    dve.wait_ge(y_sent[s], 8 * (g - s))
                dve.tensor_copy(rid[:, s:s + 1], meta[:, s, 3:4]).then_inc(rid_done, 1)
                dve.wait_ge(rid_done, g + 1)
                dve.wait_ge(y_done, g + 1)
                dve.tensor_scalar(yout[:, s], bank[6][:, 0:D], meta[:, s, 4:5], None, ALU.mult).then_inc(yout_done, 1)

            def pair(p):
                for s in range(2):
                    g = 2 * p + s
                    middle(g, 0)
                    if not isinstance(g, int) or g:
                        low_turned(g - 1, 1)
                    rows(g + 1, 1 - s)
                    middle(g, 1)
                    low_turned(g, 0)
                    if not isinstance(g, int) or g:
                        weigh(g - 1, 1 - s)
                    row_meta(g + 1, 1 - s)
            npair = dve.value_load(tab_n[0:1, 0:1], min_val=SURE, max_val=NB // 2)
            row_meta(0, 0)
            rows(0, 0)
            pair(0)
            with dve.Fori(0, SURE - 1) as it:
                pair(it + 1)
            with dve.Fori(0, NB // 2 - SURE) as it:
                with dve.If(npair - it > SURE):
                    pair(it + SURE)
            last = dve.value_load(tab_n[0:1, 1:2], min_val=2 * SURE - 2, max_val=NB - 2) + 1
            low_turned(last, 1)
            weigh(last, 1)

            for b in range(B):
                tiles = slice(NQ * b, NQ * (b + 1))
                dve.wait_ge(y_back[b], 32)
                if b == 0:
                    dve.wait_ge(scattered, 16 * 2 * NT)
                link(dve.tensor_tensor(ya[:, tiles, :], ya[:, tiles, :], yb[:, tiles, :], ALU.add))
                link(dve.tensor_tensor(xtok[:, tiles, 0:D], xtok[:, tiles, 0:D], ya[:, tiles, :], ALU.add))
                layernorm(range(NQ * b, NQ * (b + 1)), 1e-5).then_inc(fin_done, 1)

        @block.tensor
        def _(pe):
            def claim(item):
                k, n = place[item]
                if n:
                    pe.wait_ge(drained[k], n)
                return bank[k]

            def fill(item, ins):
                ins.then_inc(filled[place[item][0]], 1)

            def project(kind, n):
                b, j = divmod(n, NJ)
                o = claim((kind, n))
                col = (0 if kind == "xp" else DI) + j * P
                for k in range(KD):
                    mm = pe.matmul(o[:, :], winT[:, k, col:col + P], xcol[:, k, b * S:(b + 1) * S],
                                   start=(k == 0), stop=(k == KD - 1))
                fill((kind, n), mm)

            def scan_inputs(b):
                pe.wait_ge(xc_done, NJ * (b + 1))
                o = claim(("xd", b))
                for q in range(NQ):
                    t = b * S + q * P
                    for j in range(NJ):
                        mm = pe.matmul(o[:, q * NX:(q + 1) * NX], xc[:, j, t:t + P], wxT[:, j, :],
                                       start=(j == 0), stop=(j == NJ - 1))
                fill(("xd", b), mm)
                for q in range(NQ):
                    i = NQ * b + q
                    o = claim(("xt", i))
                    for j in range(NJ):
                        mm = pe.transpose(o[:, j * P:(j + 1) * P], xc[:, j, i * P:(i + 1) * P], ident[:, :])
                    fill(("xt", i), mm)
            pe.wait_ge(ld_first, 32)
            for n in range(B * NJ):
                project("xp", n)
                project("z", n)
                if n % NJ == 1 and n > NJ:
                    if n < 2 * NJ:
                        pe.wait_ge(consts_done, 1)
                        pe.wait_ge(ld_conv, 16 * 3)
                    scan_inputs(n // NJ - 1)
            scan_inputs(B - 1)

            pe.wait_ge(dtA_done, 1)

            def total(item, h, left, last=False):
                mm = pe.matmul(ps(item)[:, h * 256:(h + 1) * 256], left, dtA[:, :, 0:NS], start=True, stop=True)
                if last:
                    fill(item, mm)
            claim("cumA")
            total("cumA", 0, tri32[:, :])
            total("cumA", 1, tri[:, :], True)
            claim("cumB")
            total("cumB", 0, upto[:, 0:P])
            total("cumB", 1, upto[:, P:2 * P], True)
            claim("cumC")
            total("cumC", 0, upto[:, 2 * P:3 * P])
            total("cumC", 1, ones[:, :], True)
            claim("cumD")
            total("cumD", 0, own[:, :])

            def same_place(t, q):
                return t[:, B * q:B * (q + 1), :].rearrange("p b n -> p (b n)")
            for q in range(NQ):
                mm = pe.matmul(ps("cumD")[:, 256 + q:257 + q], same_place(dtA, q), ones[:, 0:1], start=True, stop=True)
            fill("cumD", mm)
            pe.wait_ge(exp_done, 3)
            pe.wait_ge(guard_in, 1)

            def turn4(item, src):
                o = claim(item)
                for q in range(NQ):
                    mm = pe.transpose(o[:, q * P:(q + 1) * P], src(q), ident[:, :])
                fill(item, mm)
            turn4("abT", lambda q: same_place(abar, q))
            turn4("vbT", lambda q: same_place(vabs, q))
            pe.wait_ge(factors_done, 1)
            turn4("gcT", lambda q: same_place(rc, q))
            turn4("lbT", lambda q: same_place(lb, q))
            turn4("rbT", lambda q: same_place(rb, q))
            for name, src in (("laT", la), ("raT", ra)):
                for g in range(2):
                    turn4((name, g), lambda q: src[:, B * q + 2 * g:B * q + 2 * g + 2, :].rearrange("p b n -> p (b n)"))
            for q in range(NQ - 1):
                o = claim(("S", q))
                for b in range(B):
                    mm = pe.matmul(o[NSP * b:NSP * (b + 1), :], wt[:, B * q + b, :], xct(b, q), start=True, stop=True)
                fill(("S", q), mm)
            for item in ("gcT", "lbT", "rbT", ("laT", 0), ("laT", 1), ("raT", 0), ("raT", 1)):
                wait_drained(pe, item)

            def mixes(b):
                o = claim(("M1", b))
                r = slice(NSP * b, NSP * (b + 1))
                for q in range(NQ):
                    mm = pe.matmul(o[:, q * P:(q + 1) * P], lbT[r, q, :], rbT[r, q, :], start=True, stop=True)
                fill(("M1", b), mm)
                o = claim(("M2", b))
                r = slice(64 * (b % 2), 64 * (b % 2) + 64)
                for q in range(NQ):
                    mm = pe.matmul(o[:, q * P:(q + 1) * P], laT[r, b // 2, q, :], raT[r, b // 2, q, :], start=True, stop=True)
                fill(("M2", b), mm)

            def outputs(b):
                wait_drained(pe, ("M2", b))
                r = slice(NSP * b, NSP * (b + 1))
                for j in range(NJ):
                    o = claim(("y", b, j))
                    for q in range(NQ):
                        part = o[:, q * P:(q + 1) * P]
                        mm = pe.matmul(part, xct(b, q)[:, j * P:(j + 1) * P], mts[:, b % 2, q, :], start=True, stop=(q == 0))
                        if q:
                            mm = pe.matmul(part, hst[r, q - 1, j * P:(j + 1) * P], gcT[r, q, :], start=False, stop=True)
                    fill(("y", b, j), mm)
            def out_project(b):
                pe.wait_ge(gated, NJ * (b + 1))
                if b == 0:
                    pe.wait_ge(ld_x, 32)
                for o2 in range(2):
                    o = claim(("o", b, o2))
                    for q in range(2):
                        t = (NQ * b + 2 * o2 + q) * P
                        for j in range(NJ):
                            mm = pe.matmul(o[:, q * D:(q + 1) * D], zs[:, j, t:t + P], woutT[:, j, :],
                                           start=(j == 0), stop=(j == NJ - 1))
                    fill(("o", b, o2), mm)

            def turn_norm1(b):
                pe.wait_ge(x1_done, b + 1)
                for k in range(KD):
                    o = claim(("x1t", b, k))
                    for q in range(NQ):
                        mm = pe.transpose(o[:, q * P:(q + 1) * P], xtok[:, NQ * b + q, k * P:(k + 1) * P], ident[:, :])
                    fill(("x1t", b, k), mm)
            def gates(b):
                for k in range(KD):
                    wait_drained(pe, ("x1t", b, k))
                if b == 0:
                    pe.wait_ge(ld_ctx, 16 * (1 + H))
                    pe.wait_ge(gk_done, 1)
                    claim("g")
                for i in range(NQ * b, NQ * (b + 1)):
                    t = slice(i * P, (i + 1) * P)
                    for n, src in enumerate((xcol, ctxc)):
                        for k in range(KD):
                            mm = pe.matmul(ps("g")[:, i * 2 * H:(i + 1) * 2 * H], src[:, k, t], gk[:, n * KD + k, :],
                                           start=(n == 0 and k == 0), stop=(n == 1 and k == KD - 1))
                if b == B - 1:
                    fill("g", mm)
            mixes(0)
            for b in range(B + 2):
                if b + 1 < B:
                    mixes(b + 1)
                if b == 0:
                    pe.wait_ge(hst_done, 1)
                    pe.wait_ge(scan_checked, 1)
                if b < B:
                    outputs(b)
                if 1 <= b <= B:
                    out_project(b - 1)
                if b >= 2:
                    turn_norm1(b - 2)
                    gates(b - 2)

            pe.wait_ge(lf_done, 1)
            o = claim("cum")
            pe.matmul(o[:, 0:NT * H], tri[:, :], lfb, start=True, stop=False)
            fill("cum", pe.matmul(o[:, 0:NT * H], ones[:, :], lfpre, start=False, stop=True))
            pe.wait_ge(a_done, 1)
            o = claim("aT")
            for i in range(NT):
                b, q = divmod(i, NQ)
                mm = pe.matmul(o[NSP * b:NSP * (b + 1), q * P:(q + 1) * P], apad[:, i, :], ident[:, :], start=True, stop=True)
            fill("aT", mm)
            pe.wait_ge(mrow_done, 1)
            o = claim("mT")
            for q in range(NQ):
                mm = pe.transpose(o[:, q * P:(q + 1) * P], mrow[:, q * P:(q + 1) * P], ident[:, :])
            fill("mT", mm)
            pe.wait_ge(z_done, 1)
            o = claim("R")
            fill("R", pe.matmul(o[:, :], ones[:, :], zsel, start=True, stop=True))

            def states(b):
                pe.wait_ge(kw_done, b + 1)
                pe.wait_ge(vones_done, 1)
                o = claim(("H", b))
                n = 0
                for c in range(1, NQ):
                    for h in range(H):
                        r = slice(64 * (h % 2), 64 * (h % 2) + 64)
                        col = ((c - 1) * 2 + h // 2) * DV
                        for s in range(c):
                            mm = pe.matmul(o[r, col:col + DV], kw[:, n + s, h, :], vaug[:, NQ * b + s, h, :],
                                           start=(s == 0), stop=(s == c - 1))
                    n += c
                fill(("H", b), mm)

            def front(i):
                b, c = divmod(i, NQ)
                t = slice(i * P, (i + 1) * P)
                if c == 0:
                    states(b)
                o = claim(("nm", i))
                r = slice(NSP * b, NSP * (b + 1))
                for h in range(H):
                    mm = pe.matmul(o[:, h * P:(h + 1) * P], negsel[r, h, :], mrow[r, c * P:(c + 1) * P],
                                   start=True, stop=True)
                fill(("nm", i), mm)
                if c:
                    wait_drained(pe, ("H", b))
                for par, item in ((0, ("sA", i)), (1, ("sB", i))):
                    o = claim(item)
                    r = slice(64 * par, 64 * par + 64)
                    for k in range(KD):
                        mm = pe.matmul(o[:, k * P:(k + 1) * P], ctxc[r, k, t], xcol[r, k, t], start=True, stop=True)
                    for k in range(KD if c else 0):
                        mm = pe.matmul(o[:, 2 * P + k * DV:2 * P + (k + 1) * DV], xcol[r, k, t], hs[r, b % 2, c - 1, k, :],
                                       start=True, stop=True)
                    fill(item, mm)

            def values(i):
                pe.wait_ge(prob_done, 2 * (i + 1))
                o = claim(("num", i))
                for h in range(H):
                    mm = pe.matmul(o[:, h * DV:(h + 1) * DV], prob[:, i % 2, h, :], vaug[:, i, h, :], start=True, stop=True)
                fill(("num", i), mm)

            def turn_norm2(b):
                pe.wait_ge(x2_done, b + 1)
                for i in range(NQ * b, NQ * (b + 1)):
                    o = claim(("x2t", i))
                    for k in range(KD):
                        mm = pe.transpose(o[:, k * P:(k + 1) * P], xtok[:, i, k * P:(k + 1) * P], ident[:, :])
                    fill(("x2t", i), mm)

            def logits(b):
                o = claim(("lg", b))
                for q in range(NQ):
                    wait_drained(pe, ("x2t", NQ * b + q))
                    for k in range(KD):
                        mm = pe.matmul(o[:, q * E:(q + 1) * E], x2c[:, q, k, :], rw[:, k, :],
                                       start=(k == 0), stop=(k == KD - 1))
                fill(("lg", b), mm)

            def ranks(b):
                pe.wait_ge(picks_done, 2 * (b + 1))
                o = claim(("rk", b))
                pe.matmul(o[:, 0:NQ * E], before16[:, :], picks[:, NQ * b:NQ * (b + 1), :], start=True, stop=False)
                fill(("rk", b), pe.matmul(o[:, 0:NQ * E], ones16[:, :], picksum[:, NQ * b:NQ * (b + 1), :],
                                          start=False, stop=True))
            front(0)
            for i in range(NT):
                if i + 1 < NT:
                    front(i + 1)
                if i % NQ == 2 and i > NQ:
                    turn_norm2(i // NQ - 1)
                    logits(i // NQ - 1)
                if i % NQ == 3 and i > NQ:
                    ranks(i // NQ - 1)
                values(i)
            turn_norm2(B - 1)
            logits(B - 1)
            ranks(B - 1)
            fill("cnt", pe.matmul(claim("cnt")[:, 0:E], ones16[:, :], picksum[:, NT, :], start=True, stop=True))

            wait_drained(pe, "cnt")
            pe.wait_ge(tables_done, 1)
            THREE = ((0, 0), (0, 1), (1, 0))

            def turn_rows(g, s):
                pe.wait_ge(xg_loaded[s], 8 * (g - s) + 16)
                if not isinstance(g, int) or g:
                    pe.wait_ge(xgT_done, g)
                for k in range(KD):
                    mm = pe.transpose(bank[7][:, k * P:(k + 1) * P], xg[:, s, k * P:(k + 1) * P], ident[:, :])
                mm.then_inc(xg_turned, 1)

            def moving(off, part, col, n):
                at = part * WCOLS + col
                return wslot(off)[:, at:at + n]

            def up(g, s, u, off):
                pe.wait_ge(xgT_done, g + 1)
                if not isinstance(g, int) or g:
                    pe.wait_ge(mid_done, 2 * g + (u - 1))
                for m in range(2):
                    for k in range(KD):
                        for a, w in THREE:
                            mm = pe.matmul(bank[2 * u + m][:, :], (xTh, xTl)[a][:, s, k, :],
                                           moving(off, w, m * KD * F + k * F + u * HALF, HALF),
                                           start=(k == 0 and a + w == 0), stop=(k == KD - 1 and a == 1))
                mm.then_inc(up_done, 1)

            def turn(g, u):
                pe.wait_ge(mid_done, 2 * g + (u + 1))
                if not isinstance(g, int) or g:
                    pe.wait_ge(hTl_done, 2 * g + (u - 1))
                for c in range(4):
                    mm = pe.transpose(bank[4 + u][:, c * P:(c + 1) * P], hmid[:, u, c * P:(c + 1) * P], ident[:, :])
                mm.then_inc(turned, 1)

            def down(g, u, off):
                pe.wait_ge(hTh_done, 2 * g + (u + 1))
                pe.wait_ge(hTl_done, 2 * g + (u + 1))
                if u == 0 and (not isinstance(g, int) or g):
                    pe.wait_ge(yout_done, g)
                for c in range(4):
                    for a, w in THREE:
                        mm = pe.matmul(bank[6][:, 0:D], (hTh, hTl)[a][:, u, c, :],
                                       moving(off, w, 2 * KD * F + (4 * u + c) * D, D),
                                       start=(u == 0 and c == 0 and a + w == 0), stop=(u == 1 and c == 3 and a == 1))
                if u == 1:
                    mm.then_inc(y_done, 1)

            def event_of(g):
                return pe.value_load(tab_event[0:1, bass.ds(g, 1)]) & (E - 1)

            def offset_of(event):
                return ((event & 1) * (slot_at[1] - slot_at[0]) + slot_at[0]).with_bounds(min_val=0, max_val=max(slot_at))

            def pair(p):
                off = None
                for s in range(2):
                    g = 2 * p + s
                    first = isinstance(g, int) and g == 0
                    event = event_of(g)
                    last_off, off = off, offset_of(event)
                    pe.wait_ge(w_ready, event + 1)
                    up(g, s, 0, off)
                    if s == 0 and not first:
                        last_off = offset_of(event_of(g - 1))
                    if not first:
                        turn(g - 1, 1)
                        down(g - 1, 0, last_off)
                    turn_rows(g + 1, 1 - s)
                    up(g, s, 1, off)
                    turn(g, 0)
                    if not first:
                        down(g - 1, 1, last_off)
            turn_rows(0, 0)
            npair = pe.value_load(tab_n[0:1, 0:1], min_val=SURE, max_val=NB // 2)
            pair(0)
            with pe.Fori(0, SURE - 1) as it:
                pair(it + 1)
            with pe.Fori(0, NB // 2 - SURE) as it:
                with pe.If(npair - it > SURE):
                    pair(it + SURE)
            last = pe.value_load(tab_n[0:1, 1:2], min_val=2 * SURE - 2, max_val=NB - 2) + 1
            off = offset_of(event_of(last))
            turn(last, 1)
            down(last, 0, off)
            down(last, 1, off)


_INS = ["x", "xT", "ctx", "ctxT", "w_inT", "conv_w", "conv_b", "w_xT", "a_log", "d_param", "w_outT", "gate_k", "gate_b",
        "outnorm", "router_w", "w_exp"]


def kernel(**inputs):
    import numpy as np
    import concourse.bacc as bacc
    from concourse.bass_utils import run_bass_kernel_spmd

    a = {k: np.asarray(v) for k, v in inputs.items()}
    x, ctx = (a[k].reshape(T, D) for k in ("x", "ctx_1024"))
    w1, w3 = (a[k].reshape(E, KD, P, F).transpose(0, 2, 1, 3).reshape(E, P, KD * F) for k in ("L0_ffn_w1", "L0_ffn_w3"))
    w2 = a["L0_ffn_w2"].reshape(E, F // P, P, D).transpose(0, 2, 1, 3).reshape(E, P, (F // P) * D)
    laid = {
        "x": x, "xT": x.T, "ctx": ctx, "ctxT": ctx.T,
        "w_inT": a["L0_attn_W_in"].T, "conv_w": a["L0_attn_conv_w"], "conv_b": a["L0_attn_conv_b"].reshape(NJ, P).T,
        "w_xT": a["L0_attn_W_xproj"].T, "a_log": a["L0_attn_A_log"], "d_param": a["L0_attn_D_param"].reshape(NJ, P).T,
        "w_outT": a["L0_attn_W_out"].T,
        "gate_k": np.concatenate([a["L0_xattn_ig_kernel"], a["L0_xattn_fg_kernel"]], axis=1),
        "gate_b": np.concatenate([a["L0_xattn_ig_bias"], a["L0_xattn_fg_bias"]]),
        "outnorm": a["L0_xattn_outnorm_weight"].reshape(D), "router_w": a["L0_ffn_gate_w"],
        "w_exp": np.concatenate([w1, w3, w2], axis=2),
    }
    nc = bacc.Bacc("TRN2", target_bir_lowering=False, num_devices=1)
    arrays, args = {}, []
    for name in _INS:
        v = np.ascontiguousarray(laid[name])
        arrays[f"in_{name}"] = v
        args.append(nc.dram_tensor(f"in_{name}", v.shape, mybir.dt.from_np(v.dtype), kind="ExternalInput").ap())
    args.append(nc.dram_tensor("out", (T, D), F32, kind="ExternalOutput").ap())
    decoder_kernel(nc, *args)
    r = run_bass_kernel_spmd(nc, [arrays], core_ids=[0])
    return r.results[0]["out"].reshape(B, S, D)
```

```python
from contextlib import ExitStack

import concourse.bass as bass
from concourse import mybir

F32 = mybir.dt.float32
F32R = mybir.dt.float32r
BF16 = mybir.dt.bfloat16
I32 = mybir.dt.int32
ALU = mybir.AluOpType
ACT = mybir.ActivationFunctionType
AX_X = mybir.AxisListType.X
RMAX = bass.bass_isa.ReduceOp.max

P = 128
B, S, D = 4, 512, 256
T = B * S
NQ = S // P
NT = T // P
KD = D // P
DI = 2 * D
NJ = DI // P
NS, NSP = 16, 32
TAPS = 4
NX = 2 * NS + 1
CH = 32
NC = P // CH
H = 4
DH = D // H
DV = DH + 1
E, F = 8, 1024
HALF = F // 2
NB = (2 * T + E * (P - 1)) // P + 1
NB += NB % 2
REGION = T + P
ROW = D + 4
WCOLS = 2 * KD * F + (F // P) * D
SURE = 2 * T // P // 2
DT_MIN, DT_MAX = 0.001, 0.1
CLIP = 100.0
JITTER2 = 0.02
BIG = 3.0e38
HORNER = 10
GATES_LAST = (B - 1) * NJ
GROUPS = ((0, 2), (2, 1), (3, 1))
UNITS = tuple((NQ * b, NQ) for b in range(B - 1)) + ((NT - NQ, NQ - 1), (NT - 1, 1))
ROUTE_AT = NT - 3
STATE_LIMIT, DECAY_LIMIT = 99.0, 80.0


def decoder_kernel(nc, x, xT, ctx, ctxT, w_inT, conv_w, conv_b, w_xT, a_log, d_param, w_outT, gate_k, gate_b,
                   outnorm, router_w, w_exp, out):
    slots = nc.dram_tensor("slots", [(E * REGION) + P, ROW], F32).ap()
    yrows = nc.dram_tensor("yrows", [2 * T + P, D], F32).ap()
    yscan = nc.dram_tensor("scan_out", [P, B, NJ, S], F32).ap()
    coef = nc.dram_tensor("scan_coef", [S, 3 * B * NS], F32).ap()

    with ExitStack() as stack:
        def sb(name, cols, dt=F32):
            return stack.enter_context(nc.sbuf_tensor(name, [P, cols], dt))

        def sem(name):
            return stack.enter_context(nc.semaphore(name))

        xtok = sb("xtok", NT * ROW)[:, :].rearrange("p (i c) -> p i c", c=ROW)
        xcol = sb("xcol", KD * T)[:, :].rearrange("p (k t) -> p k t", k=KD)
        n1, n2, n3, n4 = KD * 2 * DI + 4 * 516 + 2 * S, NT * H * DV + KD * T, NJ * T, 3 * WCOLS
        with ExitStack() as early:
            region1, region2, region3, region4 = (
                early.enter_context(nc.sbuf_tensor(f"region{k + 1}", [P, n], F32))[:, :] for k, n in enumerate((n1, n2, n3, n4)))
        with nc.sbuf_tensor("under_wstage", [P, n1 + n2 + n3], F32), nc.sbuf_tensor("wstage", [P, WCOLS], F32) as raw:
            wstage = raw[:, :]
        region1r = sb("experts_x", n1, F32R)
        bigr = sb("experts_w", n2 + n3 + n4, F32R)
        region3r = bigr[:, n2:n2 + n3]

        def carve(region, at, shape):
            n = 1
            for s in shape:
                n *= s
            v = region[:, at[0]:at[0] + n]
            at[0] += n
            names = "abcdef"[:len(shape)]
            if len(shape) == 1:
                return v
            return v.rearrange(f"p ({' '.join(names)}) -> p {' '.join(names)}",
                               **{c: s for c, s in zip(names[1:], shape[1:])})

        at = [0]
        winT = carve(region1, at, (KD, 2 * DI))
        xpad = carve(region1, at, (4, 516))
        cbuf = carve(region1, at, (2, S))
        at = [0]
        gcT = carve(region1, at, (NQ, P))
        lbT = carve(region1, at, (NQ, P))
        rbT = carve(region1, at, (NQ, P))
        laT = carve(region1, at, (2, NQ, P))
        raT = carve(region1, at, (2, NQ, P))
        hst = carve(region1, at, (NQ - 1, DI))
        at = [0]
        xdbl = carve(region2, at, (NT, NX))
        dtA = carve(region2, at, (NT, NSP))
        abar = carve(region2, at, (NT, NSP))
        vabs = carve(region2, at, (NT, NSP))
        bbar = carve(region2, at, (NT, NS))
        cumt = carve(region2, at, (NT, NS))
        ediff = carve(region2, at, (NC - 1, NT, NS))
        la = carve(region2, at, (NT, 4 * NS))
        ra = carve(region2, at, (NT, 4 * NS))
        lb = carve(region2, at, (NT, NSP))
        rb = carve(region2, at, (NT, NSP))
        rc = carve(region2, at, (NT, NSP))
        wt = carve(region2, at, (NT, NSP))
        aneg = carve(region2, at, (NS,))
        assert at[0] <= NT * H * DV + KD * T, at
        at = [0]
        vaug = carve(region2, at, (NT, H, DV))
        ctxc = carve(region2, at, (KD, T))
        at = [0]
        xc = carve(region3, at, (NJ, T))
        at = [0]
        zsel = carve(region3, at, (NQ, P))
        decay = carve(region3, at, (2, H, P))
        prob = carve(region3, at, (2, H, P))
        kw = carve(region3, at, (6, H, DH))
        hs = carve(region3, at, (2, NQ - 1, 2, 2, DV))
        late = 2 * WCOLS - n2
        tot_at = NJ * T - 2 * NQ * H * DV
        assert max(at[0], late) <= tot_at, at
        tot = carve(region3, [tot_at], (2, NQ, H, DV))
        at = [0]
        zs = carve(region4, at, (NJ, T))
        yx = carve(region4, at, (B + 1, NQ * DI))
        assert at[0] <= 3 * WCOLS, at

        def xct(b, q):
            return yx[:, b + 1, q * DI:(q + 1) * DI]

        def ybuf(b, j):
            return yx[:, b, j * S:(j + 1) * S]
        gT = ybuf(0, 0)
        slot_at = (n2 + n3 + WCOLS, 0)

        def wslot(off):
            return bigr[:, bass.ds(off, 2 * WCOLS)]
        at = [0]
        xg = carve(region1, at, (2, ROW))
        xTh = carve(region1r, at, (2, KD, P))
        xTl = carve(region1r, at, (2, KD, P))
        gsil = carve(region1, at, (2, HALF))
        hmid = carve(region1, at, (2, HALF))
        yout = carve(region1, at, (2, D))
        assert at[0] <= KD * 2 * DI + 4 * 516 + 2 * S
        at = [late]
        hTh = carve(region3r, at, (2, 4, P))
        hTl = carve(region3r, at, (2, 4, P))
        assert at[0] <= NJ * T, at
        ya = region2[:, 0:NT * D].rearrange("p (i d) -> p i d", d=D)
        yb = region2[:, NT * D:2 * NT * D].rearrange("p (i d) -> p i d", d=D)

        woutT = sb("woutT", NJ * D)[:, :].rearrange("p (j d) -> p j d", j=NJ)
        wxT = sb("wxT", NJ * NX)[:, :].rearrange("p (j n) -> p j n", j=NJ)
        convw = sb("convw", NJ * TAPS)[:, :].rearrange("p (j k) -> p j k", j=NJ)
        convb = sb("convb", NJ)
        dpar = sb("dpar", NJ)
        alog = sb("alog", NS)
        gk = sb("gk", 3 * KD * 2 * H)[:, :].rearrange("p (k g) -> p k g", k=3 * KD)
        gb = sb("gb", 2 * H)
        onw = sb("onw", D)
        rw = sb("rw", KD * E)[:, :].rearrange("p (k e) -> p k e", k=KD)

        ident = sb("ident", P)
        ones = sb("ones", P)
        tri = sb("tri", P)
        tri32 = sb("tri32", P)
        own = sb("own", P)
        upto = sb("upto", (NC - 1) * P)
        gkpad = upto[:, 0:2 * KD * NSP].rearrange("p (k n) -> p k n", k=2 * KD)
        before16 = sb("before16", P, BF16)
        ones16 = sb("ones16", P, BF16)
        never16 = sb("never16", P, BF16)
        headneg = [sb(f"headneg{n}", H) for n in range(3)]
        notfirst, lastpart = sb("notfirst", 1), sb("lastpart", 1)
        mask_la = sb("mask_la", NC - 1)
        mask_ra = sb("mask_ra", NC - 1)
        eid = sb("eid", E)
        eoff = sb("eoff", E)
        tokid = sb("tokid", NT)
        steps128 = sb("steps128", NT)
        blkid = sb("blkid", NB + 2)
        padrow = sb("padrow", ROW)

        small = sb("small", 997)
        at = [0]
        dtv = carve(small, at, (NT,))
        expv = carve(small, at, (NT,))
        horner = carve(small, at, (NT,))
        xmax = carve(small, at, (NT,))
        guard = carve(small, at, (2,))
        guardall = carve(small, at, (2,))
        dec = carve(small, at, (NQ,))
        stats = carve(small, at, (NQ * H, 6))
        mv = carve(small, at, (NQ * H, 2))
        rsv = carve(small, at, (NQ * H,))
        rsy = carve(small, at, (NQ * H,))
        gt = carve(small, at, (NT, 2 * H))
        lfa = carve(small, at, (NT, H))
        lfb = carve(small, at, (NT, H))
        lfpre = carve(small, at, (B, NQ, H))
        av = carve(small, at, (NT, H))
        cumS = carve(small, at, (NT, H))
        emx = carve(small, at, (NT, H))
        fac = carve(small, at, (9, B, H))
        den = carve(small, at, (NQ, H))
        neghalf = carve(small, at, (1,))
        shift = horner[:, 0:B * NQ]
        assert at[0] <= 997, at
        bad = sb("bad", 1, I32)

        at = [0]
        mneg = carve(region1, at, (NQ, H, P // 2)).bitcast(BF16)
        mrest = region3[:, 0:S]
        mpart = prob.rearrange("p a h t -> p (a h t)")[:, 0:S // 2].bitcast(BF16)
        apad = carve(region1, at, (NT, NSP))
        hbuf = carve(region1, at, (NQ, H, DH))
        mS = carve(region1, [at[0] - NQ * D], (NQ, B, NSP))
        mrow = carve(region1, [at[0] - NQ * D + NQ * B * NSP], (S,))
        assert NQ * D >= NQ * B * NSP + S
        x2c = carve(region1, at, (NQ, KD, P))
        cmp16 = carve(region1, at, (E, NT))
        cmpb = carve(region1, at, (NB + 2, E))
        lgs = carve(region1, at, (NT, E))
        MOST = NQ * max(n for _, n in GROUPS)
        lg2, oh1, oh2, labs, cand, exp1, exp2, slotf = (carve(region1, at, (MOST, E)) for _ in range(8))
        top1 = carve(region1, at, (MOST,))
        top2 = carve(region1, at, (MOST,))
        posf = carve(region1, at, (2, MOST))
        sums = carve(region1, at, (2, MOST))
        assert at[0] <= KD * 2 * DI + 4 * 516 + 2 * S
        pos = sb("pos", 2 * NT, I32)[:, :].rearrange("p (k i) -> p k i", k=2)
        picks = sb("picks", NT * E, BF16)[:, :].rearrange("p (i e) -> p i e", e=E)
        picksum = sb("picksum", (NT + 1) * E, BF16)[:, :].rearrange("p (i e) -> p i e", e=E)
        cnt = sb("cnt", E)
        nblk = sb("nblk", E)
        endblk = sb("endblk", E)
        eblk = sb("eblk", NB + 2)
        sblk = sb("sblk", NB + 2)
        hasblk = sb("hasblk", E)
        cumev = sb("cumev", E)
        evblk = sb("evblk", NB)
        tab_slot = sb("tab_slot", NB + 2, I32)
        tab_event = sb("tab_event", NB, I32)
        tab_noff = sb("tab_noff", NB, I32)
        tab_first = sb("tab_first", NB, I32)
        tab_pad = sb("tab_pad", E, I32)
        tab_ev = sb("tab_ev", E + 2, I32)
        tab_n = sb("tab_n", 3, I32)
        ringf = sb("ringf", NB + 2)
        ringg = sb("ringg", NB)
        zero = sb("zero", 1)
        meta = sb("meta", 2 * 6)[:, :].rearrange("p (s c) -> p s c", s=2)
        rid = sb("rid", 2, I32)
        fb_c = carve(region1, [2 * B * NJ * NS], (4 * 3 * B * NS,))
        mts = xcol[:, :, (B - 1) * S:].rearrange("p s (q t) -> p s q t", q=NQ)
        fb_h = carve(region1, [0], (B, NJ, NS))
        fb_t = carve(region1, [B * NJ * NS], (B, NJ, NS))
        fb_y = carve(region1, [2 * B * NJ * NS + 4 * 3 * B * NS], (B, NJ, 4))

        bank = [stack.enter_context(nc.psum_tensor(f"bank{k}", [P, 512], F32)) for k in range(8)]

        place, turns = {}, [0] * 8

        def plan(item, k):
            place[item] = (k, turns[k])
            turns[k] += 1

        for n in range(B * NJ):
            plan(("xp", n), n % 2)
            if n < GATES_LAST:
                plan(("z", n), 2 + n % 2)
            if n % NJ == 1 and n > NJ:
                b = n // NJ - 1
                plan(("xd", b), 4)
                for q in range(NQ):
                    plan(("xt", NQ * b + q), 5 + (NQ * b + q) % 3)
        for n in range(GATES_LAST, B * NJ):
            plan(("z", n), 2 + n % 2)
        plan(("xd", B - 1), 4)
        for q in range(NQ):
            plan(("xt", NQ * (B - 1) + q), 5 + (NQ * (B - 1) + q) % 3)
        for n, k in (("cumA", 0), ("cumB", 1), ("cumC", 2), ("cumD", 3), ("abT", 4), ("vbT", 5), ("gcT", 6),
                     ("lbT", 7), ("rbT", 0), (("laT", 0), 1), (("laT", 1), 2), (("raT", 0), 3), (("raT", 1), 4)):
            plan(n, k)
        for q in range(NQ - 1):
            plan(("S", q), (7, 5, 6)[q])
        for b in range(B + 2):
            for m in ((0, 1) if b == 0 else (b + 1,)):
                if m < B:
                    plan(("M1", m), 4)
                    plan(("M2", m), 5)
            for j in range(NJ if b < B else 0):
                plan(("y", b, j), (NJ * b + j) % 3)
            for o in range(2 if 1 <= b <= B else 0):
                plan(("o", b - 1, o), 6 + o)
            for k in range(KD if b >= 2 else 0):
                plan(("x1t", b - 2, k), 4 + k)
        plan("gT", 3)
        plan("g", 2)
        plan("cum", 2)
        plan("aT", 3)
        plan("mT", 5)
        plan("R", 6)

        def plan_front(i):
            if i % NQ == 0:
                plan(("H", i // NQ), 2)
            plan(("nm", i), 5)
            plan(("sA", i), (6, 0)[i % 2])
            plan(("sB", i), (7, 1)[i % 2])

        def halves(u):
            first, n = UNITS[u]
            return [range(i, min(i + 2, first + n)) for i in range(first, first + n, 2)]

        def plan_norm2(u):
            for o in range(len(halves(u))):
                plan(("x2t", u, o), 3)
            plan(("lg", u), 2)
        plan_front(0)
        for i in range(NT):
            if i + 1 < NT:
                plan_front(i + 1)
            if i == ROUTE_AT + 1:
                plan(("rk", 0), 2)
            plan(("num", i), 4)
            if i % NQ == 3 and i > NQ:
                plan_norm2(i // NQ - 1)
        for u in range(B - 1, len(UNITS)):
            plan_norm2(u)
        plan(("rk", 1), 2)
        plan(("rk", 2), 2)
        plan("cnt", 2)

        WPARTS = 6
        WPART = WCOLS // WPARTS
        SPLIT_HI, SPLIT_LO = 0, 6
        ACT_PART = 2 * WCOLS // 3

        def hi_of(off):
            return wslot(off)[:, 0:WCOLS]

        def lo_of(off):
            return wslot(off)[:, WCOLS:2 * WCOLS]

        filled = [sem(f"bank{k}_filled") for k in range(8)]
        drained = [sem(f"bank{k}_drained") for k in range(8)]
        ld_conv, ld_x, ld_small, ld_ctx = (sem(f"{n}_loaded") for n in ("conv", "x", "small", "ctx"))
        ld_win, ld_xT = [sem(f"win{n}_loaded") for n in range(2)], [sem(f"xT{b}_loaded") for b in range(B)]
        consts_done = sem("consts_done")
        pool_step, dve_step, act_step = sem("pool_step"), sem("dve_step"), sem("act_step")
        conv_done, xc_done = sem("conv_done"), sem("xc_done")
        vmin_done, exp_done, dtA_done = sem("vmin_done"), sem("exp_done"), sem("dtA_done")
        cum_ready, cumexp_done = sem("cum_ready"), sem("cumexp_done")
        la_done, ediff_done, factors_done, guard_in = (sem(n) for n in ("la_done", "ediff_done", "factors_done", "guard_in_done"))
        guard_done, guard_red, bad_done, scan_checked = (sem(n) for n in ("guard_done", "guard_reduced", "bad_done", "scan_checked"))
        hst_done, gated = sem("hst_done"), sem("gated")
        x1_done, gk_done, mneg_done, pads_known = sem("x1_done"), sem("gk_done"), sem("mneg_done"), sem("pads_known")
        gabs_done, gexp_done, lf_done, a_done, mrow_done, z_done, args_done, fac_done = (sem(n) for n in (
            "gabs_done", "gln_done", "lf_done", "a_done", "mrow_done", "zsel_done", "args_done", "fac_done"))
        vones_done, kw_done = sem("vones_done"), sem("kw_done")
        prob_done, heads_done, resid_done, x2_done = (sem(n) for n in ("prob_done", "heads_done", "resid_done", "x2_done"))
        var_done, rs_done = sem("var_done"), sem("rs_done")
        rows_added = sem("rows_added")
        picks_done, rexp_in, rexp_done, row_done, scattered = (sem(n) for n in (
            "picks_done", "router_exp_in", "router_exp_done", "row_done", "scattered"))
        tables_done, events_done, padded = sem("tables_done"), sem("events_done"), sem("padded")
        fb_dma, fb_step, fb_gate, fb_out = (sem(f"fallback_{n}") for n in ("dma", "step", "gate", "out"))
        w_loaded, w_hi, w_ready, w_again, w_step = (sem(n) for n in ("w_loaded", "w_hi", "w_ready", "w_again", "w_step"))
        w_lo, w_part, w_rest, pool_gate, act_gate = (sem(n) for n in ("w_lo", "w_part", "w_rest", "pool_gate", "act_gate"))
        xg_loaded = [sem(f"xg{s}_loaded") for s in range(2)]
        (xg_turned, xgh_done, xgT_done, meta_step, meta_done, up_done, sil_done, mid_done, turned, hTh_done, hTl_done, y_done,
         rid_done, yout_done) = (sem(n) for n in (
             "xg_turned", "xgh_done", "xgT_done", "meta_step", "meta_done", "up_done", "silu_done", "mid_done", "h_turned",
             "hTh_done", "hTl_done", "y_done", "rid_done", "yout_done"))
        y_sent = [sem(f"y{s}_sent") for s in range(2)]
        y_back = [sem(f"yback{b}_loaded") for b in range(B)]
        shift_done, fin_done, out_done = sem("shift_done"), sem("fin_done"), sem("out_done")

        def wait_filled(eng, item):
            k, n = place[item]
            eng.wait_ge(filled[k], n + 1)

        def wait_drained(eng, item):
            k, n = place[item]
            eng.wait_ge(drained[k], n + 1)

        def drain(item, ins):
            ins.then_inc(drained[place[item][0]], 1)

        def ps(item):
            return bank[place[item][0]]

        def bc(ap, axis, shape):
            return ap.unsqueeze(axis).to_broadcast(shape)

        block = stack.enter_context(nc.Block())

        @block.sync
        def _(sp):
            w_in, xk = w_inT.rearrange("(k p) m -> p k m", p=P), xT.rearrange("(k p) t -> p k t", p=P)

            def input_of(b):
                part = slice(b * S, (b + 1) * S)
                sp.dma_start(xcol[:, :, part], xk[:, :, part]).then_inc(ld_xT[b], 16)
            sp.dma_start(winT[:, :, 0:DI], w_in[:, :, 0:DI]).then_inc(ld_win[0], 16)
            input_of(0)
            sp.dma_start(winT[:, :, DI:], w_in[:, :, DI:]).then_inc(ld_win[1], 16)
            input_of(1)
            sp.dma_start(convw, conv_w.rearrange("(j p) k -> p j k", p=P)).then_inc(ld_conv, 16)
            sp.dma_start(convb[:, :], conv_b).then_inc(ld_conv, 16)
            sp.dma_start(wxT, w_xT.rearrange("(j p) n -> p j n", p=P)).then_inc(ld_conv, 16)
            for b in range(2, B):
                input_of(b)
            sp.dma_start(xtok[:, :, 0:D], x.rearrange("(i p) d -> p i d", p=P)).then_inc(ld_x, 16)
            sp.dma_start(woutT, w_outT.rearrange("(j p) d -> p j d", p=P)).then_inc(ld_x, 16)
            sp.dma_start(dpar[:, :], d_param).then_inc(ld_small, 16)
            sp.dma_start(alog[:, :], a_log.partition_broadcast(P)).then_inc(ld_small, 16)
            sp.dma_start(gk, gate_k.rearrange("(k p) g -> p k g", p=P)).then_inc(ld_small, 16)
            sp.dma_start(gb[:, :], gate_b.partition_broadcast(P)).then_inc(ld_small, 16)
            sp.dma_start(onw[:, :], outnorm.partition_broadcast(P)).then_inc(ld_small, 16)
            sp.dma_start(rw, router_w.rearrange("(k p) e -> p k e", p=P)).then_inc(ld_small, 16)
            sp.wait_ge(scan_checked, 1)
            for item in (("laT", 0), ("laT", 1), ("raT", 0), ("raT", 1)):
                wait_filled(sp, item)
            wait_drained(sp, "cumD")
            sp.dma_start(ctxc, ctxT.rearrange("(k p) t -> p k t", p=P)).then_inc(ld_ctx, 16)
            for h in range(H):
                sp.dma_start(vaug[:, :, h, 0:DH], ctx.rearrange("(i p) (h d) -> h p i d", p=P, h=H)[h]).then_inc(ld_ctx, 16)
            for b in range(B):
                for o in range(2):
                    wait_filled(sp, ("o", b, o))
            for e in range(2):
                if e:
                    sp.wait_ge(w_ready, 1)
                sp.dma_start(wstage, w_exp[e]).then_inc(w_loaded, 16)

            sp.wait_ge(pads_known, 1)
            for e in range(E):
                row = sp.value_load(tab_pad[0:1, e:e + 1], min_val=0, max_val=E * REGION)
                sp.dma_start(slots[bass.ds(row, P), :], padrow[:, :]).then_inc(padded, 16)
            sp.dma_start(slots[E * REGION:E * REGION + P, :], padrow[:, :]).then_inc(padded, 16)
            sp.wait_ge(tables_done, 1)
            npair = sp.value_load(tab_n[0:1, 0:1], min_val=SURE, max_val=NB // 2)
            sp.wait_ge(events_done, 1)
            events = sp.value_load(tab_n[0:1, 2:3], min_val=2, max_val=E)
            for n in range(2, E):
                with sp.If(events > n):
                    e = sp.value_load(tab_ev[0:1, n:n + 1], min_val=0, max_val=E - 1)
                    sp.wait_ge(w_ready, n)
                    sp.dma_start(wstage, w_exp[bass.ds(e, 1)].squeeze(0)).then_inc(w_loaded, 16)
            sent, loaded = 16 * npair, 16 * npair + 16
            for s in range(2):
                sp.wait_ge(xg_loaded[s], loaded)
                sp.wait_ge(y_sent[s], sent)
            for b in range(B):
                for k, dst in ((0, ya), (1, yb)):
                    sp.dma_start(dst[:, b * NQ:(b + 1) * NQ, :],
                                 yrows[k * T + b * S:k * T + (b + 1) * S, :].rearrange("(i p) d -> p i d", p=P)
                                 ).then_inc(y_back[b], 16)
            for b in range(B):
                sp.wait_ge(fin_done, b + 1)
                sp.dma_start(out[b * S:(b + 1) * S, :].rearrange("(i p) d -> p i d", p=P),
                             xtok[:, b * NQ:(b + 1) * NQ, 0:D]).then_inc(out_done, 16)
            sp.wait_ge(out_done, 16 * B)

        def scan_step_by_step(pool):
            n = [0]

            def link(ins):
                n[0] += 1
                ins.then_inc(fb_step, 1)
                pool.wait_ge(fb_step, n[0])
            dst = coef.rearrange("(q p) (w b n) -> w b p q n", p=P, w=3, b=B)
            for w, src in enumerate((abar[:, :, 0:NS], bbar, xdbl[:, :, NS:2 * NS])):
                for b in range(B):
                    pool.dma_start(dst[w, b], src.rearrange("p (q b) n -> p b q n", b=B)[:, b]).then_inc(fb_dma, 16)
            pool.wait_ge(fb_dma, 16 * 3 * B)
            for item in ("gcT", "lbT", "rbT", ("laT", 0), ("laT", 1), ("raT", 0), ("raT", 1)):
                wait_drained(pool, item)
            for q in range(NQ - 1):
                wait_filled(pool, ("S", q))
            for b in range(2):
                wait_filled(pool, ("M1", b))
                wait_filled(pool, ("M2", b))
            pool.wait_ge(hst_done, 1)
            link(pool.memset(fb_h, 0.0))
            per = 4
            base = n[0]
            ops = 9
            with pool.Fori(0, S // per) as it:
                pool.dma_start(fb_c, coef.rearrange("(c s) w -> c (s w)", s=per)[bass.ds(it, 1), :]
                               .squeeze(0).partition_broadcast(P)).then_inc(fb_dma, 16)
                pool.wait_ge(fb_dma, 16 * 3 * B + 16 * (it + 1))
                for s in range(per):
                    done = [it * (per * ops) + (base + s * ops)]

                    def step(ins):
                        done[0] = done[0] + 1
                        ins.then_inc(fb_step, 1)
                        pool.wait_ge(fb_step, done[0])
                    c = fb_c[:, s * 3 * B * NS:(s + 1) * 3 * B * NS].rearrange("p (w b n) -> p w b n", w=3, b=B)
                    full = [P, B, NJ, NS]
                    xs = xc.rearrange("p j (b t) -> p b j t", b=B)[:, :, :, bass.ds(it * per + s, 1)].to_broadcast(full)
                    step(pool.tensor_tensor(fb_h, fb_h, bc(c[:, 0], 2, full), ALU.mult))
                    step(pool.tensor_tensor(fb_t, xs, bc(c[:, 1], 2, full), ALU.mult))
                    step(pool.tensor_tensor(fb_h, fb_h, fb_t, ALU.add))
                    pool.sem_inc(fb_gate, 1)
                    step(pool.tensor_scalar(fb_h, fb_h, CLIP, -CLIP, ALU.min, ALU.max))
                    step(pool.tensor_tensor(fb_t, fb_h, bc(c[:, 2], 2, full), ALU.mult))
                    for w in (8, 4):
                        step(pool.tensor_tensor(fb_t[:, :, :, 0:w], fb_t[:, :, :, 0:w], fb_t[:, :, :, w:2 * w], ALU.add))
                    step(pool.tensor_tensor(fb_t[:, :, :, 0:2], fb_t[:, :, :, 0:2], fb_t[:, :, :, 2:4], ALU.add))
                    step(pool.tensor_tensor(fb_y[:, :, :, s:s + 1], fb_t[:, :, :, 0:1], fb_t[:, :, :, 1:2], ALU.add))
                pool.sem_inc(fb_gate, 1)
                pool.dma_start(yscan.rearrange("p b j t -> p (b j) t")[:, :, bass.ds(it * per, per)],
                               fb_y.rearrange("p b j t -> p (b j) t")).then_inc(fb_out, 16)
                pool.wait_ge(fb_out, 16 * (it + 1))
            pool.dma_start(yx[:, 0:B, :], yscan.rearrange("p b j t -> p b (j t)")).then_inc(fb_out, 16)
            pool.wait_ge(fb_out, 16 * (S // per + 1))

        @block.gpsimd
        def _(pool):
            count = [0]

            def link(ins):
                count[0] += 1
                ins.then_inc(pool_step, 1)
                pool.wait_ge(pool_step, count[0])

            def keep(ap, pattern, base, cm, op=ALU.is_ge, fill=0.0, out=None):
                link(pool.affine_select(out=out if out is not None else ap, in_=ap, pattern=pattern, compare_op=op,
                                        fill=fill, base=base, channel_multiplier=cm))
            link(pool.memset(xpad[:, :, 0:TAPS - 1], 0.0))
            link(pool.memset(ident[:, :], 0.0))
            keep(ident[:, :], [[-1, P]], 0, 1, ALU.not_equal, 1.0)
            link(pool.memset(ones[:, :], 1.0))
            keep(ones[:, :], [[1, P]], 0, -1, out=tri[:, :])
            keep(tri[:, :].rearrange("p (c t) -> p c t", t=CH), [[-CH, NC], [0, CH]], 0, 1,
                 out=tri32[:, :].rearrange("p (c t) -> p c t", t=CH))
            keep(ones[:, :].rearrange("p (c t) -> p c t", t=CH), [[CH, NC], [0, CH]], CH - 1, -1,
                 out=own[:, :].rearrange("p (c t) -> p c t", t=CH))
            for r in range(NC - 1):
                keep(ones[:, :], [[0, P]], CH * (r + 1) - 1, -1, out=upto[:, r * P:(r + 1) * P])
            keep(ones[:, 0:NC - 1], [[-CH, NC - 1]], 0, 1, out=mask_la[:, :])
            keep(mask_la[:, :], [[CH, NC - 1]], CH - 1, -1)
            keep(ones[:, 0:NC - 1], [[-CH, NC - 1]], -CH, 1, out=mask_ra[:, :])
            link(pool.memset(ones16[:, :], 1.0))
            keep(ones16[:, :], [[1, P]], 0, -1, ALU.is_gt, out=before16[:, :])
            link(pool.memset(never16[:, :], 0.0))
            keep(never16[:, :], [[-1, P]], 0, 1, ALU.not_equal, -1.0e30)
            link(pool.memset(neghalf, -0.5))
            link(pool.iota(eid[:, :], [[1, E]], base=0, channel_multiplier=0, allow_small_or_imprecise_dtypes=True))
            link(pool.iota(eoff[:, :], [[REGION, E]], base=0, channel_multiplier=0, allow_small_or_imprecise_dtypes=True))
            link(pool.iota(tokid[:, :], [[P, NT]], base=0, channel_multiplier=1, allow_small_or_imprecise_dtypes=True))
            link(pool.iota(steps128[:, :], [[P, NT]], base=0, channel_multiplier=0, allow_small_or_imprecise_dtypes=True))
            link(pool.iota(blkid[:, :], [[1, NB + 2]], base=0, channel_multiplier=0, allow_small_or_imprecise_dtypes=True))
            link(pool.memset(zero[:, :], 0.0))
            link(pool.memset(padrow[:, :], 0.0))
            link(pool.iota(padrow[:, D:D + 1], [[0, 1]], base=T, channel_multiplier=1, allow_small_or_imprecise_dtypes=True))
            link(pool.memset(padrow[:, D + 1:D + 2], -1.0))
            for t in (dtA, abar, vabs, la, ra, lb, rb, rc, wt):
                link(pool.memset(t, 0.0))
            pool.memset(picksum[:, 0, :], 0.0).then_inc(consts_done, 1)
            link(pool.memset(headneg[0][:, :], 0.0))
            for n in range(3):
                for b in range(B):
                    keep(headneg[max(n - 1, 0) if b == 0 else n][:, :], [[-1, H]], -(NSP * b + (2 - n) * H), 1, ALU.not_equal,
                         -1.0, out=headneg[n][:, :])

            pool.wait_ge(cumexp_done, 4)
            for t, other in ((rc, xdbl[:, :, NS:2 * NS]), (lb, bbar), (rb, xdbl[:, :, NS:2 * NS]), (wt, bbar)):
                pool.tensor_tensor(t[:, :, 0:NS], t[:, :, 0:NS], other, ALU.mult).then_inc(factors_done, 1)

            pool.wait_ge(guard_done, 1)
            pool.partition_all_reduce(guardall, guard, P, RMAX).then_inc(guard_red, 1)
            pool.wait_ge(bad_done, 1)
            with pool.If(pool.value_load(bad[0:1, 0:1], min_val=0, max_val=1) > 0):
                scan_step_by_step(pool)
            pool.sem_inc(scan_checked, 1)

            asked = [0]

            def rsqrt(n, at=0):
                asked[0] += 1
                pool.wait_ge(var_done, asked[0])
                pool.tensor_tensor(rsy[:, at:at + n], rsv[:, at:at + n], neghalf.to_broadcast([P, n]), ALU.pow).then_inc(rs_done, 1)

            for b in range(B):
                if b == B - 1:
                    pool.wait_ge(gated, NJ * B)
                    link(pool.memset(hs, 0.0))
                rsqrt(NQ)

            for item in (("laT", 0), ("laT", 1), ("raT", 0), ("raT", 1)):
                wait_filled(pool, item)
            wait_drained(pool, "cumD")
            pool.memset(vaug[:, :, :, DH:DV], 1.0).then_inc(vones_done, 1)
            pool.wait_ge(fac_done, 1)
            pool.wait_ge(ld_ctx, 16 * (1 + H))

            def weigh_keys(b):
                if b:
                    wait_filled(pool, ("H", b - 1))
                pairs = [(s, c) for c in range(1, NQ) for s in range(c)]
                for n, (s, c) in enumerate(pairs):
                    ins = pool.tensor_tensor(kw[:, n], vaug[:, NQ * b + s, :, 0:DH],
                                             bc(fac[:, NQ - 1 + n, b, :], 2, [P, H, DH]), ALU.mult)
                ins.then_inc(kw_done, 1)

            def head_weights(u):
                pool.wait_ge(heads_done, u + 1)
                first, n = UNITS[u]
                rows = hbuf[:, first % NQ:first % NQ + n].rearrange("p q h d -> p q (h d)")
                here = xtok[:, first:first + n, 0:D]
                link(pool.tensor_tensor(rows, rows, bc(onw[:, :], 1, [P, n, D]), ALU.mult))
                pool.tensor_tensor(here, here, rows, ALU.add).then_inc(resid_done, 1)

            def scatter(tiles, g):
                pool.wait_ge(row_done, g + 1)
                for i in tiles:
                    for k in range(2):
                        pool.indirect_dma_start(
                            out=slots, out_offset=bass.IndirectOffsetOnAxis(ap=pos[:, k, i:i + 1], axis=0),
                            in_=xtok[:, i, :], in_offset=None).then_inc(scattered, 16)

            weigh_keys(0)
            for i in range(NT):
                b, c = divmod(i, NQ)
                if b and c == 0:
                    rsqrt(NQ * H)
                if b and c == 1:
                    head_weights(b - 1)
                if b and c == 2:
                    rsqrt(NQ)
                if c == 0 and b + 1 < B:
                    weigh_keys(b + 1)
                if SPLIT_LO <= i < SPLIT_LO + WPARTS:
                    part = slice((i - SPLIT_LO) * WPART, (i - SPLIT_LO + 1) * WPART)
                    if i == SPLIT_LO:
                        pool.wait_ge(w_hi, 1)
                    pool.tensor_tensor(lo_of(slot_at[0])[:, part], wstage[:, part], hi_of(slot_at[0]).bitcast(F32)[:, part],
                                       ALU.subtract).then_inc(w_lo, 1)
                    if i == SPLIT_LO + WPARTS - 1:
                        pool.wait_ge(w_lo, WPARTS)
                        pool.sem_inc(w_ready, 1)
                if i == ROUTE_AT + 1:
                    scatter(range(NQ - 1), 0)
            u, late = B - 1, UNITS[B - 1][1]
            rsqrt(late * H)
            head_weights(u)
            rsqrt((NQ - late) * H, late * H)
            rsqrt(late)
            head_weights(u + 1)
            rsqrt(NQ - late, late)
            scatter(range(NQ - 1, 2 * NQ), 0)
            scatter(range(2 * NQ, 3 * NQ), 1)
            scatter(range(3 * NQ, NT), 2)
            pool.wait_ge(w_hi, 2)
            pool.tensor_tensor(lo_of(slot_at[1]), wstage, hi_of(slot_at[1]).bitcast(F32), ALU.subtract).then_inc(w_lo, 1)
            pool.wait_ge(events_done, 1)

            pool.wait_ge(w_lo, WPARTS + 1)
            e = pool.value_load(tab_ev[0:1, 1:2], min_val=1, max_val=E - 1)
            with pool.If(e > 1):
                pool.dma_start(wstage, w_exp[bass.ds(e, 1)].squeeze(0)).then_inc(w_again, 16)
                pool.wait_ge(w_again, 16)
                pool.tensor_tensor(hi_of(slot_at[1]), wstage, bc(zero[:, 0], 1, [P, WCOLS]), ALU.add).then_inc(w_step, 1)
                pool.wait_ge(w_step, 1)
                pool.tensor_tensor(lo_of(slot_at[1]), wstage, hi_of(slot_at[1]).bitcast(F32), ALU.subtract).then_inc(w_step, 1)
                pool.wait_ge(w_step, 2)
            pool.sem_inc(w_ready, 1)
            npair = pool.value_load(tab_n[0:1, 0:1], min_val=SURE, max_val=NB // 2)

            def event_of(g):
                return pool.value_load(tab_event[0:1, bass.ds(g, 1)], min_val=1, max_val=E - 1)

            def next_off(g):
                return pool.value_load(tab_noff[0:1, bass.ds(g, 1)], min_val=0, max_val=max(slot_at))

            def next_high(g):
                event, off = event_of(g), next_off(g)
                if not isinstance(g, int) or g:
                    pool.wait_ge(y_done, g)
                pool.wait_ge(w_loaded, 16 * event + 32)
                pool.sem_inc(pool_gate, 1)
                pool.tensor_tensor(hi_of(off)[:, ACT_PART:], wstage[:, ACT_PART:], bc(zero[:, 0], 1, [P, WCOLS - ACT_PART]),
                                   ALU.add).then_inc(w_rest, 1)

            def next_low(g, half):
                event, off = event_of(g), next_off(g)
                part = slice(half * WCOLS // 2, (half + 1) * WCOLS // 2)
                if half == 0:
                    pool.wait_ge(w_hi, event + 2)
                    pool.wait_ge(w_rest, event)
                    pool.sem_inc(pool_gate, 1)
                ins = pool.tensor_tensor(lo_of(off)[:, part], wstage[:, part], hi_of(off).bitcast(F32)[:, part], ALU.subtract)
                ins.then_inc(w_ready if half else w_lo, 1)

            def send_block(g, s):
                if isinstance(g, int):
                    if g:
                        pool.wait_ge(y_sent[0], 16 * g)
                else:
                    pool.wait_ge(y_sent[1 - s], 8 * (g + s))
                pool.wait_ge(yout_done, g + 1)
                pool.sem_inc(pool_gate, 1)
                pool.indirect_dma_start(out=yrows, out_offset=bass.IndirectOffsetOnAxis(ap=rid[:, s:s + 1], axis=0),
                                        in_=yout[:, s], in_offset=None).then_inc(y_sent[s], 16)

            def pair(p):
                for s in range(2):
                    g = 2 * p + s
                    start = isinstance(g, int) and g == 0
                    first = pool.value_load(tab_first[0:1, bass.ds(g, 1)], min_val=0, max_val=1)
                    if not start:
                        half_done = pool.value_load(tab_first[0:1, bass.ds(g - 1, 1)], min_val=0, max_val=1)
                    with pool.If(first > 0):
                        if not start:
                            with pool.If(half_done > 0):
                                next_low(g - 1, 1)
                        next_high(g)
                    send_block(g, s)
                    if not start:
                        with pool.If(first < 1):
                            with pool.If(half_done > 0):
                                next_low(g - 1, 1)
                    with pool.If(first > 0):
                        next_low(g, 0)
            pair(0)
            with pool.Fori(0, SURE - 1) as it:
                pair(it + 1)
            with pool.Fori(0, NB // 2 - SURE) as it:
                with pool.If(npair - it > SURE):
                    pair(it + SURE)
            def expert_rows(b):
                tiles = slice(NQ * b, NQ * (b + 1))
                pool.wait_ge(y_back[b], 32)
                pool.tensor_tensor(ya[:, tiles, :], ya[:, tiles, :], yb[:, tiles, :], ALU.add).then_inc(rows_added, 1)
            expert_rows(0)
            for b in range(B):
                if b + 1 < B:
                    expert_rows(b + 1)
                rsqrt(NQ, NQ * b)

        @block.scalar
        def _(act):
            def conv_in(n):
                wait_filled(act, ("xp", n))
                if n == 0:
                    act.wait_ge(pool_step, 1)
                if n >= 4:
                    act.wait_ge(conv_done, n - 3)
                drain(("xp", n), act.copy(xpad[:, n % 4, TAPS - 1:TAPS - 1 + S], ps(("xp", n))[:, :]))

            def gate_in(n):
                b, j = divmod(n, NJ)
                wait_filled(act, ("z", n))
                drain(("z", n), act.activation(zs[:, j, b * S:(b + 1) * S], ps(("z", n))[:, :], ACT.Silu))

            def conv_out(n):
                b, j = divmod(n, NJ)
                act.wait_ge(conv_done, n + 1)
                act.activation(xc[:, j, b * S:(b + 1) * S], cbuf[:, n % 2], ACT.Silu).then_inc(xc_done, 1)

            def by_tokens(b):
                for q in range(NQ):
                    i = NQ * b + q
                    wait_filled(act, ("xt", i))
                    drain(("xt", i), act.copy(xct(b, q), ps(("xt", i))[:, :]))
            for n in range(B * NJ):
                if n % NJ == 2 and n > NJ:
                    by_tokens(n // NJ - 1)
                conv_in(n)
                if n < GATES_LAST:
                    gate_in(n)
                if n:
                    conv_out(n - 1)
            for n in range(GATES_LAST, B * NJ):
                gate_in(n)
                if n == GATES_LAST + 1:
                    conv_out(B * NJ - 1)

            act.wait_ge(ld_small, 16 * 6)
            act.activation(aneg, alog[:, :], ACT.Exp).then_inc(exp_done, 1)
            act.wait_ge(vmin_done, 1)
            act.activation(expv, horner, ACT.Exp).then_inc(exp_done, 1)
            by_tokens(B - 1)
            act.wait_ge(dtA_done, 1)
            act.activation(abar[:, :, 0:NS], dtA[:, :, 0:NS], ACT.Exp).then_inc(exp_done, 1)
            act.wait_ge(cum_ready, 1)

            def cum(item, h):
                return ps(item)[:, h * 256:(h + 1) * 256].rearrange("p (i n) -> p i n", n=NS)
            act.activation(lb[:, :, 0:NS], cum("cumA", 0), ACT.Exp, scale=-1.0).then_inc(cumexp_done, 1)
            act.activation(rb[:, :, 0:NS], cum("cumA", 0), ACT.Exp).then_inc(cumexp_done, 1)
            act.activation(rc[:, :, 0:NS], cum("cumA", 1), ACT.Exp).then_inc(cumexp_done, 1)
            act.wait_ge(ediff_done, 1)
            act.activation(wt[:, :, 0:NS], wt[:, :, 0:NS], ACT.Exp).then_inc(cumexp_done, 1)
            act.activation(la[:, :, 3 * NS:4 * NS], la[:, :, 3 * NS:4 * NS], ACT.Exp).then_inc(cumexp_done, 1)
            act.activation(ediff, ediff, ACT.Exp).then_inc(cumexp_done, 1)
            wait_filled(act, "cumD")
            drain("cumD", act.activation(dec, ps("cumD")[:, 256:256 + NQ], ACT.Exp))
            for item, dst in (("gcT", gcT), ("lbT", lbT), ("rbT", rbT), ("abT", hst[:, 0]), (("laT", 0), laT[:, 0]),
                              (("laT", 1), laT[:, 1]), (("raT", 0), raT[:, 0]), (("raT", 1), raT[:, 1])):
                wait_filled(act, item)
                src = ps(item)[:, :]
                drain(item, act.copy(dst, src if item == "abT" else src.rearrange("p (q t) -> p q t", t=P)))
            act.wait_ge(scan_checked, 1)
            clipped = act.value_load(bad[0:1, 0:1], min_val=0, max_val=1)

            def scan_out(b):
                with act.If(clipped < 1):
                    for j in range(NJ):
                        wait_filled(act, ("y", b, j))
                        drain(("y", b, j), act.copy(ybuf(b, j), ps(("y", b, j))[:, :]))
                with act.If(clipped > 0):
                    for j in range(NJ):
                        wait_filled(act, ("y", b, j))
                        act.sem_inc(drained[place[("y", b, j)][0]], 1)

            def norm1_turned(b):
                for k in range(KD):
                    wait_filled(act, ("x1t", b, k))
                    drain(("x1t", b, k), act.copy(xcol[:, k, b * S:(b + 1) * S], ps(("x1t", b, k))[:, :]))
            for b in range(B + 2):
                if b < B:
                    scan_out(b)
                if b >= 2:
                    norm1_turned(b - 2)

            wait_filled(act, "gT")
            drain("gT", act.copy(gT, ps("gT")[:, :]))
            act.wait_ge(gabs_done, 1)
            act.activation(lfb, lfa, ACT.Exp, scale=-1.0).then_inc(act_step, 1)
            act.wait_ge(act_step, 1)
            act.activation(lfa, lfb, ACT.Ln, bias=1.0).then_inc(gexp_done, 1)
            wait_filled(act, "mT")
            drain("mT", act.copy(mS, ps("mT")[:, :].rearrange("p (q b n) -> p q b n", q=NQ, b=B)))
            act.wait_ge(args_done, 1)
            act.activation(fac, fac, ACT.Exp).then_inc(fac_done, 1)
            act.activation(emx, emx, ACT.Exp).then_inc(fac_done, 1)

            def states(b):
                wait_filled(act, ("H", b))
                for par in range(2):
                    r = slice(64 * par, 64 * par + 64)
                    ins = act.copy(hs[r, b % 2, :, :, par, :], ps(("H", b))[r, 0:(NQ - 1) * 2 * DV].rearrange(
                        "p (c h d) -> p c h d", c=NQ - 1, h=2))
                drain(("H", b), ins)

            def decays(i):
                wait_filled(act, ("nm", i))
                if i >= 2:
                    act.wait_ge(prob_done, 2 * (i - 1))
                for h in range(H):
                    ins = act.activation(decay[:, i % 2, h, :], ps(("nm", i))[:, h * P:(h + 1) * P], ACT.Exp,
                                         bias=av[:, i, h:h + 1])
                drain(("nm", i), ins)

            def norm2_turned(u):
                for o, tiles in enumerate(halves(u)):
                    wait_filled(act, ("x2t", u, o))
                    if u and o == 0:
                        wait_filled(act, ("lg", u - 1))
                    n, q = len(tiles), tiles[0] % NQ
                    drain(("x2t", u, o), act.copy(x2c[:, q:q + n], ps(("x2t", u, o))[:, 0:n * D].rearrange(
                        "p (q k t) -> p q k t", q=n, k=KD)))

            def router_exp(g):
                n = NQ * GROUPS[g][1]
                act.wait_ge(rexp_in, g + 1)
                act.activation(exp1[:, 0:n], exp1[:, 0:n], ACT.Exp).then_inc(rexp_done, 1)
                act.activation(exp2[:, 0:n], exp2[:, 0:n], ACT.Exp).then_inc(rexp_done, 1)
            decays(0)
            states(0)
            for i in range(NT):
                if i + 1 < NT:
                    decays(i + 1)
                    if (i + 1) % NQ == 0:
                        states((i + 1) // NQ)
                if i % NQ == 3 and i > NQ:
                    norm2_turned(i // NQ - 1)
                if i == ROUTE_AT:
                    router_exp(0)
                if SPLIT_HI <= i < SPLIT_HI + WPARTS:
                    if i == SPLIT_HI:
                        act.wait_ge(w_loaded, 16)
                    part = slice((i - SPLIT_HI) * WPART, (i - SPLIT_HI + 1) * WPART)
                    ins = act.copy(hi_of(slot_at[0])[:, part], wstage[:, part])
                    ins.then_inc(w_part if i < SPLIT_HI + WPARTS - 1 else w_hi, 1)
            for u in range(B - 1, len(UNITS)):
                norm2_turned(u)
            router_exp(1)
            router_exp(2)
            wait_filled(act, ("num", NT - 1))
            act.wait_ge(w_loaded, 32)
            act.copy(hi_of(slot_at[1]), wstage).then_inc(w_hi, 1)

            def slot_of(g):
                return act.value_load(tab_slot[0:1, bass.ds(g, 1)], min_val=0, max_val=E * REGION)

            def load_block(slot, s):
                act.dma_start(xg[:, s], slots[bass.ds(slot, P), :]).then_inc(xg_loaded[s], 16)

            def silu(g, u):
                act.wait_ge(up_done, 2 * g + (u + 1))
                act.activation(gsil[:, u], bank[2 * u][:, :], ACT.Silu).then_inc(sil_done, 1)

            def high_turned(g, u):
                act.wait_ge(turned, 2 * g + (u + 1))
                act.copy(hTh[:, u], bank[4 + u][:, :].rearrange("p (c t) -> p c t", t=P)).then_inc(hTh_done, 1)

            def pair(p):
                for s in range(2):
                    g = 2 * p + s
                    silu(g, 0)
                    if not isinstance(g, int) or g:
                        high_turned(g - 1, 1)
                    slot = slot_of(g + 2)
                    act.wait_ge(xg_turned, g + 1)
                    act.wait_ge(meta_done, g + 1)
                    load_block(slot, s)
                    silu(g, 1)
                    high_turned(g, 0)
                    with act.If(act.value_load(tab_first[0:1, bass.ds(g, 1)], min_val=0, max_val=1) > 0):
                        next_high(g)
            def next_high(g):
                event = act.value_load(tab_event[0:1, bass.ds(g, 1)], min_val=1, max_val=E - 1)
                off = act.value_load(tab_noff[0:1, bass.ds(g, 1)], min_val=0, max_val=max(slot_at))
                if not isinstance(g, int) or g:
                    act.wait_ge(y_done, g)
                act.wait_ge(w_loaded, 16 * event + 32)
                act.sem_inc(act_gate, 1)
                act.copy(hi_of(off)[:, 0:ACT_PART], wstage[:, 0:ACT_PART]).then_inc(w_hi, 1)
            act.wait_ge(tables_done, 1)
            slot = [slot_of(s) for s in range(2)]
            npair = act.value_load(tab_n[0:1, 0:1], min_val=SURE, max_val=NB // 2)
            act.wait_ge(scattered, 16 * 2 * NT)
            act.wait_ge(padded, 16 * (E + 1))
            for s in range(2):
                load_block(slot[s], s)
            act.wait_ge(events_done, 1)
            pair(0)
            with act.Fori(0, SURE - 1) as it:
                pair(it + 1)
            with act.Fori(0, NB // 2 - SURE) as it:
                with act.If(npair - it > SURE):
                    pair(it + SURE)
            last = (act.value_load(tab_n[0:1, 1:2], min_val=2 * SURE - 2, max_val=NB - 2) + 1)
            high_turned(last, 1)

            for b in range(B):
                act.wait_ge(shift_done, b + 1)
                for k in range(NQ):
                    n, row = NQ * b + k, xtok[:, NQ * b + k, 0:D]
                    ins = act.activation(row, row, ACT.Identity, bias=shift[:, n:n + 1], scale=rsy[:, n:n + 1])
                ins.then_inc(fin_done, 1)

        @block.vector
        def _(dve):
            count = [0]

            def link(ins):
                count[0] += 1
                ins.then_inc(dve_step, 1)
                dve.wait_ge(dve_step, count[0])

            def note(ins, s, value):
                ins.then_inc(s, 1)
                dve.wait_ge(s, value)

            def convolve(n):
                j = n % NJ
                src = xpad[:, n % 4]
                dst = cbuf[:, n % 2]
                wait_drained(dve, ("xp", n))
                if n >= 2:
                    dve.wait_ge(xc_done, n - 1)
                link(dve.tensor_scalar(dst, src[:, 0:S], convw[:, j, 0:1], convb[:, j:j + 1], ALU.mult, ALU.add))
                for k in range(1, TAPS - 1):
                    link(dve.scalar_tensor_tensor(dst, src[:, k:k + S], convw[:, j, k:k + 1], dst, ALU.mult, ALU.add))
                note(dve.scalar_tensor_tensor(dst, src[:, TAPS - 1:TAPS - 1 + S], convw[:, j, TAPS - 1:TAPS], dst,
                                              ALU.mult, ALU.add), conv_done, n + 1)

            def scan_inputs(b):
                wait_filled(dve, ("xd", b))
                drain(("xd", b), dve.tensor_copy(xdbl.rearrange("p (q b) n -> p b q n", b=B)[:, b],
                                                 ps(("xd", b))[:, 0:NQ * NX].rearrange("p (q n) -> p q n", n=NX)))

            def largest_input(b):
                for q in range(NQ):
                    wait_drained(dve, ("xt", NQ * b + q))
                    ins = dve.tensor_reduce(xmax[:, B * q + b:B * q + b + 1], xct(b, q), AX_X, ALU.max,
                                            apply_absolute_value=True)
                return ins
            dve.wait_ge(ld_conv, 16 * 3)
            for n in range(B * NJ):
                convolve(n)
                if n % NJ == 2 and n > NJ:
                    scan_inputs(n // NJ - 1)
                    link(largest_input(n // NJ - 1))
            dve.wait_ge(consts_done, 1)
            scan_inputs(B - 1)
            for b in range(B):
                wait_drained(dve, ("xd", b))
            note(dve.tensor_scalar(horner, xdbl[:, :, 2 * NS], -2.0, None, ALU.min), vmin_done, 1)
            dve.wait_ge(exp_done, 2)
            link(dve.tensor_scalar(aneg, aneg, -1.0, None, ALU.mult))
            link(dve.tensor_scalar(horner, expv, (-1.0) ** (HORNER + 1) / HORNER, None, ALU.mult))
            for k in range(HORNER - 1, 0, -1):
                link(dve.scalar_tensor_tensor(horner, horner, (-1.0) ** (k + 1) / k, expv, ALU.add, ALU.mult))
            link(dve.tensor_scalar(dtv, horner, DT_MIN, DT_MAX, ALU.max, ALU.min))
            full = [P, NT, NS]
            link(dve.tensor_tensor(dtA[:, :, 0:NS], bc(dtv, 2, full), bc(aneg, 1, full), ALU.mult))
            note(dve.tensor_scalar(dtA[:, :, 0:NS], dtA[:, :, 0:NS], -20.0, 0.0, ALU.max, ALU.min), dtA_done, 1)
            link(dve.tensor_tensor(bbar, xdbl[:, :, 0:NS], bc(dtv, 2, full), ALU.mult))
            link(dve.tensor_scalar(bbar, bbar, -10.0, 10.0, ALU.max, ALU.min))

            def cum(item, h):
                return ps(item)[:, h * 256:(h + 1) * 256].rearrange("p (i n) -> p i n", n=NS)
            cmat = xdbl[:, :, NS:2 * NS]
            wait_filled(dve, "cumA")
            link(dve.tensor_copy(cumt, cum("cumA", 1)))
            note(dve.tensor_reduce(guard[:, 1:2], ps("cumA")[:, 0:256], AX_X, ALU.min, negate=True), cum_ready, 1)
            wait_filled(dve, "cumB")
            for r in range(2):
                link(dve.tensor_tensor(ediff[:, r], cumt, cum("cumB", r), ALU.subtract))
            wait_filled(dve, "cumC")
            link(dve.tensor_tensor(ediff[:, 2], cumt, cum("cumC", 0), ALU.subtract))
            link(dve.tensor_scalar(ediff, ediff, 0.0, None, ALU.min))
            drain("cumC", dve.tensor_tensor(wt[:, :, 0:NS], cum("cumC", 1), cumt, ALU.subtract))
            wait_drained(dve, "cumC")
            wait_filled(dve, "cumD")
            note(dve.tensor_tensor(la[:, :, 3 * NS:4 * NS], cum("cumD", 0), cumt, ALU.subtract), ediff_done, 1)
            link(dve.scalar_tensor_tensor(vabs[:, :, 0:NS], bbar, -1.0, bbar, ALU.mult, ALU.max))
            link(largest_input(B - 1))
            note(dve.tensor_tensor(vabs[:, :, 0:NS], vabs[:, :, 0:NS], bc(xmax, 2, full), ALU.mult), guard_in, 1)
            dve.wait_ge(cumexp_done, 6)
            dve.sem_inc(drained[place["cumA"][0]], 1)
            dve.sem_inc(drained[place["cumB"][0]], 1)
            for r in range(NC - 1):
                link(dve.scalar_tensor_tensor(la[:, :, r * NS:(r + 1) * NS], la[:, :, 3 * NS:4 * NS], mask_la[:, r:r + 1],
                                              bbar, ALU.mult, ALU.mult))
                link(dve.scalar_tensor_tensor(ra[:, :, r * NS:(r + 1) * NS], ediff[:, r], mask_ra[:, r:r + 1],
                                              cmat, ALU.mult, ALU.mult))
            note(dve.memset(la[:, :, 3 * NS:4 * NS], 0.0), la_done, 1)
            wait_drained(dve, "abT")
            wait_filled(dve, "vbT")
            drain("vbT", dve.tensor_tensor_scan(hst[:, 1], hst[:, 0], ps("vbT")[:, :], 0.0, ALU.mult, ALU.add))
            wait_drained(dve, "vbT")
            note(dve.tensor_reduce(guard[:, 0:1], hst[:, 1], AX_X, ALU.max), guard_done, 1)
            dve.wait_ge(guard_red, 1)
            link(dve.tensor_scalar(guardall[:, 0:1], guardall[:, 0:1], STATE_LIMIT, None, ALU.is_lt))
            link(dve.scalar_tensor_tensor(guardall[:, 0:1], guardall[:, 1:2], DECAY_LIMIT, guardall[:, 0:1],
                                          ALU.is_lt, ALU.mult))
            note(dve.tensor_scalar(bad[:, :], guardall[:, 0:1], -1.0, 1.0, ALU.mult, ALU.add), bad_done, 1)
            wait_drained(dve, "cumD")
            for q in range(NQ - 1):
                wait_filled(dve, ("S", q))
                if q == 0:
                    ins = dve.tensor_copy(hst[:, 0], ps(("S", 0))[:, :])
                else:
                    ins = dve.scalar_tensor_tensor(hst[:, q], hst[:, q - 1], dec[:, q:q + 1], ps(("S", q))[:, :],
                                                   ALU.mult, ALU.add)
                drain(("S", q), ins)
                wait_drained(dve, ("S", q))
            dve.sem_inc(hst_done, 1)

            def mix(b):
                m1 = ps(("M1", b))[:, :].rearrange("p (q t) -> p q t", t=P)
                mt = mts[:, b % 2]
                wait_filled(dve, ("M1", b))
                if b >= 2:
                    wait_filled(dve, ("y", b - 2, NJ - 1))
                drain(("M1", b), dve.tensor_tensor(mt, m1, bc(tri32[:, :], 1, [P, NQ, P]), ALU.mult))
                wait_drained(dve, ("M1", b))
                wait_filled(dve, ("M2", b))
                drain(("M2", b), dve.tensor_tensor(mt, mt, ps(("M2", b))[:, :].rearrange("p (q t) -> p q t", t=P), ALU.add))

            def gate(b):
                for j in range(NJ):
                    part = slice(b * S, (b + 1) * S)
                    wait_drained(dve, ("y", b, j))
                    link(dve.tensor_tensor(zs[:, j, part], zs[:, j, part], ybuf(b, j), ALU.mult))
                    note(dve.scalar_tensor_tensor(zs[:, j, part], xc[:, j, part], dpar[:, j:j + 1], zs[:, j, part],
                                                  ALU.mult, ALU.add), gated, NJ * b + j + 1)

            asked = [0]

            def ask(var, add, at=0):
                asked[0] += 1
                n = var.shape[1]
                if isinstance(add, float):
                    ins = dve.tensor_scalar(rsv[:, at:at + n], var, add, None, ALU.add)
                else:
                    ins = dve.tensor_tensor(rsv[:, at:at + n], var, add, ALU.add)
                ins.then_inc(var_done, 1)
                return asked[0]

            def norm_stats(first, n, eps, at):
                for k in range(n):
                    ins = dve.bn_stats(stats[:, at + k, :], xtok[:, first + k, 0:D])
                link(ins)
                for k in range(n):
                    ins = dve.bn_aggr(mv[:, at + k, :], stats[:, at + k, :])
                link(ins)
                return ask(mv[:, at:at + n, 1], eps, at)

            def norm_apply(first, n, at, asked_as):
                dve.wait_ge(rs_done, asked_as)
                for k in range(n):
                    row = xtok[:, first + k, 0:D]
                    ins = dve.tensor_scalar(row, row, mv[:, at + k, 0:1], rsy[:, at + k:at + k + 1], ALU.subtract, ALU.mult)
                return ins

            def norm1(b):
                for o in range(2):
                    wait_filled(dve, ("o", b, o))
                    two = xtok[:, NQ * b + 2 * o:NQ * b + 2 * o + 2, 0:D]
                    drain(("o", b, o), dve.tensor_tensor(two, two, ps(("o", b, o))[:, :].rearrange("p (i d) -> p i d", d=D),
                                                         ALU.add))
                for o in range(2):
                    wait_drained(dve, ("o", b, o))
                note(norm_apply(NQ * b, NQ, 0, norm_stats(NQ * b, NQ, 1e-5, 0)), x1_done, b + 1)
            dve.wait_ge(ld_x, 32)
            dve.wait_ge(ld_small, 16 * 6)
            link(dve.memset(gkpad, 0.0))
            dve.tensor_copy(gkpad[:, 0:KD, 0:2 * H], gk[:, 0:KD])
            dve.tensor_tensor(gkpad[:, KD:, 0:2 * H], gk[:, KD:2 * KD], gk[:, 2 * KD:], ALU.add).then_inc(gk_done, 1)
            mix(0)
            for b in range(B + 1):
                if b + 1 < B:
                    mix(b + 1)
                if b < B:
                    gate(b)
                if b:
                    norm1(b - 1)

            wait_filled(dve, "g")
            drain("g", dve.tensor_tensor(gt.rearrange("p (b q) g -> p b q g", b=B),
                                         ps("g")[:, :].rearrange("p (q b n) -> p b q n", q=NQ, b=B)[:, :, :, 0:2 * H],
                                         gb[:, :].unsqueeze(1).unsqueeze(1).to_broadcast([P, B, NQ, 2 * H]), ALU.add))
            wait_drained(dve, "g")
            note(dve.scalar_tensor_tensor(lfa, gt[:, :, H:2 * H], -1.0, gt[:, :, H:2 * H], ALU.mult, ALU.max), gabs_done, 1)
            dve.memset(apad, 0.0)
            link(dve.memset(lfpre[:, :, 0, :], 0.0))
            dve.wait_ge(gexp_done, 1)
            link(dve.scalar_tensor_tensor(lfb, gt[:, :, H:2 * H], 0.0, lfa, ALU.min, ALU.subtract))
            lf4 = lfb.rearrange("p (b q) h -> p b q h", b=B)
            for q in range(1, NQ):
                link(dve.tensor_tensor(lfpre[:, :, q, :], lfpre[:, :, q - 1, :], lf4[:, :, q - 1, :], ALU.add))
            dve.sem_inc(lf_done, 1)
            wait_filled(dve, "cum")
            csum = ps("cum")[:, 0:NT * H].rearrange("p (i h) -> p i h", h=H)
            link(dve.tensor_tensor(av, gt[:, :, 0:H], csum, ALU.subtract))
            drain("cum", dve.tensor_copy(cumS, csum))
            note(dve.tensor_copy(apad[:, :, 0:3 * H].rearrange("p i (r h) -> p i r h", r=3), bc(av, 2, [P, NT, 3, H])), a_done, 1)
            wait_filled(dve, "aT")
            note(dve.tensor_tensor_scan(mrow, ps("aT")[:, :], zero[:, :].to_broadcast([P, S]), -BIG, ALU.max, ALU.add), mrow_done, 1)
            dve.sem_inc(drained[place["aT"][0]], 1)
            note(dve.tensor_tensor(zsel, bc(ident[:, :], 1, [P, NQ, P]), bc(mrow[:, P - 1:S:P], 2, [P, NQ, P]), ALU.mult),
                 z_done, 1)
            wait_drained(dve, "mT")
            wait_filled(dve, "R")
            rend = ps("R")[:, :].rearrange("p (q b n) -> p q b n", q=NQ, b=B)
            av4 = av.rearrange("p (b q) h -> p b q h", b=B)
            n = NQ - 1
            for c in range(1, NQ):
                link(dve.tensor_tensor(fac[:, c - 1], rend[:, c - 1, :, 0:H], mS[:, c, :, 0:H], ALU.subtract))
                for s in range(c):
                    ins = dve.tensor_tensor(fac[:, n], av4[:, :, s, :], rend[:, c - 1, :, 0:H], ALU.subtract)
                    n += 1
            drain("R", ins)
            wait_drained(dve, "R")
            wait_drained(dve, "cum")
            for q in range(NQ):
                cq = cumS.rearrange("p (b q) h -> p b q h", b=B)[:, :, q, :]
                ins = dve.scalar_tensor_tensor(emx.rearrange("p (b q) h -> p b q h", b=B)[:, :, q, :], cq, -1.0,
                                               mS[:, q, :, 0:H], ALU.mult, ALU.subtract)
            note(ins, args_done, 1)
            dve.tensor_reduce(lastpart[:, :], headneg[0][:, :], AX_X, ALU.add)
            link(dve.tensor_reduce(notfirst[:, :], headneg[1][:, :], AX_X, ALU.add))
            link(dve.tensor_copy(mpart, mrow))
            link(dve.scalar_tensor_tensor(mrest, mpart, notfirst[:, 0:1], mrow, ALU.mult, ALU.add))
            link(dve.tensor_copy(mpart, mrest))
            link(dve.scalar_tensor_tensor(mrest, mpart, lastpart[:, 0:1], mrest, ALU.mult, ALU.add))
            for q in range(NQ):
                dve.tensor_tensor(mneg[:, q], bc(mrest[:, q * P:(q + 1) * P], 1, [P, H, P]),
                                  bc(headneg[2][:, :], 2, [P, H, P]), ALU.mult).then_inc(mneg_done, 1)
            dve.wait_ge(fac_done, 2)
            link(dve.tensor_scalar(fac[:, 0:NQ - 1], fac[:, 0:NQ - 1], DH ** -0.5, None, ALU.mult))

            def weights(i):
                b, c = divmod(i, NQ)
                wait_drained(dve, ("nm", i))
                if i >= 2:
                    wait_filled(dve, ("num", i - 2))
                for par, item in ((0, ("sA", i)), (1, ("sB", i))):
                    wait_filled(dve, item)
                    sc = ps(item)[:, 0:2 * P].rearrange("p (h s) -> p h s", h=2)
                    ins = dve.scalar_tensor_tensor(prob[:, i % 2, par::2, :], sc, DH ** -0.5, decay[:, i % 2, par::2, :],
                                                   ALU.mult, ALU.mult)
                    ins.then_inc(prob_done, 1)
                    if c:
                        st = ps(item)[:, 2 * P:2 * P + 2 * DV].rearrange("p (h d) -> p h d", h=2)
                        two = slice(2 * par, 2 * par + 2)
                        ins = dve.tensor_tensor(tot[:, b % 2, c, two, :], st, bc(fac[:, c - 1, b, two], 2, [P, 2, DV]), ALU.mult)
                        drain(item, ins)
                    else:
                        dve.wait_ge(prob_done, 2 * i + par + 1)
                        dve.sem_inc(drained[place[item][0]], 1)

            def sums_of(i):
                b, c = divmod(i, NQ)
                tt = tot[:, b % 2, c]
                wait_filled(dve, ("num", i))
                num = ps(("num", i))[:, 0:H * DV].rearrange("p (h d) -> p h d", h=H)
                if c:
                    wait_drained(dve, ("sA", i))
                    wait_drained(dve, ("sB", i))
                    drain(("num", i), dve.tensor_tensor(tt, tt, num, ALU.add))
                else:
                    drain(("num", i), dve.tensor_copy(tt, num))

            head_asked, norm2_asked = {}, {}

            def head_stats(u):
                first, n = UNITS[u]
                q0 = first % NQ
                tt, dn = tot[:, first // NQ % 2, q0:q0 + n], den[:, q0:q0 + n]
                heads = range(q0 * H, (q0 + n) * H)
                for i in range(first, first + n):
                    wait_drained(dve, ("num", i))
                link(dve.scalar_tensor_tensor(dn, tt[:, :, :, DH], -1.0, tt[:, :, :, DH], ALU.mult, ALU.max))
                link(dve.tensor_tensor(dn, dn, emx[:, first:first + n, :], ALU.max))
                link(dve.tensor_scalar(dn, dn, 1e-6, None, ALU.add))
                dve.scalar_tensor_tensor(dn, dn, 1e-6, dn, ALU.mult, ALU.mult)
                for m in heads:
                    ins = dve.bn_stats(stats[:, m, :], tt[:, m // H - q0, m % H, 0:DH])
                link(ins)
                for m in heads:
                    ins = dve.bn_aggr(mv[:, m, :], stats[:, m, :])
                link(ins)
                part = slice(heads[0], heads[-1] + 1)
                head_asked[u] = ask(mv[:, part, 1], dn.rearrange("p q h -> p (q h)"), part.start)

            def head_apply(u):
                first, n = UNITS[u]
                q0 = first % NQ
                part, full = slice(q0 * H, (q0 + n) * H), [P, n * H, DH]
                tt = tot[:, first // NQ % 2, q0:q0 + n].rearrange("p q h d -> p (q h) d")[:, :, 0:DH]
                heads = hbuf[:, q0:q0 + n].rearrange("p q h d -> p (q h) d")
                link(dve.tensor_tensor(heads, tt, bc(mv[:, part, 0], 2, full), ALU.subtract))
                dve.wait_ge(rs_done, head_asked[u])
                dve.tensor_tensor(heads, heads, bc(rsy[:, part], 2, full), ALU.mult).then_inc(heads_done, 1)

            def norm2_stats(u):
                first, n = UNITS[u]
                dve.wait_ge(resid_done, u + 1)
                norm2_asked[u] = norm_stats(first, n, 1e-5, first % NQ)

            def norm2_apply(u):
                first, n = UNITS[u]
                note(norm_apply(first, n, first % NQ, norm2_asked[u]), x2_done, u + 1)

            def take_logits(u):
                first, n = UNITS[u]
                wait_filled(dve, ("lg", u))
                drain(("lg", u), dve.tensor_copy(lgs[:, first:first + n, :], ps(("lg", u))[:, 0:n * E].rearrange(
                    "p (q e) -> p q e", e=E)))

            def pick(dst, chosen, values, top):
                n = values.shape[1]
                full = [P, n, E]
                link(dve.tensor_reduce(top, values, AX_X, ALU.max))
                link(dve.tensor_tensor(cand[:, 0:n], values, bc(top, 2, full), ALU.not_equal))
                link(dve.scalar_tensor_tensor(cand[:, 0:n], cand[:, 0:n], float(E), bc(eid[:, :], 1, full), ALU.mult, ALU.add))
                link(dve.tensor_reduce(chosen, cand[:, 0:n], AX_X, ALU.min))
                link(dve.tensor_tensor(dst, bc(chosen, 2, full), bc(eid[:, :], 1, full), ALU.is_equal))

            def route_choose(g):
                first, n = GROUPS[g][0] * NQ, GROUPS[g][1] * NQ
                full, tiles = [P, n, E], slice(first, first + n)
                lg, l2, o1, o2, ab = lgs[:, tiles], lg2[:, 0:n], oh1[:, 0:n], oh2[:, 0:n], labs[:, 0:n]
                for u, (i, _) in enumerate(UNITS):
                    if first <= i < first + n:
                        wait_drained(dve, ("lg", u))
                dve.scalar_tensor_tensor(ab, lg, -1.0, lg, ALU.mult, ALU.max)
                pick(o1, sums[:, 0, 0:n], lg, top1[:, 0:n])
                dve.tensor_copy(xtok[:, tiles, D + 1], sums[:, 0, 0:n])
                link(dve.scalar_tensor_tensor(l2, o1, -BIG, lg, ALU.mult, ALU.add))
                pick(o2, sums[:, 1, 0:n], l2, top2[:, 0:n])
                link(dve.tensor_tensor(picks[:, tiles, :], o1, o2, ALU.add))
                for i in range(first, first + n):
                    ins = dve.tensor_tensor(picksum[:, i + 1, :], picksum[:, i, :], picks[:, i, :], ALU.add)
                    if i + 1 < first + n:
                        link(ins)
                note(ins, picks_done, g + 1)
                for top, dst, base in ((top1, exp1, lg), (top2, exp2, l2)):
                    tb, dst, far = bc(top[:, 0:n], 2, full), dst[:, 0:n], cand[:, 0:n]
                    dve.tensor_tensor(dst, tb, lg, ALU.subtract)
                    link(dve.tensor_tensor(far, ab, tb, ALU.max))
                    link(dve.scalar_tensor_tensor(far, far, JITTER2, dst, ALU.mult, ALU.is_lt))
                    link(dve.tensor_tensor(dst, base, tb, ALU.subtract))
                    link(dve.scalar_tensor_tensor(dst, far, -1.0e30, dst, ALU.mult, ALU.add))
                dve.sem_inc(rexp_in, 1)

            def route_place(g):
                first, n = GROUPS[g][0] * NQ, GROUPS[g][1] * NQ
                full, tiles = [P, n, E], slice(first, first + n)
                wait_filled(dve, ("rk", g))
                rank = ps(("rk", g))[:, 0:n * E].rearrange("p (q e) -> p q e", e=E)
                drain(("rk", g), dve.tensor_tensor(slotf[:, 0:n], rank, bc(eoff[:, :], 1, full), ALU.add))
                wait_drained(dve, ("rk", g))
                dve.tensor_tensor(lg2[:, 0:n], oh1[:, 0:n], slotf[:, 0:n], ALU.mult)
                link(dve.tensor_tensor(cand[:, 0:n], oh2[:, 0:n], slotf[:, 0:n], ALU.mult))
                dve.tensor_reduce(posf[:, 0, 0:n], lg2[:, 0:n], AX_X, ALU.add)
                link(dve.tensor_reduce(posf[:, 1, 0:n], cand[:, 0:n], AX_X, ALU.add))
                dve.tensor_copy(pos[:, :, tiles], posf[:, :, 0:n])
                dve.wait_ge(rexp_done, 2 * (g + 1))
                dve.tensor_reduce(sums[:, 0, 0:n], exp1[:, 0:n], AX_X, ALU.add)
                link(dve.tensor_reduce(sums[:, 1, 0:n], exp2[:, 0:n], AX_X, ALU.add))
                link(dve.reciprocal(sums[:, :, 0:n], sums[:, :, 0:n]))
                dve.tensor_copy(xtok[:, tiles, D + 2], sums[:, 0, 0:n])
                dve.tensor_copy(xtok[:, tiles, D + 3], sums[:, 1, 0:n])
                note(dve.tensor_copy(xtok[:, tiles, D], tokid[:, tiles]), row_done, g + 1)

            dve.wait_ge(consts_done, 1)
            for i in range(NT):
                b, c = divmod(i, NQ)
                weights(i)
                if b and c == 0:
                    head_stats(b - 1)
                    if b >= 2:
                        take_logits(b - 2)
                if b and c == 1:
                    head_apply(b - 1)
                if b and c == 2:
                    norm2_stats(b - 1)
                if i == ROUTE_AT:
                    route_choose(0)
                if i == ROUTE_AT + 1:
                    route_place(0)
                if i == NT - 1:
                    head_stats(B - 1)
                    head_apply(B - 1)
                sums_of(i)
                if b and c == 2:
                    norm2_apply(b - 1)
            head_stats(B)
            norm2_stats(B - 1)
            take_logits(B - 2)
            head_apply(B)
            norm2_apply(B - 1)
            norm2_stats(B)
            norm2_apply(B)
            take_logits(B - 1)
            route_choose(1)
            take_logits(B)
            route_place(1)
            route_choose(2)
            route_place(2)

            wait_filled(dve, "cnt")
            drain("cnt", dve.tensor_copy(cnt[:, :], ps("cnt")[:, 0:E]))
            wait_drained(dve, "cnt")
            dve.tensor_tensor(cmp16, bc(cnt[:, :], 2, [P, E, NT]), bc(steps128[:, :], 1, [P, E, NT]), ALU.is_gt)
            dve.memset(ringf[:, 0:E], 0.0)
            link(dve.tensor_tensor(ringg[:, 0:E], cnt[:, :], eoff[:, :], ALU.add))
            dve.tensor_copy(tab_pad[:, :], ringg[:, 0:E]).then_inc(pads_known, 1)
            link(dve.tensor_reduce(nblk[:, :], cmp16, AX_X, ALU.add))
            link(dve.tensor_tensor_scan(endblk[:, :], nblk[:, :], ringf[:, 0:E], 0.0, ALU.add, ALU.add))
            full = [P, NB + 2, E]
            link(dve.tensor_tensor(cmpb, bc(blkid[:, :], 2, full), bc(endblk[:, :], 1, full), ALU.is_ge))
            link(dve.tensor_reduce(eblk[:, :], cmpb, AX_X, ALU.add))
            link(dve.tensor_scalar(hasblk[:, :], nblk[:, :], 0.0, None, ALU.is_gt))
            link(dve.memset(hasblk[:, 0:1], 1.0))
            link(dve.tensor_tensor_scan(cumev[:, :], hasblk[:, :], ringf[:, 0:E], 0.0, ALU.add, ALU.add))
            full2 = [P, NB, E]
            cmp2 = cmpb[:, 0:NB, :]
            link(dve.tensor_tensor(cmpb, cmpb, bc(nblk[:, :], 1, full), ALU.mult))
            link(dve.tensor_reduce(sblk[:, :], cmpb, AX_X, ALU.add))
            link(dve.tensor_tensor(cmp2, bc(blkid[:, 0:NB], 2, full2), bc(endblk[:, :], 1, full2), ALU.is_ge))
            link(dve.tensor_tensor(cmp2, cmp2, bc(hasblk[:, :], 1, full2), ALU.mult))
            link(dve.tensor_reduce(evblk[:, :], cmp2, AX_X, ALU.add))
            link(dve.tensor_scalar(ringg[:, 0:1], cumev[:, E - 1:E], -1.0, None, ALU.add))
            link(dve.tensor_scalar(evblk[:, :], evblk[:, :], ringg[:, 0:1], None, ALU.min))
            link(dve.tensor_tensor(sblk[:, :], blkid[:, :], sblk[:, :], ALU.subtract))
            link(dve.tensor_scalar(ringf[:, :], eblk[:, :], float(REGION), None, ALU.mult))
            link(dve.scalar_tensor_tensor(sblk[:, :], sblk[:, :], float(P), ringf[:, :], ALU.mult, ALU.add))
            link(dve.tensor_scalar(sblk[:, :], sblk[:, :], float(E * REGION), None, ALU.min))
            link(dve.tensor_copy(tab_slot[:, :], sblk[:, :]))
            link(dve.tensor_copy(ringf[:, 0:1], evblk[:, 0:1]))
            link(dve.tensor_tensor(ringf[:, 1:NB], evblk[:, 1:NB], evblk[:, 0:NB - 1], ALU.subtract))
            link(dve.scalar_tensor_tensor(ringf[:, 0:NB], evblk[:, :], ringg[:, 0:1], ringf[:, 0:NB], ALU.is_lt, ALU.mult))
            link(dve.tensor_copy(tab_first[:, :], ringf[:, 0:NB]))
            link(dve.tensor_copy(tab_event[:, :], evblk[:, :]))
            link(dve.tensor_scalar(ringf[:, 0:NB // 2], blkid[:, 0:NB:2], endblk[:, E - 1:E], None, ALU.is_lt))
            link(dve.tensor_reduce(ringg[:, 0:1], ringf[:, 0:NB // 2], AX_X, ALU.add))
            link(dve.tensor_scalar(ringg[:, 1:2], ringg[:, 0:1], 2.0, -2.0, ALU.mult, ALU.add))
            link(dve.tensor_copy(ringg[:, 2:3], cumev[:, E - 1:E]))
            note(dve.tensor_copy(tab_n[:, :], ringg[:, 0:3]), tables_done, 1)
            link(dve.tensor_scalar(ringf[:, 0:NB], evblk[:, :], 1.0, None, ALU.is_ge))
            for v in range(2, E):
                link(dve.scalar_tensor_tensor(ringf[:, 0:NB], evblk[:, :], float(v), ringf[:, 0:NB], ALU.is_ge,
                                              ALU.subtract))
            link(dve.tensor_tensor(ringf[:, 0:NB], ringf[:, 0:NB], ringf[:, 0:NB], ALU.mult))
            link(dve.tensor_scalar(ringg[:, :], ringf[:, 0:NB], float(slot_at[0] - slot_at[1]), float(slot_at[1]),
                                   ALU.mult, ALU.add))
            link(dve.tensor_copy(tab_noff[:, :], ringg[:, :]))
            full = [P, E + 2, E]
            cmp2 = cmpb[:, 0:E + 2, :]
            link(dve.tensor_tensor(cmp2, bc(blkid[:, 0:E + 2], 2, full), bc(cumev[:, :], 1, full), ALU.is_ge))
            link(dve.tensor_reduce(ringf[:, 0:E + 2], cmp2, AX_X, ALU.add))
            link(dve.tensor_scalar(ringf[:, 0:E + 2], ringf[:, 0:E + 2], float(E - 1), None, ALU.min))
            note(dve.tensor_copy(tab_ev[:, :], ringf[:, 0:E + 2]), events_done, 1)

            def row_meta(g, s):
                m = meta[:, s]
                first, a, b_ = m[:, 0:1], m[:, 1:2], m[:, 2:3]
                done = [g * 5]

                def chain(ins):
                    done[0] = done[0] + 1
                    ins.then_inc(meta_step, 1)
                    dve.wait_ge(meta_step, done[0])
                dve.wait_ge(xg_loaded[s], 16 * (g // 2 + 1) if isinstance(g, int) else 8 * (g - s) + 16)
                chain(dve.tensor_tensor(first, xg[:, s, D + 1:D + 2], eblk[:, bass.ds(g, 1)], ALU.is_equal))
                chain(dve.tensor_tensor(a, xg[:, s, D + 2:D + 3], first, ALU.mult))
                chain(dve.tensor_scalar(b_, first, -1.0, 1.0, ALU.mult, ALU.add))
                chain(dve.scalar_tensor_tensor(m[:, 3:4], b_, float(T), xg[:, s, D:D + 1], ALU.mult, ALU.add))
                chain(dve.tensor_tensor(b_, b_, xg[:, s, D + 3:D + 4], ALU.mult))
                dve.tensor_tensor(m[:, 4:5], a, b_, ALU.add).then_inc(meta_done, 1)

            def rows(g, s):
                src = bank[7][:, 0:D].rearrange("p (k t) -> p k t", k=KD)
                dve.wait_ge(xg_turned, g + 1)
                dve.tensor_copy(xTh[:, s], src).then_inc(xgh_done, 1)
                dve.wait_ge(xgh_done, g + 1)
                dve.tensor_tensor(xTl[:, s], src, xTh[:, s].bitcast(F32), ALU.subtract).then_inc(xgT_done, 1)

            def middle(g, u):
                dve.wait_ge(sil_done, 2 * g + (u + 1))
                dve.tensor_tensor(hmid[:, u], gsil[:, u], bank[2 * u + 1][:, :], ALU.mult).then_inc(mid_done, 1)

            def low_turned(g, u):
                dve.wait_ge(hTh_done, 2 * g + (u + 1))
                dve.tensor_tensor(hTl[:, u], bank[4 + u][:, :].rearrange("p (c t) -> p c t", t=P), hTh[:, u].bitcast(F32),
                                  ALU.subtract).then_inc(hTl_done, 1)

            def weigh(g, s):
                dve.wait_ge(meta_done, g + 1)
                if not isinstance(g, int) or g >= 2:
                    dve.wait_ge(y_sent[s], 8 * (g - s))
                dve.tensor_copy(rid[:, s:s + 1], meta[:, s, 3:4]).then_inc(rid_done, 1)
                dve.wait_ge(rid_done, g + 1)
                dve.wait_ge(y_done, g + 1)
                dve.tensor_scalar(yout[:, s], bank[6][:, 0:D], meta[:, s, 4:5], None, ALU.mult).then_inc(yout_done, 1)

            def pair(p):
                for s in range(2):
                    g = 2 * p + s
                    middle(g, 0)
                    if not isinstance(g, int) or g:
                        low_turned(g - 1, 1)
                    rows(g + 1, 1 - s)
                    middle(g, 1)
                    low_turned(g, 0)
                    if not isinstance(g, int) or g:
                        weigh(g - 1, 1 - s)
                    row_meta(g + 1, 1 - s)
            npair = dve.value_load(tab_n[0:1, 0:1], min_val=SURE, max_val=NB // 2)
            row_meta(0, 0)
            rows(0, 0)
            pair(0)
            with dve.Fori(0, SURE - 1) as it:
                pair(it + 1)
            with dve.Fori(0, NB // 2 - SURE) as it:
                with dve.If(npair - it > SURE):
                    pair(it + SURE)
            last = dve.value_load(tab_n[0:1, 1:2], min_val=2 * SURE - 2, max_val=NB - 2) + 1
            low_turned(last, 1)
            weigh(last, 1)

            dve.wait_ge(scattered, 16 * 2 * NT)
            for b in range(B + 1):
                if b < B:
                    tiles = slice(NQ * b, NQ * (b + 1))
                    dve.wait_ge(rows_added, b + 1)
                    link(dve.tensor_tensor(xtok[:, tiles, 0:D], xtok[:, tiles, 0:D], ya[:, tiles, :], ALU.add))
                    norm_stats(NQ * b, NQ, 1e-5, NQ * b)
                if b:
                    n = slice(NQ * (b - 1), NQ * b)
                    dve.wait_ge(rs_done, asked[0] - (1 if b < B else 0))
                    dve.scalar_tensor_tensor(shift[:, n], mv[:, n, 0], -1.0, rsy[:, n], ALU.mult, ALU.mult).then_inc(shift_done, 1)

        @block.tensor
        def _(pe):
            def claim(item):
                k, n = place[item]
                if n:
                    pe.wait_ge(drained[k], n)
                return bank[k]

            def fill(item, ins):
                ins.then_inc(filled[place[item][0]], 1)

            def project(kind, n):
                b, j = divmod(n, NJ)
                o = claim((kind, n))
                col = (0 if kind == "xp" else DI) + j * P
                for k in range(KD):
                    mm = pe.matmul(o[:, :], winT[:, k, col:col + P], xcol[:, k, b * S:(b + 1) * S],
                                   start=(k == 0), stop=(k == KD - 1))
                fill((kind, n), mm)

            def scan_inputs(b):
                pe.wait_ge(xc_done, NJ * (b + 1))
                o = claim(("xd", b))
                for q in range(NQ):
                    t = b * S + q * P
                    for j in range(NJ):
                        mm = pe.matmul(o[:, q * NX:(q + 1) * NX], xc[:, j, t:t + P], wxT[:, j, :],
                                       start=(j == 0), stop=(j == NJ - 1))
                fill(("xd", b), mm)
                for q in range(NQ):
                    i = NQ * b + q
                    o = claim(("xt", i))
                    for j in range(NJ):
                        mm = pe.transpose(o[:, j * P:(j + 1) * P], xc[:, j, i * P:(i + 1) * P], ident[:, :])
                    fill(("xt", i), mm)
            pe.wait_ge(ld_win[0], 16)
            for n in range(B * NJ):
                if n % NJ == 0:
                    pe.wait_ge(ld_xT[n // NJ], 16)
                project("xp", n)
                if n == 0:
                    pe.wait_ge(ld_win[1], 16)
                if n < GATES_LAST:
                    project("z", n)
                if n % NJ == 1 and n > NJ:
                    if n < 2 * NJ:
                        pe.wait_ge(consts_done, 1)
                        pe.wait_ge(ld_conv, 16 * 3)
                    scan_inputs(n // NJ - 1)
            for n in range(GATES_LAST, B * NJ):
                project("z", n)
            scan_inputs(B - 1)

            pe.wait_ge(dtA_done, 1)

            def total(item, h, left, last=False):
                mm = pe.matmul(ps(item)[:, h * 256:(h + 1) * 256], left, dtA[:, :, 0:NS], start=True, stop=True)
                if last:
                    fill(item, mm)
            claim("cumA")
            total("cumA", 0, tri32[:, :])
            total("cumA", 1, tri[:, :], True)
            claim("cumB")
            total("cumB", 0, upto[:, 0:P])
            total("cumB", 1, upto[:, P:2 * P], True)
            claim("cumC")
            total("cumC", 0, upto[:, 2 * P:3 * P])
            total("cumC", 1, ones[:, :], True)
            claim("cumD")
            total("cumD", 0, own[:, :])

            def same_place(t, q):
                return t[:, B * q:B * (q + 1), :].rearrange("p b n -> p (b n)")
            for q in range(NQ):
                mm = pe.matmul(ps("cumD")[:, 256 + q:257 + q], same_place(dtA, q), ones[:, 0:1], start=True, stop=True)
            fill("cumD", mm)

            def turn4(item, src):
                o = claim(item)
                for q in range(NQ):
                    mm = pe.transpose(o[:, q * P:(q + 1) * P], src(q), ident[:, :])
                fill(item, mm)
            for n, (item, src) in enumerate((("gcT", rc), ("lbT", lb), ("rbT", rb))):
                pe.wait_ge(factors_done, n + 1)
                turn4(item, lambda q: same_place(src, q))
            pe.wait_ge(exp_done, 3)
            pe.wait_ge(guard_in, 1)
            turn4("abT", lambda q: same_place(abar, q))
            turn4("vbT", lambda q: same_place(vabs, q))
            pe.wait_ge(factors_done, 4)
            for q in range(NQ - 1):
                o = claim(("S", q))
                for b in range(B):
                    mm = pe.matmul(o[NSP * b:NSP * (b + 1), :], wt[:, B * q + b, :], xct(b, q), start=True, stop=True)
                fill(("S", q), mm)
            pe.wait_ge(la_done, 1)
            for name, src in (("laT", la), ("raT", ra)):
                for g in range(2):
                    turn4((name, g), lambda q: src[:, B * q + 2 * g:B * q + 2 * g + 2, :].rearrange("p b n -> p (b n)"))
            for item in ("gcT", "lbT", "rbT", ("laT", 0), ("laT", 1), ("raT", 0), ("raT", 1)):
                wait_drained(pe, item)

            def mixes(b):
                o = claim(("M1", b))
                r = slice(NSP * b, NSP * (b + 1))
                for q in range(NQ):
                    mm = pe.matmul(o[:, q * P:(q + 1) * P], lbT[r, q, :], rbT[r, q, :], start=True, stop=True)
                fill(("M1", b), mm)
                o = claim(("M2", b))
                r = slice(64 * (b % 2), 64 * (b % 2) + 64)
                for q in range(NQ):
                    mm = pe.matmul(o[:, q * P:(q + 1) * P], laT[r, b // 2, q, :], raT[r, b // 2, q, :], start=True, stop=True)
                fill(("M2", b), mm)

            def outputs(b):
                wait_drained(pe, ("M2", b))
                r = slice(NSP * b, NSP * (b + 1))
                for j in range(NJ):
                    o = claim(("y", b, j))
                    for q in range(NQ):
                        part = o[:, q * P:(q + 1) * P]
                        mm = pe.matmul(part, xct(b, q)[:, j * P:(j + 1) * P], mts[:, b % 2, q, :], start=True, stop=(q == 0))
                        if q:
                            mm = pe.matmul(part, hst[r, q - 1, j * P:(j + 1) * P], gcT[r, q, :], start=False, stop=True)
                    fill(("y", b, j), mm)
            def out_project(b):
                pe.wait_ge(gated, NJ * (b + 1))
                if b == 0:
                    pe.wait_ge(ld_x, 32)
                for o2 in range(2):
                    o = claim(("o", b, o2))
                    for q in range(2):
                        t = (NQ * b + 2 * o2 + q) * P
                        for j in range(NJ):
                            mm = pe.matmul(o[:, q * D:(q + 1) * D], zs[:, j, t:t + P], woutT[:, j, :],
                                           start=(j == 0), stop=(j == NJ - 1))
                    fill(("o", b, o2), mm)

            def turn_norm1(b):
                pe.wait_ge(x1_done, b + 1)
                for k in range(KD):
                    o = claim(("x1t", b, k))
                    for q in range(NQ):
                        mm = pe.transpose(o[:, q * P:(q + 1) * P], xtok[:, NQ * b + q, k * P:(k + 1) * P], ident[:, :])
                    fill(("x1t", b, k), mm)
            def gates(b):
                for k in range(KD):
                    wait_drained(pe, ("x1t", b, k))
                if b == 0:
                    pe.wait_ge(ld_ctx, 16 * (1 + H))
                    pe.wait_ge(gk_done, 1)
                    claim("gT")
                for n in range(2 * KD):
                    src = (xcol, ctxc)[n // KD]
                    mm = pe.matmul(ps("gT")[NSP * b:NSP * (b + 1), :], gkpad[:, n, :], src[:, n % KD, b * S:(b + 1) * S],
                                   start=(n == 0), stop=(n == 2 * KD - 1))
                if b == B - 1:
                    fill("gT", mm)
            mixes(0)
            for b in range(B + 2):
                if b + 1 < B:
                    mixes(b + 1)
                if b == 0:
                    pe.wait_ge(hst_done, 1)
                    pe.wait_ge(scan_checked, 1)
                if b < B:
                    outputs(b)
                if 1 <= b <= B:
                    out_project(b - 1)
                if b >= 2:
                    turn_norm1(b - 2)
                    gates(b - 2)

            wait_drained(pe, "gT")
            turn4("g", lambda q: gT[:, q * P:(q + 1) * P])
            pe.wait_ge(lf_done, 1)
            o = claim("cum")
            pe.matmul(o[:, 0:NT * H], tri[:, :], lfb, start=True, stop=False)
            fill("cum", pe.matmul(o[:, 0:NT * H], ones[:, :], lfpre, start=False, stop=True))
            pe.wait_ge(a_done, 1)
            o = claim("aT")
            for i in range(NT):
                b, q = divmod(i, NQ)
                mm = pe.matmul(o[NSP * b:NSP * (b + 1), q * P:(q + 1) * P], apad[:, i, :], ident[:, :], start=True, stop=True)
            fill("aT", mm)
            pe.wait_ge(mrow_done, 1)
            o = claim("mT")
            for q in range(NQ):
                mm = pe.transpose(o[:, q * P:(q + 1) * P], mrow[:, q * P:(q + 1) * P], ident[:, :])
            fill("mT", mm)
            pe.wait_ge(z_done, 1)
            o = claim("R")
            fill("R", pe.matmul(o[:, :], ones[:, :], zsel, start=True, stop=True))

            def states(b):
                pe.wait_ge(kw_done, b + 1)
                pe.wait_ge(vones_done, 1)
                o = claim(("H", b))
                n = 0
                for c in range(1, NQ):
                    for h in range(H):
                        r = slice(64 * (h % 2), 64 * (h % 2) + 64)
                        col = ((c - 1) * 2 + h // 2) * DV
                        for s in range(c):
                            mm = pe.matmul(o[r, col:col + DV], kw[:, n + s, h, :], vaug[:, NQ * b + s, h, :],
                                           start=(s == 0), stop=(s == c - 1))
                    n += c
                fill(("H", b), mm)

            def front(i):
                b, c = divmod(i, NQ)
                t = slice(i * P, (i + 1) * P)
                def maxima():
                    o = claim(("nm", i))
                    r = slice(NSP * b, NSP * (b + 1))
                    if b == 0:
                        pe.wait_ge(mneg_done, c + 1)
                    pe.matmul(o[:, :], before16[:, :], bc(never16[:, :], 1, [P, H, P]), start=True, stop=False)
                    fill(("nm", i), pe.matmul(o[:, :], ones16[r, :], mneg[r, c], start=False, stop=True))
                if i:
                    maxima()
                if c:
                    wait_drained(pe, ("H", b))
                for par, item in ((0, ("sA", i)), (1, ("sB", i))):
                    o = claim(item)
                    r = slice(64 * par, 64 * par + 64)
                    for k in range(KD):
                        mm = pe.matmul(o[:, k * P:(k + 1) * P], ctxc[r, k, t], xcol[r, k, t], start=True, stop=True)
                    if c:
                        mm = pe.matmul(o[:, 2 * P:2 * P + 2 * DV], xcol[:, par, t], hs[:, b % 2, c - 1, par], start=True, stop=True)
                    fill(item, mm)
                if i == 0:
                    maxima()
                if c == 0:
                    states(b)

            def values(i):
                pe.wait_ge(prob_done, 2 * (i + 1))
                o = claim(("num", i))
                for h in range(H):
                    mm = pe.matmul(o[:, h * DV:(h + 1) * DV], prob[:, i % 2, h, :], vaug[:, i, h, :], start=True, stop=True)
                fill(("num", i), mm)

            def turn_norm2(u):
                pe.wait_ge(x2_done, u + 1)
                for half, tiles in enumerate(halves(u)):
                    o = claim(("x2t", u, half))
                    for n in range(len(tiles) * KD):
                        q, k = divmod(n, KD)
                        mm = pe.transpose(o[:, n * P:(n + 1) * P], xtok[:, tiles[q], k * P:(k + 1) * P], ident[:, :])
                    fill(("x2t", u, half), mm)

            def logits(u):
                o = claim(("lg", u))
                for half, tiles in enumerate(halves(u)):
                    wait_drained(pe, ("x2t", u, half))
                    for i in tiles:
                        q = i - UNITS[u][0]
                        for k in range(KD):
                            mm = pe.matmul(o[:, q * E:(q + 1) * E], x2c[:, i % NQ, k, :], rw[:, k, :],
                                           start=(k == 0), stop=(k == KD - 1))
                fill(("lg", u), mm)

            def ranks(g):
                first, n = GROUPS[g][0] * NQ, GROUPS[g][1] * NQ
                pe.wait_ge(picks_done, g + 1)
                o = claim(("rk", g))
                pe.matmul(o[:, 0:n * E], before16[:, :], picks[:, first:first + n, :], start=True, stop=False)
                fill(("rk", g), pe.matmul(o[:, 0:n * E], ones16[:, :], picksum[:, first:first + n, :], start=False, stop=True))
            front(0)
            for i in range(NT):
                if i + 1 < NT:
                    front(i + 1)
                if i == ROUTE_AT + 1:
                    ranks(0)
                values(i)
                if i % NQ == 3 and i > NQ:
                    turn_norm2(i // NQ - 1)
                    logits(i // NQ - 1)
            for u in range(B - 1, len(UNITS)):
                turn_norm2(u)
                logits(u)
            ranks(1)
            ranks(2)
            fill("cnt", pe.matmul(claim("cnt")[:, 0:E], ones16[:, :], picksum[:, NT, :], start=True, stop=True))

            wait_drained(pe, "cnt")
            pe.wait_ge(tables_done, 1)
            THREE = ((0, 0), (0, 1), (1, 0))

            def turn_rows(g, s):
                pe.wait_ge(xg_loaded[s], 8 * (g - s) + 16)
                if not isinstance(g, int) or g:
                    pe.wait_ge(xgT_done, g)
                for k in range(KD):
                    mm = pe.transpose(bank[7][:, k * P:(k + 1) * P], xg[:, s, k * P:(k + 1) * P], ident[:, :])
                mm.then_inc(xg_turned, 1)

            def moving(off, part, col, n):
                at = part * WCOLS + col
                return wslot(off)[:, at:at + n]

            def up(g, s, u, off):
                pe.wait_ge(xgT_done, g + 1)
                if not isinstance(g, int) or g:
                    pe.wait_ge(mid_done, 2 * g + (u - 1))
                for m in range(2):
                    for k in range(KD):
                        for a, w in THREE:
                            mm = pe.matmul(bank[2 * u + m][:, :], (xTh, xTl)[a][:, s, k, :],
                                           moving(off, w, m * KD * F + k * F + u * HALF, HALF),
                                           start=(k == 0 and a + w == 0), stop=(k == KD - 1 and a == 1))
                mm.then_inc(up_done, 1)

            def turn(g, u):
                pe.wait_ge(mid_done, 2 * g + (u + 1))
                if not isinstance(g, int) or g:
                    pe.wait_ge(hTl_done, 2 * g + (u - 1))
                for c in range(4):
                    mm = pe.transpose(bank[4 + u][:, c * P:(c + 1) * P], hmid[:, u, c * P:(c + 1) * P], ident[:, :])
                mm.then_inc(turned, 1)

            def down(g, u, off):
                pe.wait_ge(hTh_done, 2 * g + (u + 1))
                pe.wait_ge(hTl_done, 2 * g + (u + 1))
                if u == 0 and (not isinstance(g, int) or g):
                    pe.wait_ge(yout_done, g)
                for c in range(4):
                    for a, w in THREE:
                        mm = pe.matmul(bank[6][:, 0:D], (hTh, hTl)[a][:, u, c, :],
                                       moving(off, w, 2 * KD * F + (4 * u + c) * D, D),
                                       start=(u == 0 and c == 0 and a + w == 0), stop=(u == 1 and c == 3 and a == 1))
                if u == 1:
                    mm.then_inc(y_done, 1)

            def event_of(g):
                return pe.value_load(tab_event[0:1, bass.ds(g, 1)]) & (E - 1)

            def offset_of(event):
                return ((event & 1) * (slot_at[1] - slot_at[0]) + slot_at[0]).with_bounds(min_val=0, max_val=max(slot_at))

            def pair(p):
                off = None
                for s in range(2):
                    g = 2 * p + s
                    first = isinstance(g, int) and g == 0
                    event = event_of(g)
                    last_off, off = off, offset_of(event)
                    pe.wait_ge(w_ready, event + 1)
                    up(g, s, 0, off)
                    if s == 0 and not first:
                        last_off = offset_of(event_of(g - 1))
                    if not first:
                        turn(g - 1, 1)
                        down(g - 1, 0, last_off)
                    turn_rows(g + 1, 1 - s)
                    up(g, s, 1, off)
                    turn(g, 0)
                    if not first:
                        down(g - 1, 1, last_off)
            turn_rows(0, 0)
            npair = pe.value_load(tab_n[0:1, 0:1], min_val=SURE, max_val=NB // 2)
            pair(0)
            with pe.Fori(0, SURE - 1) as it:
                pair(it + 1)
            with pe.Fori(0, NB // 2 - SURE) as it:
                with pe.If(npair - it > SURE):
                    pair(it + SURE)
            last = pe.value_load(tab_n[0:1, 1:2], min_val=2 * SURE - 2, max_val=NB - 2) + 1
            off = offset_of(event_of(last))
            turn(last, 1)
            down(last, 0, off)
            down(last, 1, off)


_INS = ["x", "xT", "ctx", "ctxT", "w_inT", "conv_w", "conv_b", "w_xT", "a_log", "d_param", "w_outT", "gate_k", "gate_b",
        "outnorm", "router_w", "w_exp"]


def kernel(**inputs):
    import numpy as np
    import concourse.bacc as bacc
    from concourse.bass_utils import run_bass_kernel_spmd

    a = {k: np.asarray(v) for k, v in inputs.items()}
    x, ctx = (a[k].reshape(T, D) for k in ("x", "ctx_1024"))
    w1, w3 = (a[k].reshape(E, KD, P, F).transpose(0, 2, 1, 3).reshape(E, P, KD * F) for k in ("L0_ffn_w1", "L0_ffn_w3"))
    w2 = a["L0_ffn_w2"].reshape(E, F // P, P, D).transpose(0, 2, 1, 3).reshape(E, P, (F // P) * D)
    laid = {
        "x": x, "xT": x.T, "ctx": ctx, "ctxT": ctx.T,
        "w_inT": a["L0_attn_W_in"].T, "conv_w": a["L0_attn_conv_w"], "conv_b": a["L0_attn_conv_b"].reshape(NJ, P).T,
        "w_xT": a["L0_attn_W_xproj"].T, "a_log": a["L0_attn_A_log"], "d_param": a["L0_attn_D_param"].reshape(NJ, P).T,
        "w_outT": a["L0_attn_W_out"].T,
        "gate_k": np.concatenate([a["L0_xattn_ig_kernel"], a["L0_xattn_fg_kernel"]], axis=1),
        "gate_b": np.concatenate([a["L0_xattn_ig_bias"], a["L0_xattn_fg_bias"]]),
        "outnorm": a["L0_xattn_outnorm_weight"].reshape(D), "router_w": a["L0_ffn_gate_w"],
        "w_exp": np.concatenate([w1, w3, w2], axis=2),
    }
    nc = bacc.Bacc("TRN2", target_bir_lowering=False, num_devices=1)
    arrays, args = {}, []
    for name in _INS:
        v = np.ascontiguousarray(laid[name])
        arrays[f"in_{name}"] = v
        args.append(nc.dram_tensor(f"in_{name}", v.shape, mybir.dt.from_np(v.dtype), kind="ExternalInput").ap())
    args.append(nc.dram_tensor("out", (T, D), F32, kind="ExternalOutput").ap())
    decoder_kernel(nc, *args)
    r = run_bass_kernel_spmd(nc, [arrays], core_ids=[0])
    return r.results[0]["out"].reshape(B, S, D)
```
